# Optimizing a Trainium2 kernel written in Bass

```python
import numpy as np
import jax
import jax.numpy as jnp

def _softmax(x, axis=-1):
    return jax.nn.softmax(x, axis=axis)

def _gelu(x):
    return jax.nn.gelu(x, approximate=True)

def _silu(x):
    return jax.nn.silu(x)

def _sigmoid(x):
    return jax.nn.sigmoid(x)

def _layernorm(x, axis=-1, eps=1e-05):
    m = jnp.mean(x, axis=axis, keepdims=True)
    v = jnp.var(x, axis=axis, keepdims=True)
    return (x - m) / jnp.sqrt(v + eps)

def _scatter_add(tgt, idx, src, axis=0):
    return tgt.at[idx].add(src)

def _segment_sum(src, seg, n):
    return jax.ops.segment_sum(src, seg, n)
kernel_name = 'mk_audio_tower_d2_tok_aud1d768_r4_74d876'

def setup_inputs(seed: int=0):
    np.random.seed(seed)
    _w = jnp.asarray

    def _rec_inputs():
        import jax
        import jax.numpy as jnp
        _rk = jax.random.key(seed)
        x = -0.000869125 + 1.00042 * jax.random.normal(jax.random.fold_in(_rk, 1), (64, 4000), jnp.float32)
        return x
    x = _rec_inputs()

    def _L0_tok_setup():
        import jax, jax.numpy as jnp
        import numpy as np
        CONVS = [(128, 10, 5)] + [(128, 3, 2)] * 4 + [(128, 2, 2)] * 2

        def _fp32_layernorm(x, g, b, eps=1e-05):
            xf = x.astype(jnp.float32)
            mu = xf.mean(-1, keepdims=True)
            var = xf.var(-1, keepdims=True)
            y = (xf - mu) * jax.lax.rsqrt(var + eps) * g.astype(jnp.float32) + b.astype(jnp.float32)
            return y.astype(x.dtype)

        def _conv1d(x, w, stride):
            return jax.lax.conv_general_dilated(x, w, (stride,), 'VALID', dimension_numbers=('NCH', 'OIH', 'NCH'))
        key = jax.random.key(seed)
        keys = jax.random.split(key, 16)
        inp = {'x': jax.random.normal(keys[0], (8, 40000), jnp.float32)}
        in_d = 1
        for i, (dim, k, s) in enumerate(CONVS):
            fan_in = in_d * k
            inp[f'conv_w{i}'] = jax.random.normal(keys[1 + i], (dim, in_d, k), jnp.float32) * np.float32(np.sqrt(2.0 / fan_in))
            inp[f'ln_g{i}'] = jnp.ones((dim,), jnp.float32)
            inp[f'ln_b{i}'] = jnp.zeros((dim,), jnp.float32)
            in_d = dim
        inp['fln_g'] = jnp.ones((128,), jnp.float32)
        inp['fln_b'] = jnp.zeros((128,), jnp.float32)
        inp['proj_w'] = jax.random.normal(keys[9], (128, 192), jnp.float32) * np.float32(0.02)
        inp['proj_b'] = jnp.zeros((192,), jnp.float32)
        return inp
    _L0_tok_all = _L0_tok_setup()
    _L0_tok_in = {k: v for k, v in _L0_tok_all.items() if k in ('conv_w0', 'ln_g0', 'ln_b0', 'conv_w1', 'ln_g1', 'ln_b1', 'conv_w2', 'ln_g2', 'ln_b2', 'conv_w3', 'ln_g3', 'ln_b3', 'conv_w4', 'ln_g4', 'ln_b4', 'conv_w5', 'ln_g5', 'ln_b5', 'conv_w6', 'ln_g6', 'ln_b6', 'fln_g', 'fln_b', 'proj_w', 'proj_b')}
    del _L0_tok_all

    def _L0_attn_setup():
        import jax, jax.numpy as jnp
        import numpy as np
        import math
        H = 12

        def _ln(x, w, b, eps=1e-05):
            mu = x.mean(-1, keepdims=True)
            var = ((x - mu) ** 2).mean(-1, keepdims=True)
            return (x - mu) / jnp.sqrt(var + eps) * w + b

        def _reference_tuple_inner(x, Wqkv, bqkv, Wb1, Wb2, temperature, Wproj, bproj, ln_w, ln_b, mn_w, mn_b):
            B, L, D = x.shape
            d = D // H
            x_norm = _ln(x, ln_w, ln_b)
            qkv = x_norm @ Wqkv + bqkv
            q, k, v = jnp.split(qkv, 3, axis=-1)
            params = (jax.nn.silu(x @ Wb1) @ Wb2).reshape(B, L, H, 5)
            sem_amp = jax.nn.sigmoid(params[..., 0])
            sem_phase = jnp.tanh(params[..., 1]) * math.pi
            ctx_amp = jax.nn.sigmoid(params[..., 2])
            ctx_phase = jnp.tanh(params[..., 3]) * math.pi
            temp = jnp.clip(temperature, 0.1, 2.0)
            interference = jnp.tanh(sem_amp * ctx_amp * jnp.cos(sem_phase - ctx_phase)) * temp
            gate = jax.nn.sigmoid(interference)
            q_f = (jax.nn.elu(q) + 1.0).reshape(B, L, H, d)
            k_f = (jax.nn.elu(k) + 1.0).reshape(B, L, H, d)
            v_f = v.reshape(B, L, H, d)
            kv_gated = jnp.einsum('blhd,blhe->blhde', k_f, v_f) * (1.0 + gate)[..., None, None]
            kv_states = jnp.cumsum(kv_gated, axis=1)
            z_states = jnp.cumsum(k_f, axis=1)
            out_num = jnp.einsum('blhd,blhde->blhe', q_f, kv_states)
            den = jnp.sum(q_f * z_states, axis=-1, keepdims=True) + 1e-06
            out = _ln(out_num / den, mn_w, mn_b)
            attn_out = out.reshape(B, L, D)
            return (attn_out @ Wproj + bproj, gate)
        key = jax.random.key(seed)
        B, L, D, R = (2, 256, 192, 128)
        d_head = D // H
        ks = jax.random.split(key, 6)
        s = 0.02
        return {'x': jax.random.normal(ks[0], (B, L, D), jnp.float32), 'Wqkv': jax.random.normal(ks[1], (D, 3 * D), jnp.float32) * s, 'bqkv': jnp.zeros((3 * D,), jnp.float32), 'Wb1': jax.random.normal(ks[2], (D, R), jnp.float32) * s, 'Wb2': jax.random.normal(ks[3], (R, H * 5), jnp.float32) * s, 'temperature': jnp.ones((1,), jnp.float32) * 0.5, 'Wproj': jax.random.normal(ks[4], (D, D), jnp.float32) * s, 'bproj': jnp.zeros((D,), jnp.float32), 'ln_w': jnp.ones((D,), jnp.float32), 'ln_b': jnp.zeros((D,), jnp.float32), 'mn_w': jnp.ones((d_head,), jnp.float32), 'mn_b': jnp.zeros((d_head,), jnp.float32)}
    _L0_attn_all = _L0_attn_setup()
    _L0_attn_in = {k: v for k, v in _L0_attn_all.items() if k in ('Wqkv', 'bqkv', 'Wb1', 'Wb2', 'temperature', 'Wproj', 'bproj', 'ln_w', 'ln_b', 'mn_w', 'mn_b')}
    del _L0_attn_all

    def _L0_ffn_setup():
        import jax, jax.numpy as jnp
        import numpy as np
        TOP_K = 2
        ROUTED_SCALE = 1.0

        def _swiglu_all(x, gw, uw, dw):
            g = jnp.einsum('th,eih->tei', x, gw)
            u = jnp.einsum('th,eih->tei', x, uw)
            h = jax.nn.silu(g) * u
            return jnp.einsum('tei,ehi->teh', h, dw)
        key = jax.random.key(seed)
        ks = jax.random.split(key, 8)
        B, S, H, I, E, NS = (2, 256, 192, 768, 8, 2)
        w = lambda k, shape: jax.random.normal(k, shape, jnp.float32) * 0.02
        return {'hidden_states': jax.random.normal(ks[0], (B, S, H), jnp.float32), 'gate_w': w(ks[1], (E, H)), 'shared_gate': w(ks[2], (NS, I, H)), 'shared_up': w(ks[3], (NS, I, H)), 'shared_down': w(ks[4], (NS, H, I)), 'routed_gate': w(ks[5], (E, I, H)), 'routed_up': w(ks[6], (E, I, H)), 'routed_down': w(ks[7], (E, H, I))}
    _L0_ffn_all = _L0_ffn_setup()
    _L0_ffn_in = {k: v for k, v in _L0_ffn_all.items() if k in ('gate_w', 'shared_gate', 'shared_up', 'shared_down', 'routed_gate', 'routed_up', 'routed_down')}
    del _L0_ffn_all

    def _L1_attn_setup():
        import jax, jax.numpy as jnp
        import numpy as np
        B, N, D = (2, 512, 192)
        H = 12
        DH = D // H
        SCALE = DH ** (-0.5)
        key = jax.random.key(seed)
        k1, k2, k3 = jax.random.split(key, 3)
        x = jax.random.normal(k1, (B, N, D), dtype=jnp.float32)
        w_qkv = jax.random.normal(k2, (D, 3 * D), dtype=jnp.float32) * D ** (-0.5)
        b_qkv = jnp.zeros((3 * D,), dtype=jnp.float32)
        w_proj = jax.random.normal(k3, (D, D), dtype=jnp.float32) * D ** (-0.5)
        b_proj = jnp.zeros((D,), dtype=jnp.float32)
        return {'x': x, 'w_qkv': w_qkv, 'b_qkv': b_qkv, 'w_proj': w_proj, 'b_proj': b_proj}
    _L1_attn_all = _L1_attn_setup()
    _L1_attn_in = {k: v for k, v in _L1_attn_all.items() if k in ('w_qkv', 'b_qkv', 'w_proj', 'b_proj')}
    del _L1_attn_all

    def _L1_ffn_setup():
        import jax, jax.numpy as jnp
        import numpy as np
        GT0 = [[0, 1, 0, 0, 1, 0], [0, 1, 0, 0, 0, 1], [0, 0, 1, 0, 1, 0], [0, 0, 1, 0, 0, 1], [0, 0, 0, 1, 1, 0], [0, 0, 0, 1, 0, 1]]
        NCLS = 6
        K = 1

        def _expert_pairs():
            pairs = []
            for i in range(NCLS):
                p = [(j - 1, k - 1) for j in range(1, 6) for k in range(1, 6) if j != k and GT0[i][j] == 1 and (GT0[i][k] == 1)]
                pairs.append(p)
            return pairs
        PAIRS = _expert_pairs()
        B, P, D, H = (64, 64, 192, 768)

        def _gelu(t):
            return jax.nn.gelu(t, approximate=False)
        key = jax.random.key(seed)
        ks = jax.random.split(key, 8)
        s = 0.02
        x = jax.random.normal(ks[0], (B, NCLS + P, D), dtype=jnp.float32)
        mids = jax.random.randint(ks[1], (B,), 0, 6)
        moe0_W1 = jax.random.normal(ks[2], (D, H), dtype=jnp.float32) * s
        moe0_b1 = jnp.zeros((H,), jnp.float32)
        moe0_W2 = jax.random.normal(ks[3], (H, D), dtype=jnp.float32) * s
        moe0_b2 = jnp.zeros((D,), jnp.float32)
        A1_W = jax.random.normal(ks[4], (5, D, H), dtype=jnp.float32) * s
        A1_b = jnp.zeros((5, H), jnp.float32)
        A2_W = jax.random.normal(ks[5], (5, H, D), dtype=jnp.float32) * s
        A2_b = jnp.zeros((5, D), jnp.float32)
        G_W = jax.random.normal(ks[6], (NCLS, D, 2), dtype=jnp.float32) * s
        return {'x': x, 'moe0_W1': moe0_W1, 'moe0_b1': moe0_b1, 'moe0_W2': moe0_W2, 'moe0_b2': moe0_b2, 'A1_W': A1_W, 'A1_b': A1_b, 'A2_W': A2_W, 'A2_b': A2_b, 'G_W': G_W, 'mids': mids}
    _L1_ffn_all = _L1_ffn_setup()
    _L1_ffn_in = {k: v for k, v in _L1_ffn_all.items() if k in ('moe0_W1', 'moe0_b1', 'moe0_W2', 'moe0_b2', 'A1_W', 'A1_b', 'A2_W', 'A2_b', 'G_W', 'mids')}
    del _L1_ffn_all
    return {'x': x, 'L0_tok_conv_w0': _L0_tok_in['conv_w0'], 'L0_tok_ln_g0': _L0_tok_in['ln_g0'], 'L0_tok_ln_b0': _L0_tok_in['ln_b0'], 'L0_tok_conv_w1': _L0_tok_in['conv_w1'], 'L0_tok_ln_g1': _L0_tok_in['ln_g1'], 'L0_tok_ln_b1': _L0_tok_in['ln_b1'], 'L0_tok_conv_w2': _L0_tok_in['conv_w2'], 'L0_tok_ln_g2': _L0_tok_in['ln_g2'], 'L0_tok_ln_b2': _L0_tok_in['ln_b2'], 'L0_tok_conv_w3': _L0_tok_in['conv_w3'], 'L0_tok_ln_g3': _L0_tok_in['ln_g3'], 'L0_tok_ln_b3': _L0_tok_in['ln_b3'], 'L0_tok_conv_w4': _L0_tok_in['conv_w4'], 'L0_tok_ln_g4': _L0_tok_in['ln_g4'], 'L0_tok_ln_b4': _L0_tok_in['ln_b4'], 'L0_tok_conv_w5': _L0_tok_in['conv_w5'], 'L0_tok_ln_g5': _L0_tok_in['ln_g5'], 'L0_tok_ln_b5': _L0_tok_in['ln_b5'], 'L0_tok_conv_w6': _L0_tok_in['conv_w6'], 'L0_tok_ln_g6': _L0_tok_in['ln_g6'], 'L0_tok_ln_b6': _L0_tok_in['ln_b6'], 'L0_tok_fln_g': _L0_tok_in['fln_g'], 'L0_tok_fln_b': _L0_tok_in['fln_b'], 'L0_tok_proj_w': _L0_tok_in['proj_w'], 'L0_tok_proj_b': _L0_tok_in['proj_b'], 'L0_attn_Wqkv': _L0_attn_in['Wqkv'], 'L0_attn_bqkv': _L0_attn_in['bqkv'], 'L0_attn_Wb1': _L0_attn_in['Wb1'], 'L0_attn_Wb2': _L0_attn_in['Wb2'], 'L0_attn_temperature': _L0_attn_in['temperature'], 'L0_attn_Wproj': _L0_attn_in['Wproj'], 'L0_attn_bproj': _L0_attn_in['bproj'], 'L0_attn_ln_w': _L0_attn_in['ln_w'], 'L0_attn_ln_b': _L0_attn_in['ln_b'], 'L0_attn_mn_w': _L0_attn_in['mn_w'], 'L0_attn_mn_b': _L0_attn_in['mn_b'], 'L0_ffn_gate_w': _L0_ffn_in['gate_w'], 'L0_ffn_shared_gate': _L0_ffn_in['shared_gate'], 'L0_ffn_shared_up': _L0_ffn_in['shared_up'], 'L0_ffn_shared_down': _L0_ffn_in['shared_down'], 'L0_ffn_routed_gate': _L0_ffn_in['routed_gate'], 'L0_ffn_routed_up': _L0_ffn_in['routed_up'], 'L0_ffn_routed_down': _L0_ffn_in['routed_down'], 'L1_attn_w_qkv': _L1_attn_in['w_qkv'], 'L1_attn_b_qkv': _L1_attn_in['b_qkv'], 'L1_attn_w_proj': _L1_attn_in['w_proj'], 'L1_attn_b_proj': _L1_attn_in['b_proj'], 'L1_ffn_moe0_W1': _L1_ffn_in['moe0_W1'], 'L1_ffn_moe0_b1': _L1_ffn_in['moe0_b1'], 'L1_ffn_moe0_W2': _L1_ffn_in['moe0_W2'], 'L1_ffn_moe0_b2': _L1_ffn_in['moe0_b2'], 'L1_ffn_A1_W': _L1_ffn_in['A1_W'], 'L1_ffn_A1_b': _L1_ffn_in['A1_b'], 'L1_ffn_A2_W': _L1_ffn_in['A2_W'], 'L1_ffn_A2_b': _L1_ffn_in['A2_b'], 'L1_ffn_G_W': _L1_ffn_in['G_W'], 'L1_ffn_mids': _L1_ffn_in['mids']}

def reference(x, L0_tok_conv_w0, L0_tok_ln_g0, L0_tok_ln_b0, L0_tok_conv_w1, L0_tok_ln_g1, L0_tok_ln_b1, L0_tok_conv_w2, L0_tok_ln_g2, L0_tok_ln_b2, L0_tok_conv_w3, L0_tok_ln_g3, L0_tok_ln_b3, L0_tok_conv_w4, L0_tok_ln_g4, L0_tok_ln_b4, L0_tok_conv_w5, L0_tok_ln_g5, L0_tok_ln_b5, L0_tok_conv_w6, L0_tok_ln_g6, L0_tok_ln_b6, L0_tok_fln_g, L0_tok_fln_b, L0_tok_proj_w, L0_tok_proj_b, L0_attn_Wqkv, L0_attn_bqkv, L0_attn_Wb1, L0_attn_Wb2, L0_attn_temperature, L0_attn_Wproj, L0_attn_bproj, L0_attn_ln_w, L0_attn_ln_b, L0_attn_mn_w, L0_attn_mn_b, L0_ffn_gate_w, L0_ffn_shared_gate, L0_ffn_shared_up, L0_ffn_shared_down, L0_ffn_routed_gate, L0_ffn_routed_up, L0_ffn_routed_down, L1_attn_w_qkv, L1_attn_b_qkv, L1_attn_w_proj, L1_attn_b_proj, L1_ffn_moe0_W1, L1_ffn_moe0_b1, L1_ffn_moe0_W2, L1_ffn_moe0_b2, L1_ffn_A1_W, L1_ffn_A1_b, L1_ffn_A2_W, L1_ffn_A2_b, L1_ffn_G_W, L1_ffn_mids):
    import jax
    import jax.numpy as jnp

    def _L0_tok_ref(x, conv_w0, ln_g0, ln_b0, conv_w1, ln_g1, ln_b1, conv_w2, ln_g2, ln_b2, conv_w3, ln_g3, ln_b3, conv_w4, ln_g4, ln_b4, conv_w5, ln_g5, ln_b5, conv_w6, ln_g6, ln_b6, fln_g, fln_b, proj_w, proj_b):
        import jax, jax.numpy as jnp
        import numpy as np
        CONVS = [(128, 10, 5)] + [(128, 3, 2)] * 4 + [(128, 2, 2)] * 2

        def _fp32_layernorm(x, g, b, eps=1e-05):
            xf = x.astype(jnp.float32)
            mu = xf.mean(-1, keepdims=True)
            var = xf.var(-1, keepdims=True)
            y = (xf - mu) * jax.lax.rsqrt(var + eps) * g.astype(jnp.float32) + b.astype(jnp.float32)
            return y.astype(x.dtype)

        def _conv1d(x, w, stride):
            return jax.lax.conv_general_dilated(x, w, (stride,), 'VALID', dimension_numbers=('NCH', 'OIH', 'NCH'))
        conv_ws = [conv_w0, conv_w1, conv_w2, conv_w3, conv_w4, conv_w5, conv_w6]
        ln_gs = [ln_g0, ln_g1, ln_g2, ln_g3, ln_g4, ln_g5, ln_g6]
        ln_bs = [ln_b0, ln_b1, ln_b2, ln_b3, ln_b4, ln_b5, ln_b6]
        strides = [s for _, _, s in CONVS]
        h = x[:, None, :]
        for w, g, b, s in zip(conv_ws, ln_gs, ln_bs, strides):
            h = _conv1d(h, w, s)
            h = jnp.swapaxes(h, -2, -1)
            h = _fp32_layernorm(h, g, b)
            h = jnp.swapaxes(h, -2, -1)
            h = jax.nn.gelu(h, approximate=False)
        h = jnp.swapaxes(h, 1, 2)
        norm_h = _fp32_layernorm(h, fln_g, fln_b)
        out = norm_h @ proj_w + proj_b
        return out

    def _L0_attn_ref(x, Wqkv, bqkv, Wb1, Wb2, temperature, Wproj, bproj, ln_w, ln_b, mn_w, mn_b):
        import jax, jax.numpy as jnp
        import numpy as np
        import math
        H = 12

        def _ln(x, w, b, eps=1e-05):
            mu = x.mean(-1, keepdims=True)
            var = ((x - mu) ** 2).mean(-1, keepdims=True)
            return (x - mu) / jnp.sqrt(var + eps) * w + b

        def _reference_tuple_inner(x, Wqkv, bqkv, Wb1, Wb2, temperature, Wproj, bproj, ln_w, ln_b, mn_w, mn_b):
            B, L, D = x.shape
            d = D // H
            x_norm = _ln(x, ln_w, ln_b)
            qkv = x_norm @ Wqkv + bqkv
            q, k, v = jnp.split(qkv, 3, axis=-1)
            params = (jax.nn.silu(x @ Wb1) @ Wb2).reshape(B, L, H, 5)
            sem_amp = jax.nn.sigmoid(params[..., 0])
            sem_phase = jnp.tanh(params[..., 1]) * math.pi
            ctx_amp = jax.nn.sigmoid(params[..., 2])
            ctx_phase = jnp.tanh(params[..., 3]) * math.pi
            temp = jnp.clip(temperature, 0.1, 2.0)
            interference = jnp.tanh(sem_amp * ctx_amp * jnp.cos(sem_phase - ctx_phase)) * temp
            gate = jax.nn.sigmoid(interference)
            q_f = (jax.nn.elu(q) + 1.0).reshape(B, L, H, d)
            k_f = (jax.nn.elu(k) + 1.0).reshape(B, L, H, d)
            v_f = v.reshape(B, L, H, d)
            kv_gated = jnp.einsum('blhd,blhe->blhde', k_f, v_f) * (1.0 + gate)[..., None, None]
            kv_states = jnp.cumsum(kv_gated, axis=1)
            z_states = jnp.cumsum(k_f, axis=1)
            out_num = jnp.einsum('blhd,blhde->blhe', q_f, kv_states)
            den = jnp.sum(q_f * z_states, axis=-1, keepdims=True) + 1e-06
            out = _ln(out_num / den, mn_w, mn_b)
            attn_out = out.reshape(B, L, D)
            return (attn_out @ Wproj + bproj, gate)
        return _reference_tuple_inner(x, Wqkv, bqkv, Wb1, Wb2, temperature, Wproj, bproj, ln_w, ln_b, mn_w, mn_b)[0]

    def _L0_ffn_ref(hidden_states, gate_w, shared_gate, shared_up, shared_down, routed_gate, routed_up, routed_down):
        import jax, jax.numpy as jnp
        import numpy as np
        TOP_K = 2
        ROUTED_SCALE = 1.0

        def _swiglu_all(x, gw, uw, dw):
            g = jnp.einsum('th,eih->tei', x, gw)
            u = jnp.einsum('th,eih->tei', x, uw)
            h = jax.nn.silu(g) * u
            return jnp.einsum('tei,ehi->teh', h, dw)
        B, S, H = hidden_states.shape
        T = B * S
        x = hidden_states.reshape(T, H)
        router_logits = x @ gate_w.T
        scores = jax.nn.softmax(router_logits, axis=-1)
        _, topk_idx = jax.lax.top_k(scores, TOP_K)
        topk_w = jnp.take_along_axis(scores, topk_idx, axis=-1)
        topk_w = topk_w / (topk_w.sum(axis=-1, keepdims=True) + 1e-08)
        topk_w = topk_w * ROUTED_SCALE
        E = gate_w.shape[0]
        combine = jnp.zeros((T, E), scores.dtype).at[jnp.arange(T)[:, None], topk_idx].add(topk_w)
        routed_all = _swiglu_all(x, routed_gate, routed_up, routed_down)
        routed_out = jnp.einsum('teh,te->th', routed_all, combine)
        NS = shared_gate.shape[0]
        shared_all = _swiglu_all(x, shared_gate, shared_up, shared_down)
        shared_out = shared_all.sum(axis=1) / NS
        out = (shared_out + routed_out).reshape(B, S, H)
        return out

    def _L1_attn_ref(x, w_qkv, b_qkv, w_proj, b_proj):
        import jax, jax.numpy as jnp
        import numpy as np
        B, N, D = (2, 512, 192)
        H = 12
        DH = D // H
        SCALE = DH ** (-0.5)
        b, n, d = x.shape
        qkv = (x @ w_qkv + b_qkv).reshape(b, n, 3, H, DH).transpose(2, 0, 3, 1, 4)
        q, k, v = (qkv[0], qkv[1], qkv[2])
        attn = jnp.einsum('bhqd,bhkd->bhqk', q, k) * SCALE
        attn = jax.nn.softmax(attn, axis=-1)
        out = jnp.einsum('bhqk,bhkd->bhqd', attn, v)
        out = out.transpose(0, 2, 1, 3).reshape(b, n, d)
        return out @ w_proj + b_proj

    def _L1_ffn_ref(x, moe0_W1, moe0_b1, moe0_W2, moe0_b2, A1_W, A1_b, A2_W, A2_b, G_W, mids):
        import jax, jax.numpy as jnp
        import numpy as np
        GT0 = [[0, 1, 0, 0, 1, 0], [0, 1, 0, 0, 0, 1], [0, 0, 1, 0, 1, 0], [0, 0, 1, 0, 0, 1], [0, 0, 0, 1, 1, 0], [0, 0, 0, 1, 0, 1]]
        NCLS = 6
        K = 1

        def _expert_pairs():
            pairs = []
            for i in range(NCLS):
                p = [(j - 1, k - 1) for j in range(1, 6) for k in range(1, 6) if j != k and GT0[i][j] == 1 and (GT0[i][k] == 1)]
                pairs.append(p)
            return pairs
        PAIRS = _expert_pairs()
        B, P, D, H = (64, 64, 192, 768)

        def _gelu(t):
            return jax.nn.gelu(t, approximate=False)
        cls_tokens = x[:, :NCLS]
        patch_tokens = x[:, NCLS:]
        patch_out = _gelu(patch_tokens @ moe0_W1 + moe0_b1) @ moe0_W2 + moe0_b2
        cls_outs = []
        for i in range(NCLS):
            tok = cls_tokens[:, i]
            eouts = [_gelu(tok @ A1_W[a] + A1_b[a]) @ A2_W[c] + A2_b[c] for a, c in PAIRS[i]]
            out = jnp.stack(eouts, axis=-1)
            gate = jax.nn.softmax(tok @ G_W[i], axis=-1)
            thr = jnp.sort(gate, axis=-1)[..., -(K + 1)]
            mask = (gate > thr[..., None]).astype(gate.dtype)
            g = gate * mask
            g = g / jnp.clip(jnp.sum(g, axis=-1, keepdims=True), 1e-06)
            cls_outs.append(jnp.sum(out * g[:, None, :], axis=-1))
        cls_out = jnp.stack(cls_outs, axis=1)
        return jnp.concatenate([cls_out, patch_out], axis=1)
    h = _L0_tok_ref(x, L0_tok_conv_w0, L0_tok_ln_g0, L0_tok_ln_b0, L0_tok_conv_w1, L0_tok_ln_g1, L0_tok_ln_b1, L0_tok_conv_w2, L0_tok_ln_g2, L0_tok_ln_b2, L0_tok_conv_w3, L0_tok_ln_g3, L0_tok_ln_b3, L0_tok_conv_w4, L0_tok_ln_g4, L0_tok_ln_b4, L0_tok_conv_w5, L0_tok_ln_g5, L0_tok_ln_b5, L0_tok_conv_w6, L0_tok_ln_g6, L0_tok_ln_b6, L0_tok_fln_g, L0_tok_fln_b, L0_tok_proj_w, L0_tok_proj_b)
    h = h + _L0_attn_ref(_layernorm(h, axis=-1), L0_attn_Wqkv, L0_attn_bqkv, L0_attn_Wb1, L0_attn_Wb2, L0_attn_temperature, L0_attn_Wproj, L0_attn_bproj, L0_attn_ln_w, L0_attn_ln_b, L0_attn_mn_w, L0_attn_mn_b)
    h = h + _L0_ffn_ref(_layernorm(h, axis=-1), L0_ffn_gate_w, L0_ffn_shared_gate, L0_ffn_shared_up, L0_ffn_shared_down, L0_ffn_routed_gate, L0_ffn_routed_up, L0_ffn_routed_down)
    h = h + _L1_attn_ref(_layernorm(h, axis=-1), L1_attn_w_qkv, L1_attn_b_qkv, L1_attn_w_proj, L1_attn_b_proj)
    h = h + _L1_ffn_ref(_layernorm(h, axis=-1), L1_ffn_moe0_W1, L1_ffn_moe0_b1, L1_ffn_moe0_W2, L1_ffn_moe0_b2, L1_ffn_A1_W, L1_ffn_A1_b, L1_ffn_A2_W, L1_ffn_A2_b, L1_ffn_G_W, L1_ffn_mids)
    return h

_drawn_inputs = setup_inputs


def setup_inputs(seed=0):
    import zlib

    import numpy as np

    out = dict(_drawn_inputs(seed))
    spreads = {'L0_tok_ln_g0': (1.0, 0.2),
     'L0_tok_ln_b0': (0.0, 0.1),
     'L0_tok_ln_g1': (1.0, 0.2),
     'L0_tok_ln_b1': (0.0, 0.1),
     'L0_tok_ln_g2': (1.0, 0.2),
     'L0_tok_ln_b2': (0.0, 0.1),
     'L0_tok_ln_g3': (1.0, 0.2),
     'L0_tok_ln_b3': (0.0, 0.1),
     'L0_tok_ln_g4': (1.0, 0.2),
     'L0_tok_ln_b4': (0.0, 0.1),
     'L0_tok_ln_g5': (1.0, 0.2),
     'L0_tok_ln_b5': (0.0, 0.1),
     'L0_tok_ln_g6': (1.0, 0.2),
     'L0_tok_ln_b6': (0.0, 0.1),
     'L0_tok_fln_g': (1.0, 0.2),
     'L0_tok_fln_b': (0.0, 0.1),
     'L0_tok_proj_b': (0.0, 0.1),
     'L0_attn_bqkv': (0.0, 0.1),
     'L0_attn_bproj': (0.0, 0.1),
     'L0_attn_ln_w': (1.0, 0.2),
     'L0_attn_ln_b': (0.0, 0.1),
     'L0_attn_mn_w': (1.0, 0.2),
     'L0_attn_mn_b': (0.0, 0.1),
     'L1_attn_b_qkv': (0.0, 0.1),
     'L1_attn_b_proj': (0.0, 0.1),
     'L1_ffn_moe0_b1': (0.0, 0.365),
     'L1_ffn_moe0_b2': (0.0, 0.1),
     'L1_ffn_A1_b': (0.0, 0.34),
     'L1_ffn_A2_b': (0.0, 0.1)}
    factors = {'L0_attn_Wb1': 8.0, 'L0_attn_Wb2': 8.0}
    for name, (base, spread) in spreads.items():
        noise = np.random.default_rng([zlib.crc32(name.encode()), seed]).standard_normal(out[name].shape)
        drawn = base * np.exp(spread * noise) if base else spread * noise
        out[name] = jnp.asarray(drawn.astype(out[name].dtype))
    for name, factor in factors.items():
        out[name] = (out[name] * factor).astype(out[name].dtype)
    return out
```

```python
from contextlib import ExitStack

import numpy as np
import concourse.bass as bass
from concourse import mybir

F32 = mybir.dt.float32
F16 = mybir.dt.float16
BF16 = mybir.dt.bfloat16
U32 = mybir.dt.uint32
ALU = mybir.AluOpType
ACT = mybir.ActivationFunctionType
AX = mybir.AxisListType.X

P = 128
BATCH = 64
CH = 128
TAPS0, STRIDE0 = 10, 5
SLOTS0 = 800
STREAM0 = BATCH * SLOTS0
GROUPS = 8
FOLD = STREAM0 // GROUPS
WROWS = GROUPS * TAPS0
PIECE = 400
PIECES = FOLD // PIECE
CHUNK = 512
BODY0 = 2048
STEPS = STREAM0 // BODY0
WS = 256.0
EPS = 1e-5
TAPS = [3, 3, 3, 3, 2, 2]
TAP0 = [0, 3, 6, 9, 12, 14]
NTAPS = 16


def conv_tail_chunks():
    out = []
    for layer, tokens in ((3, 6400), (4, 3200), (5, 1600)):
        for c in range(0, tokens, CHUNK):
            n = min(CHUNK, tokens - c)
            out.append((layer, c, [min(P, n - t) for t in range(0, n, P)]))
    for r in range(0, 12, 4):
        out.append((6, r, [BATCH] * 4))
    return out


def build_conv(nc, sb, ps, sem, t, act6, load_small):
    scr = t["scratch"]

    tail_ctx = ExitStack()
    tail_sb = lambda n, sh, dt: tail_ctx.enter_context(nc.sbuf_tensor(n, sh, dt))
    act = {2: sb("act2", [P, 12802], F32), 3: sb("act3", [P, 6401], F32), 6: act6}
    low = {2: sb("low2", [P, 12802], F16), 3: sb("low3", [P, 6401], F16)}
    act[4], act[5] = tail_sb("act4", [P, 3200], F32), tail_sb("act5", [P, 1600], F32)
    low[4], low[5] = tail_sb("low4", [P, 3200], F16), tail_sb("low5", [P, 1600], F16)
    tail_ctx.close()
    act[0], act[1] = sb("act0", [P, 1 + BODY0], F32), sb("act1", [P, 1 + BODY0 // 2], F32)
    low[0], low[1] = sb("low0", [P, 1 + BODY0], F16), sb("low1", [P, 1 + BODY0 // 2], F16)
    wt = sb("wt", [64, 2, BODY0], F16)
    high = {l: act[l][:, :].bitcast(BF16).rearrange("p (n two) -> p n two", two=2)[:, :, 1] for l in range(6)}
    win = act[2][0:WROWS, 0:FOLD]
    win_hi = low[2][0:WROWS, 0:FOLD]
    win_lo = low[2][0:WROWS, FOLD:2 * FOLD]
    raw = act[3][:, 0:NTAPS * CH].rearrange("p (t n) -> p t n", t=NTAPS)
    raw0 = act[2][0:64, 2 * FOLD - 2 * CH:2 * FOLD - CH]
    g0rows = act[2][0:64, 2 * FOLD - CH:2 * FOLD]
    w_cen = act[3][:, NTAPS * CH:2 * NTAPS * CH].rearrange("p (t n) -> p t n", t=NTAPS)
    w_hi = sb("w_hi", [P, NTAPS, CH], F16)
    w_lo = sb("w_lo", [P, NTAPS, CH], F16)
    w_mean = sb("w_mean", [P, NTAPS], F32)
    w0_mean = sb("w0_mean", [64, 1], F32)
    w0st = sb("w0st", [64, CH], F16)
    w0hi = sb("w0hi", [64, CH], F16)
    wrep = sb("wrep", [P, WROWS], F32)
    wrepc = sb("wrepc", [P, WROWS], F32)
    gram = sb("gram", [WROWS, WROWS], F32)
    blk = sb("blk", [WROWS, WROWS], F32)
    f16_area = act[2][:, FOLD:FOLD + P + PIECES * WROWS // 2].bitcast(F16)
    pick = f16_area[0:WROWS, 0:2 * P - GROUPS]
    back = f16_area[:, 2 * P:2 * P + PIECES * WROWS].rearrange("p (c r) -> p c r", c=PIECES)
    cen = sb("cen", [P, P], F32)
    gt = act[1][0:WROWS, 1:1 + 2 * PIECE].rearrange("p (k n) -> p k n", k=2)
    odd = lambda x: x.bitcast(BF16).rearrange("p (n two) -> p n two", two=2)[:, :, 1]
    gt_hi = odd(act[1][0:WROWS, 1:1 + 2 * PIECE]).rearrange("p (k n) -> p k n", k=2)
    gt_lo = low[1][0:WROWS, 1:1 + 2 * PIECE].rearrange("p (k n) -> p k n", k=2)
    sd_lo = low[0][:, 1:1 + PIECE]
    sd = sb("sd", [P, PIECE], F32)
    xn0 = act[0][0:WROWS, 1:1 + 3 * PIECE].rearrange("p (k n) -> p k n", k=3)
    ident = t["ident"]
    gb = sb("gb", [P, 7, 2], F32)
    eps1 = sb("eps1", [P, 1], F32)
    expo = sb("expo", [P, 4], F32)
    st = sb("st", [P, 3, 4, 6], F32)
    sq = sb("sq", [P, 3, 4], F32)
    s2 = sb("s2", [P, 3, 4], F32)
    var = sb("var", [P, 3, 4], F32)
    rstd = sb("rstd", [P, 3, 4], F32)
    yn = sb("yn", [P, 3, 4, CH], F32)

    yb = [ps(i) for i in range(3)]
    zb = [ps(i + 3) for i in range(3)]
    z0 = [ps(6), ps(7)]

    names = ["loaded", "loaded2", "cen_ps", "cen_sb", "gram_ps", "gram_sb", "wsplit", "w0split", "gx_ps", "gx_sb", "gx_lo", "pick_ps",
             "var_sb", "std_sb", "rstd_sb", "rstd_ps", "xn_sb", "hi_sb", "lo_sb", "w_mean", "w_cen", "ch_v", "scr_out0",
             "scr_out", "win_part0", "win_part1", "win_part2", "win_part3", "conv0_ps", "act0_w", "low0_w", "halo0", "halo1",
             "zeroed", "zeroed_p", "expo_set", "tail_y", "tail_var", "tail_rstd", "tail_norm", "tail_z",
             "tail_act", "tail_low", "ch_p"]
    s = {n: sem("c_" + n) for n in names}
    s["win_in"] = [sem(f"c_win_in{i}") for i in range(2)]
    kinds = "ABC"
    q = {n: {k: sem(f"c_{n}{k}") for k in kinds} for n in
         ["y", "var", "rstd", "norm", "z", "act", "low"]}
    tail = conv_tail_chunks()
    tail_index = {}
    for n, (l, c, sizes) in enumerate(tail):
        tail_index[(l, c)] = n

    def need(n):
        l, c, sizes = tail[n]
        if l == 3:
            return 0
        if l == 6:
            return max(i for i, (ll, cc, ss) in enumerate(tail) if ll == 5) + 1
        end = 2 * (c + sum(sizes)) + (1 if l == 4 else 0)
        return max(i for i, (ll, cc, ss) in enumerate(tail) if ll == l - 1 and cc < end) + 1

    def sync_prog(sp):
        for dst, src in ((wrep[:, :], t["w0rep"]), (blk[:, :], t["blk"]), (cen[:, :], t["cen"]),
                         (pick, t["pick"])):
            sp.dma_start(dst, src).then_inc(s["loaded"], 16)
        for part in range(4):
            cols = slice(part * FOLD // 4, (part + 1) * FOLD // 4)
            sp.dma_start(win[:, cols], t["windows"][:, cols]).then_inc(s[f"win_part{part}"], 16)
        for dst, src in ((raw, t["conv_w"]), (gb[:, :, :], t["conv_gb"]), (ident[:, :], t["ident_d"]),
                         (back, t["back"])):
            sp.dma_start(dst, src).then_inc(s["loaded2"], 16)
        for h in range(2):
            sp.dma_start(raw0[32 * h:32 * h + 20, :], t["w0rows"]).then_inc(s["loaded2"], 16)
            sp.dma_start(g0rows[32 * h:32 * h + 20, :], t["g0rows"]).then_inc(s["loaded2"], 16)
        load_small(sp)
        sp.wait_ge(s["hi_sb"], PIECES)
        sp.wait_ge(s["lo_sb"], PIECES)
        for g in range(GROUPS):
            for h, src in enumerate((win_hi, win_lo)):
                sp.dma_start(scr[h, :, g * FOLD:(g + 1) * FOLD],
                             src[g * TAPS0:(g + 1) * TAPS0, :]).then_inc(s["scr_out" if g else "scr_out0"], 16)
        rows = scr.rearrange("h k n -> (h k) n")

        def load(i, par):
            for h in range(2):
                sp.dma_start(wt[32 * h:32 * h + 20, par, :],
                             rows[:, bass.ds(i * BODY0, BODY0)]).then_inc(s["win_in"][par], 16)

        sp.wait_ge(s["scr_out0"], 16 * 2)
        sp.wait_ge(s["zeroed"], 2)
        load(0, 0)
        load(1, 1)
        sp.wait_ge(s["scr_out"], 16 * 2 * (GROUPS - 1))
        with sp.Fori(0, (STEPS - 3) // 2) as j:
            sp.wait_ge(s["conv0_ps"], 8 * j + 4)
            load(2 * j + 2, 0)
            sp.wait_ge(s["conv0_ps"], 8 * j + 8)
            load(2 * j + 3, 1)
        sp.wait_ge(s["conv0_ps"], 4 * (STEPS - 2))
        load(STEPS - 1, 0)

    def pool_prog(pool):
        nc.gpsimd.memset(expo[:, :], -0.5).then_inc(s["expo_set"], 1)
        nc.gpsimd.memset(low[3][:, 6400:6401], 0.0).then_inc(s["zeroed_p"], 1)
        pool.wait_ge(s["expo_set"], 1)

        def power(k, slot, cnt):
            pool.wait_ge(q["var"][k], cnt)
            nc.gpsimd.tensor_tensor(rstd[:, slot, :], var[:, slot, :], expo[:, :], ALU.pow).then_inc(q["rstd"][k], 1)

        def lower(k, l, off, cnt):
            pool.wait_ge(q["act"][k], cnt)
            a = act[l][:, bass.ds(off, CHUNK)]
            nc.gpsimd.tensor_tensor(low[l][:, bass.ds(off, CHUNK)], a, high[l][:, bass.ds(off, CHUNK)],
                                    ALU.subtract).then_inc(q["low"][k], 1)

        def step(i, has_b, has_c, has_y=True):
            if has_y:
                power("A", 0, i + 1)
            if has_b:
                lower("B", 1, 1 + CHUNK, i)
            if has_y:
                power("B", 1, i + 1)
            if has_c:
                lower("C", 2, (i - 2) * CHUNK, i - 1)
            if has_b:
                power("C", 2, i)
            if has_y:
                lower("A", 1, 1, i + 1)

        step(0, False, False)
        step(1, True, False)
        with pool.Fori(2, STEPS) as i:
            step(i, True, True)
        lower("B", 1, 1 + CHUNK, STEPS)
        lower("C", 2, (STEPS - 2) * CHUNK, STEPS - 1)
        power("C", 2, STEPS)
        lower("C", 2, (STEPS - 1) * CHUNK, STEPS)

        def tail_power(n):
            pool.wait_ge(s["tail_var"], n + 1)
            l, c, sizes = tail[n]
            k, m = len(sizes), sizes[-1]
            nc.gpsimd.tensor_tensor(rstd[0:m, n % 3, 0:k], var[0:m, n % 3, 0:k], expo[0:m, 0:k],
                                    ALU.pow).then_inc(s["tail_rstd"], 1)

        def tail_lower(n):
            l, c, sizes = tail[n]
            pool.wait_ge(s["tail_act"], n + 1)
            if l < 6:
                m = sum(sizes)
                nc.gpsimd.tensor_tensor(low[l][:, c:c + m], act[l][:, c:c + m], high[l][:, c:c + m],
                                        ALU.subtract).then_inc(s["tail_low"], 1)

        for kind, m in tail_schedule:
            if kind == "conv":
                tail_power(m)
            else:
                tail_lower(m)

    tail_schedule = []
    done_t = 0
    for n in range(len(tail)):
        while done_t < need(n) or done_t < n - 2:
            tail_schedule.append(("turn", done_t))
            done_t += 1
        tail_schedule.append(("conv", n))
    while done_t < len(tail):
        tail_schedule.append(("turn", done_t))
        done_t += 1

    def act_prog(a):
        a.wait_ge(s["w_mean"], 1)
        for w in range(NTAPS):
            nc.scalar.activation(w_cen[:, w, :], raw[:, w, :], ACT.Identity, bias=w_mean[:, w:w + 1],
                                 scale=WS).then_inc(s["w_cen"], 1)
        a.wait_ge(s["w_cen"], NTAPS)
        nc.scalar.activation(w_hi[:, :, :], w_cen, ACT.Copy).then_inc(s["wsplit"], 1)
        a.wait_ge(s["var_sb"], 1)
        nc.scalar.activation(sd[:, :], sd[:, :], ACT.Sqrt, bias=eps1[:, :]).then_inc(s["std_sb"], 1)
        for c in range(PIECES):
            a.wait_ge(s["xn_sb"], c + 1)
            nc.scalar.activation(win_hi[:, c * PIECE:(c + 1) * PIECE], xn0[:, c % 3, :],
                                 ACT.Copy).then_inc(s["hi_sb"], 1)

        def gelu0(i, half, first):
            for c in range(2):
                a.wait_ge(s["conv0_ps"], 4 * i + (2 * half + c + 1))
                if not first:
                    a.wait_ge(q["y"]["B"], i)
                    if half == 1 and c == 1:
                        a.wait_ge(s["halo0"], 2 * i)
                if first and half == 0 and c == 0:
                    a.wait_ge(s["zeroed"], 4)
                off = 1 + half * 1024 + c * CHUNK
                nc.scalar.activation(act[0][:, off:off + CHUNK], z0[c][:, :], ACT.Gelu,
                                     bias=gb[:, 0, 1:2], scale=1.0 / WS).then_inc(s["act0_w"], 1)

        def gelu(k, slot, l, off, cnt):
            a.wait_ge(q["z"][k], cnt)
            nc.scalar.activation(act[l][:, bass.ds(off, CHUNK)], zb[slot][:, :], ACT.Gelu,
                                 bias=gb[:, l, 1:2], scale=gb[:, l, 0:1]).then_inc(q["act"][k], 1)

        def step(i, has_b, has_c, has_next, first=False):
            if has_b:
                if not first:
                    a.wait_ge(s["halo1"], 2 * (i - 1))
                gelu("B", 1, 1, 1 + CHUNK, i)
            if has_next:
                gelu0(i + 1, 0, False)
            if has_c:
                gelu("C", 2, 2, (i - 2) * CHUNK, i - 1)
            if has_next:
                gelu0(i + 1, 1, False)
            if has_b:
                a.wait_ge(q["y"]["C"], i)
                a.wait_ge(q["low"]["B"], i)
                for x in (act[1], low[1]):
                    nc.scalar.activation(x[:, 0:1], x[:, CHUNK * 2:CHUNK * 2 + 1], ACT.Copy).then_inc(s["halo1"], 1)
            gelu("A", 0, 1, 1, i + 1)

        gelu0(0, 0, True)
        gelu0(0, 1, True)
        step(0, False, False, True)
        step(1, True, False, True, first=True)
        with a.Fori(2, STEPS - 1) as i:
            step(i, True, True, True)
        step(STEPS - 1, True, True, False)
        a.wait_ge(s["halo1"], 2 * (STEPS - 1))
        gelu("B", 1, 1, 1 + CHUNK, STEPS)
        gelu("C", 2, 2, (STEPS - 2) * CHUNK, STEPS - 1)
        gelu("C", 2, 2, (STEPS - 1) * CHUNK, STEPS)
        for kind, n in tail_schedule:
            if kind == "turn":
                l, c, sizes = tail[n]
                m = sum(sizes)
                a.wait_ge(s["tail_z"], n + 1)
                if l == 6:
                    dst = act[6][:, :].rearrange("p (b r) -> p r b", b=BATCH)[:, c:c + 4, :]
                    src = zb[n % 3][:, 0:m].rearrange("p (r b) -> p r b", r=4)
                else:
                    dst, src = act[l][:, c:c + m], zb[n % 3][:, 0:m]
                nc.scalar.activation(dst, src, ACT.Gelu,
                                     bias=gb[:, l, 1:2], scale=gb[:, l, 0:1]).then_inc(s["tail_act"], 1)

    def pe_prog(pe):
        pe.wait_ge(s["loaded"], 4 * 16)
        nc.tensor.matmul(zb[0][:, 0:WROWS], cen[:, :], wrep[:, :], start=True, stop=True).then_inc(s["cen_ps"], 1)
        pe.wait_ge(s["cen_sb"], 1)
        nc.tensor.matmul(zb[1][0:WROWS, 0:WROWS], wrepc[:, :], wrepc[:, :], start=True,
                         stop=True).then_inc(s["gram_ps"], 1)
        pe.wait_ge(s["gram_sb"], 1)
        for c in range(PIECES + 1):
            if c < PIECES:
                if c * 4 % PIECES == 0:
                    pe.wait_ge(s[f"win_part{c * 4 // PIECES}"], 16)
                if c >= 2:
                    pe.wait_ge(s["gx_sb"], c - 1)
                nc.tensor.matmul(yb[c % 2][0:WROWS, 0:PIECE], gram[:, :], win[:, c * PIECE:(c + 1) * PIECE],
                                 start=True, stop=True).then_inc(s["gx_ps"], 1)
            if c >= 1:
                pe.wait_ge(s["gx_lo"], c)
                first = P - GROUPS - GROUPS * (c - 1)
                for n, part in enumerate((gt_hi, gt_lo)):
                    last = nc.tensor.matmul(yb[2][:, 0:PIECE], pick[:, first:first + P], part[:, (c - 1) % 2, :],
                                            start=(c == 1 and n == 0), stop=(c == PIECES and n == 1))
                last.then_inc(s["pick_ps"], 1)
        pe.wait_ge(s["loaded2"], 8 * 16)
        pe.wait_ge(s["rstd_sb"], 1)
        for c in range(PIECES):
            if c >= 3:
                pe.wait_ge(s["xn_sb"], c - 2)
            nc.tensor.matmul(zb[c % 3][0:WROWS, 0:PIECE], back[:, c, :], odd(sd[:, :]), start=True, stop=False)
            nc.tensor.matmul(zb[c % 3][0:WROWS, 0:PIECE], back[:, c, :], sd_lo, start=False,
                             stop=True).then_inc(s["rstd_ps"], 1)

        def conv0(i, half, parity, first=False):
            for c in range(2):
                off = half * 1024 + c * CHUNK
                if not first:
                    pe.wait_ge(s["act0_w"], 4 * i + 2 * half + c - 1)
                elif half == 1:
                    pe.wait_ge(s["act0_w"], c + 1)
                nc.tensor.matmul(z0[c][:, :], w0st[0:52, :], wt[0:52, parity, off:off + CHUNK],
                                 start=True, stop=True).then_inc(s["conv0_ps"], 1)

        def conv(bank, l, firsts, sizes):
            last = None
            for ti, (f, m) in enumerate(zip(firsts, sizes)):
                out = bank[0:m, ti * CH:(ti + 1) * CH]
                n, total = 0, 3 * TAPS[l - 1]
                for tap in range(TAPS[l - 1]):
                    hi, lo = f(tap)
                    w = TAP0[l - 1] + tap
                    for x, y in ((hi, w_hi), (hi, w_lo), (lo, w_hi)):
                        last = nc.tensor.matmul(out, x, y[:, w, :], start=(n == 0), stop=(n == total - 1))
                        n += 1
            return last

        def stream_conv(k, slot, l, off):
            fs = [lambda tap, o=off + 256 * j: [x[:, o + tap:o + tap + 255:2] for x in (high[l - 1], low[l - 1])]
                  for j in range(4)]
            conv(yb[slot], l, fs, [P] * 4).then_inc(q["y"][k], 1)

        def turn(k, slot, cnt, gelu_cnt):
            pe.wait_ge(q["norm"][k], cnt)
            if gelu_cnt is not None:
                pe.wait_ge(q["act"][k], gelu_cnt)
            for j in range(4):
                last = nc.tensor.transpose(zb[slot][:, j * P:(j + 1) * P], yn[:, slot, j, :], ident[:, :])
            last.then_inc(q["z"][k], 1)

        def step(i, has_b, has_c, has_next, parity=0, loads=0, z_used=True):
            pe.wait_ge(s["low0_w"], 4 * i + 2)
            pe.wait_ge(s["act0_w"], 4 * i + 2)
            if has_b:
                pe.wait_ge(s["halo0"], 2 * i)
                pe.wait_ge(q["norm"]["A"], i)
            stream_conv("A", 0, 1, 0)
            if has_b:
                turn("B", 1, i, i - 1 if z_used else None)
            pe.wait_ge(s["low0_w"], 4 * i + 4)
            if has_b:
                pe.wait_ge(q["norm"]["B"], i)
            stream_conv("B", 1, 1, 1024)
            if has_next:
                pe.wait_ge(s["win_in"][parity], loads)
                conv0(i + 1, 0, parity)
            if has_c:
                turn("C", 2, i - 1, i - 2 if z_used != "c" else None)
            if has_b:
                pe.wait_ge(q["low"]["A"], i)
                pe.wait_ge(q["low"]["B"], i)
                if has_c:
                    pe.wait_ge(s["halo1"], 2 * (i - 1))
                    pe.wait_ge(q["norm"]["C"], i - 1)
                stream_conv("C", 2, 2, 0)
            if has_next:
                conv0(i + 1, 1, parity)
            turn("A", 0, i + 1, i if has_b else None)

        pe.wait_ge(s["w0split"], 1)
        pe.wait_ge(s["win_in"][0], 32)
        conv0(0, 0, 0, True)
        conv0(0, 1, 0, True)
        pe.wait_ge(s["wsplit"], 2)
        loads = lambda i: 32 * (i // 2 + 1)
        step(0, False, False, True, 1, loads(1))
        step(1, True, False, True, 0, loads(2), z_used=False)
        step(2, True, True, True, 1, loads(3), z_used="c")
        with pe.Fori(0, (STEPS - 5) // 2) as j:
            for d in range(2):
                step(2 * j + (3 + d), True, True, True, d, 32 * j + loads(4 + d))
        step(STEPS - 2, True, True, True, (STEPS - 1) % 2, loads(STEPS - 1))
        step(STEPS - 1, True, True, False)
        turn("B", 1, STEPS, STEPS - 1)
        turn("C", 2, STEPS - 1, STEPS - 2)
        pe.wait_ge(q["low"]["A"], STEPS)
        pe.wait_ge(q["low"]["B"], STEPS)
        pe.wait_ge(s["halo1"], 2 * (STEPS - 1))
        pe.wait_ge(q["norm"]["C"], STEPS - 1)
        stream_conv("C", 2, 2, 0)
        turn("C", 2, STEPS, STEPS - 1)

        pe.wait_ge(q["low"]["C"], STEPS)
        pe.wait_ge(s["zeroed_p"], 1)
        for kind, n in tail_schedule:
            l, c, sizes = tail[n]
            if kind == "conv":
                if need(n):
                    pe.wait_ge(s["tail_low"], need(n))
                if n >= 3:
                    pe.wait_ge(s["tail_norm"], n - 2)
                fs = []
                for ti in range(len(sizes)):
                    if l == 6:
                        fs.append(lambda tap, r=c + ti: [x[:, 2 * r + tap:2 * r + tap + 25 * 63 + 1:25]
                                                         for x in (high[5], low[5])])
                    else:
                        o = 2 * (c + P * ti) + (1 if l == 3 else 0)
                        fs.append(lambda tap, o=o, m=sizes[ti]: [x[:, o + tap:o + tap + 2 * m - 1:2]
                                                              for x in (high[l - 1], low[l - 1])])
                conv(yb[n % 3], l, fs, sizes).then_inc(s["tail_y"], 1)
            else:
                pe.wait_ge(s["tail_norm"], n + 1)
                if n >= 3:
                    pe.wait_ge(s["tail_act"], n - 2)
                off = 0
                for ti, m in enumerate(sizes):
                    last = nc.tensor.transpose(zb[n % 3][:, off:off + m], yn[0:m, n % 3, ti, :], ident[0:m, 0:m])
                    off += m
                last.then_inc(s["tail_z"], 1)

    def dve_prog(v):
        chain = [0]

        def link(ins):
            chain[0] += 1
            ins.then_inc(s["ch_v"], 1)
            v.wait_ge(s["ch_v"], chain[0])

        nc.vector.memset(eps1[:, :], EPS).then_inc(s["zeroed"], 1)
        nc.vector.memset(wt[:, :, :], 0.0).then_inc(s["zeroed"], 1)
        nc.vector.memset(act[0][:, 0:1], 0.0).then_inc(s["zeroed"], 1)
        nc.vector.memset(low[0][:, 0:1], 0.0).then_inc(s["zeroed"], 1)
        link(nc.vector.memset(act[1][:, 0:1], 0.0))
        link(nc.vector.memset(low[1][:, 0:1], 0.0))
        link(nc.vector.memset(act[2][:, 12800:12802], 0.0))
        link(nc.vector.memset(low[2][:, 12800:12802], 0.0))
        link(nc.vector.memset(act[3][:, 6400:6401], 0.0))
        link(nc.vector.memset(w0st[:, :], 0.0))
        v.wait_ge(s["cen_ps"], 1)
        nc.vector.tensor_copy(wrepc[:, :], zb[0][:, 0:WROWS]).then_inc(s["cen_sb"], 1)
        v.wait_ge(s["gram_ps"], 1)
        nc.vector.scalar_tensor_tensor(out=gram[:, :], in0=zb[1][0:WROWS, 0:WROWS], scalar=1.0 / CH, in1=blk[:, :],
                                       op0=ALU.mult, op1=ALU.mult).then_inc(s["gram_sb"], 1)
        v.wait_ge(s["loaded2"], 8 * 16)
        link(nc.vector.reduce_sum(w_mean[:, :], raw, AX))
        nc.vector.tensor_scalar(w_mean[:, :], w_mean[:, :], -WS / CH, None, ALU.mult).then_inc(s["w_mean"], 1)
        for h in range(2):
            rows = slice(32 * h, 32 * h + 20)
            link(nc.vector.reduce_sum(w0_mean[rows, 0:1], raw0[rows, :], AX))
            link(nc.vector.tensor_scalar(w0_mean[rows, 0:1], w0_mean[rows, 0:1], 1.0 / CH, None, ALU.mult))
            link(nc.vector.tensor_scalar(raw0[rows, :], raw0[rows, :], w0_mean[rows, 0:1], WS / 4, ALU.subtract,
                                         ALU.mult))
            link(nc.vector.tensor_tensor(raw0[rows, :], raw0[rows, :], g0rows[rows, :], ALU.mult))
            link(nc.vector.tensor_copy(w0hi[rows, :], raw0[rows, :]))
            if h == 0:
                link(nc.vector.tensor_copy(w0st[rows, :], w0hi[rows, :]))
            else:
                nc.vector.tensor_tensor(w0st[rows, :], raw0[rows, :], w0hi[rows, :],
                                        ALU.subtract).then_inc(s["w0split"], 1)
        for c in range(PIECES):
            v.wait_ge(s["gx_ps"], c + 1)
            if c >= 2:
                v.wait_ge(s["pick_ps"], c - 1)
            nc.vector.tensor_tensor(gt[:, c % 2, :], yb[c % 2][0:WROWS, 0:PIECE],
                                    win[:, c * PIECE:(c + 1) * PIECE], ALU.mult).then_inc(s["gx_sb"], 1)
            v.wait_ge(s["gx_sb"], c + 1)
            nc.vector.tensor_tensor(gt_lo[:, c % 2, :], gt[:, c % 2, :], gt_hi[:, c % 2, :],
                                    ALU.subtract).then_inc(s["gx_lo"], 1)
            if c == PIECES - 2:
                v.wait_ge(s["wsplit"], 1)
                nc.vector.tensor_tensor(w_lo[:, :, :], w_cen, w_hi[:, :, :], ALU.subtract).then_inc(s["wsplit"], 1)
        v.wait_ge(s["pick_ps"], PIECES)
        nc.vector.tensor_scalar(sd[:, :], yb[2][:, 0:PIECE], 0.0, None, ALU.max).then_inc(s["var_sb"], 1)
        v.wait_ge(s["std_sb"], 1)
        link(nc.vector.reciprocal(sd[:, :], sd[:, :]))
        nc.vector.tensor_tensor(sd_lo, sd[:, :], odd(sd[:, :]), ALU.subtract).then_inc(s["rstd_sb"], 1)
        for c in range(PIECES + 1):
            if c < PIECES:
                v.wait_ge(s["rstd_ps"], c + 1)
                if c >= 3:
                    v.wait_ge(s["hi_sb"], c - 2)
                    v.wait_ge(s["lo_sb"], c - 2)
                nc.vector.scalar_tensor_tensor(out=xn0[:, c % 3, :], in0=win[:, c * PIECE:(c + 1) * PIECE], scalar=4.0,
                                               in1=zb[c % 3][0:WROWS, 0:PIECE], op0=ALU.mult,
                                               op1=ALU.mult).then_inc(s["xn_sb"], 1)
            if c >= 1:
                v.wait_ge(s["hi_sb"], c)
                cols = slice((c - 1) * PIECE, c * PIECE)
                nc.vector.tensor_tensor(win_lo[:, cols], xn0[:, (c - 1) % 3, :], win_hi[:, cols],
                                        ALU.subtract).then_inc(s["lo_sb"], 1)

        ch2 = s["ch_p"]

        def stats(bank, slot, sizes, done, base):
            k, m = len(sizes), sizes[-1]
            for j in range(k):
                nc.vector.bn_stats(st[0:sizes[j], slot, j, :], bank[0:sizes[j], j * CH:(j + 1) * CH]).then_inc(ch2, 1)
            v.wait_ge(ch2, base + k)
            nc.vector.tensor_tensor(sq[0:m, slot, 0:k], st[0:m, slot, 0:k, 1], st[0:m, slot, 0:k, 1],
                                    ALU.mult).then_inc(ch2, 1)
            nc.vector.tensor_tensor(s2[0:m, slot, 0:k], st[0:m, slot, 0:k, 2], st[0:m, slot, 0:k, 5],
                                    ALU.add).then_inc(ch2, 1)
            v.wait_ge(ch2, base + k + 2)
            nc.vector.scalar_tensor_tensor(out=s2[0:m, slot, 0:k], in0=s2[0:m, slot, 0:k], scalar=1.0 / CH,
                                           in1=sq[0:m, slot, 0:k], op0=ALU.mult, op1=ALU.add).then_inc(ch2, 1)
            v.wait_ge(ch2, base + k + 3)
            nc.vector.tensor_scalar(var[0:m, slot, 0:k], s2[0:m, slot, 0:k], EPS * WS * WS, None,
                                    ALU.add).then_inc(done, 1)

        def stream_stats(k, slot, cnt, base):
            v.wait_ge(q["y"][k], cnt)
            stats(yb[slot], slot, [P] * 4, q["var"][k], base)

        def norm(k, slot, cnt, reuse=True):
            v.wait_ge(q["rstd"][k], cnt)
            if reuse:
                v.wait_ge(q["z"][k], cnt - 1)
            nc.vector.tensor_tensor(yn[:, slot, :, :], yb[slot][:, :].rearrange("p (j n) -> p j n", j=4),
                                    rstd[:, slot, :].unsqueeze(2).broadcast_to([P, 4, CH]),
                                    ALU.mult).then_inc(q["norm"][k], 1)

        def low0(i, half):
            for c in range(2):
                v.wait_ge(s["act0_w"], 4 * i + 2 * half + c + 1)
                off = 1 + half * 1024 + c * CHUNK
                nc.vector.tensor_tensor(low[0][:, off:off + CHUNK], act[0][:, off:off + CHUNK],
                                        high[0][:, off:off + CHUNK], ALU.subtract).then_inc(s["low0_w"], 1)

        def step(i, has_b, has_c, has_next, base):
            n = 0
            stream_stats("A", 0, i + 1, base)
            n += 7
            if has_b:
                norm("C", 2, i - 1, has_c != "first") if has_c else None
            stream_stats("B", 1, i + 1, base + 7)
            n += 7
            norm("A", 0, i + 1, has_b)
            if has_next:
                v.wait_ge(s["low0_w"], 4 * i + 4)
                nc.vector.tensor_copy(act[0][:, 0:1], act[0][:, BODY0:BODY0 + 1]).then_inc(s["halo0"], 1)
                nc.vector.tensor_copy(low[0][:, 0:1], low[0][:, BODY0:BODY0 + 1]).then_inc(s["halo0"], 1)
                low0(i + 1, 0)
            norm("B", 1, i + 1, has_b)
            if has_b:
                stream_stats("C", 2, i, base + 14)
                n += 7
            if has_next:
                low0(i + 1, 1)
            return n

        low0(0, 0)
        low0(0, 1)
        base = step(0, False, False, True, 0)
        base += step(1, True, False, True, base)
        base += step(2, True, "first", True, base)
        with v.Fori(3, STEPS - 1) as i:
            step(i, True, True, True, 21 * i + (base - 63))
        base += 21 * (STEPS - 4)
        base += step(STEPS - 1, True, True, False, base)
        norm("C", 2, STEPS - 1)
        stream_stats("C", 2, STEPS, base)
        base += 7
        norm("C", 2, STEPS)

        def tail_norm(n):
            l, c, sizes = tail[n]
            k, m = len(sizes), sizes[-1]
            v.wait_ge(s["tail_rstd"], n + 1)
            if n >= 3:
                v.wait_ge(s["tail_z"], n - 2)
            nc.vector.tensor_tensor(yn[0:m, n % 3, 0:k, :], yb[n % 3][0:m, 0:k * CH].rearrange("p (j n) -> p j n", j=k),
                                    rstd[0:m, n % 3, 0:k].unsqueeze(2).broadcast_to([m, k, CH]),
                                    ALU.mult).then_inc(s["tail_norm"], 1)

        pending = None
        for kind, n in tail_schedule:
            if kind == "conv":
                l, c, sizes = tail[n]
                v.wait_ge(s["tail_y"], n + 1)
                stats(yb[n % 3], n % 3, sizes, s["tail_var"], base)
                base += len(sizes) + 3
                if pending is not None:
                    tail_norm(pending)
                pending = n
            elif kind == "turn" and pending == n:
                tail_norm(n)
                pending = None

    return dict(sync=sync_prog, pool=pool_prog, act=act_prog, pe=pe_prog, dve=dve_prog,
                tail=len(tail), s=s, gb=gb)


def conv_inputs(x, inputs):
    pad = np.zeros((BATCH, (SLOTS0 + 1) * STRIDE0), x.dtype)
    pad[:, :x.shape[1]] = x
    blocks = pad.reshape(BATCH, SLOTS0 + 1, STRIDE0)
    stream = np.concatenate([blocks[:, :-1], blocks[:, 1:]], axis=2).reshape(STREAM0, TAPS0)
    stream = np.concatenate([np.zeros((1, TAPS0), x.dtype), stream[:-1]])
    windows = stream.T.reshape(TAPS0, GROUPS, FOLD).transpose(1, 0, 2).reshape(WROWS, FOLD)
    w0 = inputs["L0_tok_conv_w0"][:, 0, :]
    pick = np.zeros((WROWS, 2 * P - GROUPS), np.float16)
    pick[np.arange(WROWS), P - GROUPS + np.arange(WROWS) // TAPS0] = 1
    return {
        "windows": windows,
        "w0rep": np.tile(w0, (1, GROUPS)),
        "w0rows": np.tile(w0.T, (2, 1)),
        "g0rows": np.broadcast_to(inputs["L0_tok_ln_g0"], (2 * TAPS0, CH)),
        "conv_w": np.concatenate([inputs[f"L0_tok_conv_w{l}"].transpose(1, 2, 0) for l in range(1, 7)], axis=1),
        "conv_gb": np.stack([np.stack([inputs[f"L0_tok_ln_g{l}"], inputs[f"L0_tok_ln_b{l}"]], -1)
                             for l in range(7)], axis=1),
        "blk": np.kron(np.eye(GROUPS), np.ones((TAPS0, TAPS0))).astype(np.float32),
        "pick": pick,
        "back": np.concatenate([pick[:, P - GROUPS - GROUPS * c:2 * P - GROUPS - GROUPS * c].T
                                for c in range(PIECES)], axis=1),
        "cen": (np.eye(P) - 1.0 / P).astype(np.float32),
        "ident_d": np.eye(P, dtype=np.float32),
    }


D = 192
HD = 96
NTOK = BATCH * 12
TT = NTOK // P
AT = 8
HEADS, DH = 12, 16
EXPERTS = 10
HID = 768
HT = HID // P
HALF = NTOK // 2
SOFT_SCALE = DH ** -0.5
PI_HALF = float(np.float32(np.pi / 2))


def build_rest(nc, sb, banks, sem, t, act6, conv):
    sems = {}

    shared = {}

    def share(family, tags, signals):
        for name, n in signals.items():
            for k, tag in enumerate(tags):
                shared[tag + name] = (family + name, n * k)

    share("norm", ["f", "ln0", "ln1", "ln2", "ln3", "ln4"], {"_st": TT, "_var": 1, "_std": 1, "_ln": TT})
    share("turn", ["a0", "a1", "f0", "a2", "f1"], {"_T": 3, "_xT": 3})
    share("project", ["tok", "l0p", "l1p"], {"_mm": TT})
    share("att", ["l0", "l1"], {"_qk": 8, "_qkd": 8, "_v": AT, "_vd": AT, "_blk": 2 * AT, "_s": 4 * AT, "_pv": 2 * AT,
                         "_o": AT, "_oT": 4, "_aT": 4})
    for n, name in enumerate(("gate_t", "", "", "", "gate_sin", "gate_tanh")):
        shared[name] = ("gate_act", n)
    for n, name in enumerate(("gate_arg", "gate_int", "gate_int2")):
        shared[name] = ("gate_dve", n)
    shared["x_lo2"] = ("x_lo", 1)

    def S(name):
        name = shared.get(name, (name, 0))[0]
        if name not in sems:
            sems[name] = sem("r_" + name)
        return sems[name]

    def upto(name, n):
        return S(name), shared.get(name, (name, 0))[1] + n

    ident = t["ident"]
    small = t["small_sb"]
    hm = small["headmask"]
    h = sb("h", [P, TT, D], F32)
    x_tok = sb("x_tok", [P, TT, D], F32)
    xT = sb("xT", [HD, 2, NTOK], F32)
    st = sb("r_st", [P, TT, 6], F32)
    mv = sb("r_mv", [P, TT, 2], F32)
    sdv = sb("r_sd", [P, TT], F32)
    eps = sb("r_eps", [P, 1], F32)
    one_row = sb("one_row", [1, P], F32)
    gu_raw = sb("gu_raw", [HD, 2, 2, 2 * HID], F32)
    d_raw = sb("d_raw", [P, 2, HT, D], F32)
    gu_hi = sb("gu_hi", [HD, 2, 2, 2 * HID], F16)
    gu_lo = sb("gu_lo", [HD, 2, 2, 2 * HID], F16)
    d_hi = sb("d_hi", [P, 2, HT, D], F16)
    d_lo = sb("d_lo", [P, 2, HT, D], F16)
    x_lo = sb("x_lo", [HD, 2, NTOK], F16)
    x_hi = xT[:, :, :].bitcast(BF16).rearrange("p a (n two) -> p a n two", two=2)[:, :, :, 1]
    logit = sb("logit", [P, TT, 8], F32)
    score = sb("score", [P, TT, 8], F32)
    top8 = sb("top8", [P, TT, 8], F32)
    topi = sb("topi", [P, TT, 8], U32)
    topf = sb("topf", [P, TT, 8], F32)
    r1 = [sb(f"r1_{i}", [P, TT], F32) for i in range(3)]
    mk = [sb(f"mk{i}", [P, TT, 8], F32) for i in range(2)]
    cw = sb("cw", [P, EXPERTS, TT], F32)
    cwc = sb("cwc", [P, 2, TT], F32)
    attn_ctx = ExitStack()
    attn_sb = lambda n, sh, dt: attn_ctx.enter_context(nc.sbuf_tensor(n, sh, dt))
    x2_tok = attn_sb("x2_tok", [P, TT, D], F32)
    x2T = attn_sb("x2T", [HD, 2, NTOK], F32)
    xn_f = attn_sb("xn_f", [P, TT, CH], F32)
    nT = attn_sb("nT", [P, NTOK], F32)
    qk = attn_sb("qk", [HD, 4, NTOK], F32)
    qe = attn_sb("qe", [HD, 2, HALF], F32)
    qr = attn_sb("qr", [HD, 2, HALF], F32)
    hidT = attn_sb("hidT", [P, NTOK], F32)
    par = attn_sb("par", [HD, AT * HEADS * 5], F32)
    gv = [attn_sb(f"gv{i}", [HD, AT * HEADS], F32) for i in range(5)]
    tempc = attn_sb("tempc", [HD, 1], F32)
    vg = attn_sb("vg", [HD, AT, HEADS, DH + 1], F32)
    blkd = attn_sb("blkd", [HD, 2, 6, HD], F32)
    pr = attn_sb("pr", [HD, 2, 6, HD], F32)
    pt = attn_sb("pt", [HD, 2, 6, HD], F32)
    mxs = attn_sb("mxs", [HD, 2, 6], F32)
    oa = attn_sb("oa", [HD, AT, HEADS, DH], F32)
    osq = attn_sb("osq", [HD, AT, HEADS, DH], F32)
    rden = attn_sb("rden", [HD, AT * HEADS], F32)
    omean = attn_sb("omean", [HD, AT * HEADS], F32)
    ovar = attn_sb("ovar", [HD, AT * HEADS], F32)
    attn_ctx.close()
    hid = sb("hid", [P, 2, HT, HALF], F32)
    hid_hi = hid[:, :, :, :].bitcast(BF16).rearrange("p a j (n two) -> p a j n two", two=2)[:, :, :, :, 1]
    hid_lo = sb("hid_lo", [P, 2, HT, HALF], F16)
    sg = sb("sg", [P, 2, HALF], F32)
    hc = sb("hc", [P, HT, 12, BATCH], F32)
    hc_hi = hc[:, :, :, :].bitcast(BF16).rearrange("p j s (n two) -> p j s n two", two=2)[:, :, :, :, 1]
    hc_lo = sb("hc_lo", [P, HT, 12, BATCH], F16)
    yT = sb("yT", [HD, 2, NTOK], F32)
    yd = sb("yd", [HD, 2, 2, 6, BATCH], F32)
    gl = sb("gl", [HD, 2, 6, BATCH], F32)
    gq = [sb(f"gq{i}", [HD, 6, BATCH], F32) for i in range(3)]
    outb = x_tok

    UP = [(0, (6, 1, 6), None), (1, (0, 1, 2), (0, 1, 2)), (2, (2, 1, 2), (2, 1, 2)), (3, (4, 1, 2), (4, 1, 2)),
          (4, (0, 2, 3), (6, 2, 3)), (5, (1, 2, 3), (7, 2, 3))]
    DOWN = [(0, None, None, None), (1, (6, 1, 2), 1, (0, 1, 2)), (2, (8, 1, 2), 1, (2, 1, 2)),
            (3, (10, 1, 2), 1, (4, 1, 2)), (4, (0, 2, 3), 0, (0, 2, 3)), (5, (1, 2, 3), 0, (1, 2, 3))]

    def rng(r):
        return slice(r[0], r[0] + r[1] * (r[2] - 1) + 1, r[1])

    def sync_prog(sp):
        def load(dst, src, sig):
            sp.dma_start(dst, src).then_inc(sig, 16)

        load(gu_raw[:, 0, :, :], t["gu"][0], S("gu_in0"))
        load(d_raw[:, 0, :, :], t["dn"][0], S("d_in0"))
        load(gu_raw[:, 1, :, :], t["gu"][1], S("gu_in1"))
        load(d_raw[:, 1, :, :], t["dn"][1], S("d_in1"))
        with sp.Fori(0, EXPERTS // 2 - 1) as i:
            for d in range(2):
                sp.wait_ge(*upto(f"gu_split{d}", 2 * i + 2))
                load(gu_raw[:, d, :, :], t["gu_flat"][bass.ds((2 * i + (2 + d)) * HD, HD), :], S(f"gu_in{d}"))
                sp.wait_ge(*upto(f"d_split{d}", 2 * i + 2))
                load(d_raw[:, d, :, :], t["dn_flat"][bass.ds((2 * i + (2 + d)) * P, P), :], S(f"d_in{d}"))
        for u in range(6):
            d = u % 2
            sp.wait_ge(*upto(f"gu_split{d}", EXPERTS + 2 * (u // 2)))
            load(gu_raw[:, d, :, 0:HID], t["up2"][u], S(f"gu_in{d}"))
            if u < 2:
                sp.wait_ge(*upto(f"d_split{d}", EXPERTS))
                load(d_raw[:, d, :, :], t["dn2"][u], S(f"d_in{d}"))
        for u in range(2, 6):
            d = u % 2
            sp.wait_ge(*upto(f"d_split{d}", EXPERTS + 2 * (u // 2)))
            load(d_raw[:, d, :, :], t["dn2"][u], S(f"d_in{d}"))
        sp.wait_ge(*upto("out_ready", TT))
        sp.dma_start(t["out"], outb[:, :, :]).then_inc(S("out_done"), 16)
        sp.wait_ge(*upto("out_done", 16))

    def pe_prog(pe):
        def mm(out, a, b, start=True, stop=True):
            return nc.tensor.matmul(out, a, b, start=start, stop=stop)

        def to_channels(tag, src, wait):
            for j in range(12):
                hf, tt = j // 6, j % 6
                pe.wait_ge(*upto(wait, tt + 1))
                last = nc.tensor.transpose(banks[j // 4][0:HD, (j % 4) * P:(j % 4 + 1) * P],
                                           src[:, tt, hf * HD:(hf + 1) * HD], ident[:, :])
                if j % 4 == 3:
                    last.then_inc(S(tag + "_T"), 1)

        def proj192(tag, lhs, rhs, bias, waits=None):
            for tt in range(TT):
                out = banks[4 + tt // 2][:, (tt % 2) * D:(tt % 2 + 1) * D]
                parts = lhs(tt)
                for i, (a, b) in enumerate(zip(parts, rhs)):
                    mm(out, a, b, start=(i == 0), stop=False)
                mm(out, one_row[:, :], bias, start=False).then_inc(S(tag + "_mm"), 1)

        pe.wait_ge(conv["s"]["tail_act"], conv["tail"])
        pe.wait_ge(t["small_in"], 16 * len(t["small"]))
        pe.wait_ge(*upto("const_set", 2))
        for tt in range(TT):
            nc.tensor.transpose(banks[tt // 4][:, (tt % 4) * P:(tt % 4 + 1) * P], act6[:, tt * P:(tt + 1) * P],
                                ident[:, :]).then_inc(S("f_T"), 1)
        for tt in range(TT):
            pe.wait_ge(*upto("f_ln", tt + 1))
            nc.tensor.transpose(banks[2 + tt // 4][:, (tt % 4) * P:(tt % 4 + 1) * P], xn_f[:, tt, :],
                                ident[:, :]).then_inc(S("f_T2"), 1)
        pe.wait_ge(*upto("f_nT", 2))
        proj192("tok", lambda tt: [nT[:, tt * P:(tt + 1) * P]], [small["proj_w"][:, :]], small["proj_b"][:, :])

        to_channels("a0", x_tok, "ln0_ln")
        pe.wait_ge(*upto("a0_xT", 3))
        to_channels("a1", x2_tok, "ln1_ln")
        for hf in range(2):
            for kt in range(2):
                last = mm(banks[3 + hf][:, 0:HALF], small["Wb1"][:, kt, :], xT[:, kt, hf * HALF:(hf + 1) * HALF],
                          kt == 0, kt == 1)
            last.then_inc(S("hid_mm"), 1)
        pe.wait_ge(*upto("hid_act", 2))
        for a in range(AT):
            last = mm(banks[5][0:HD, a * 60:(a + 1) * 60], hidT[:, a * HD:(a + 1) * HD], small["Wb2"][:, :])
        last.then_inc(S("par_mm"), 1)
        pe.wait_ge(*upto("a1_xT", 3))

        def qkv(tag, w, src, first_free):
            for m in range(4):
                for hf in range(2):
                    n = 2 * m + hf
                    if n >= 2:
                        pe.wait_ge(*upto(tag + "_qkd", n - 1))
                    for kt in range(2):
                        last = mm(banks[n % 2][0:HD, 0:HALF], w[:, kt, m * HD:(m + 1) * HD],
                                  src[:, kt, hf * HALF:(hf + 1) * HALF], kt == 0, kt == 1)
                    last.then_inc(S(tag + "_qk"), 1)

        def vrows(tag, w, bias, src):
            for a in range(AT):
                if a >= 4:
                    pe.wait_ge(*upto(tag + "_vd", a - 3))
                out = banks[2 + a % 4][0:HD, 0:D]
                for kt in range(2):
                    mm(out, src[:, kt, a * HD:(a + 1) * HD], w[:, kt, 2 * D:3 * D], kt == 0, False)
                mm(out, one_row[:, 0:HD], bias[:, 2 * D:3 * D], False).then_inc(S(tag + "_v"), 1)

        qkv("l0", small["Wqkv"], x2T, None)
        pe.wait_ge(*upto("gates", 1))
        vrows("l0", small["Wqkv"], small["bqkv_row"], x2T)
        pe.wait_ge(*upto("l0_vd", AT))
        for n in range(2 * AT + 1):
            if n < 2 * AT:
                a, hf = n // 2, n % 2
                pe.wait_ge(*upto("l0_blk", n + 1))
                if n >= 2:
                    pe.wait_ge(*upto("l0_p", 2 * (n - 1)))
                for g in range(2):
                    mm(banks[2 * (n % 2) + g][0:HD, 0:3 * HD], qk[:, 2 + hf, a * HD:(a + 1) * HD],
                       blkd[:, n % 2, 3 * g:3 * g + 3, :]).then_inc(S("l0_s"), 1)
            if n >= 1:
                m = n - 1
                a, hf = m // 2, m % 2
                pe.wait_ge(*upto("l0_p", 2 * (m + 1)))
                if a >= 2 and hf == 0:
                    pe.wait_ge(*upto("l0_o", a - 1))
                for hd in range(6):
                    c = (hf * 6 + hd) * (DH + 1)
                    last = mm(banks[4 + a % 2][0:HD, c:c + DH + 1], pr[:, m % 2, hd, :], vg[:, a, hf * 6 + hd, :])
                last.then_inc(S("l0_pv"), 1)

        def back(tag):
            for hf in range(2):
                for a in range(AT):
                    last = nc.tensor.transpose(banks[2 * hf + a // 4][0:HD, (a % 4) * HD:(a % 4 + 1) * HD],
                                               oa[:, a, 6 * hf:6 * hf + 6, :], ident[0:HD, 0:HD])
                    if a % 4 == 3:
                        last.then_inc(S(tag), 1)

        pe.wait_ge(*upto("l0_oln", 1))
        back("l0_oT")
        pe.wait_ge(*upto("l0_aT", 4))
        proj192("l0p", lambda tt: [xT[:, kt, tt * P:(tt + 1) * P] for kt in range(2)],
                [small["Wproj"][:, kt, :] for kt in range(2)], small["bproj_row"][:, :])

        to_channels("f0", x_tok, "ln2_ln")
        pe.wait_ge(*upto("f0_xT", 3))
        for tt in range(TT):
            for kt in range(2):
                last = mm(banks[3][:, tt * 8:tt * 8 + 8], xT[:, kt, tt * P:(tt + 1) * P], small["gate_w"][:, kt, :],
                          kt == 0, kt == 1)
        last.then_inc(S("route"), 1)
        pe.wait_ge(*upto("x_lo", 1))
        pe.wait_ge(*upto("route_read", 1))

        def gate_up_unit(i, d, hb, first):
            for j in range(HT):
                cnt = 24 * i + (12 * d + 6 * hb + j)
                if not (first and cnt_is_small(d, hb, j)):
                    pe.wait_ge(*upto("hid_w", cnt - 1))
                for g in range(2):
                    n = 0
                    m0 = g * HID + j * P
                    for kt in range(2):
                        xs = x_hi[:, kt, hb * HALF:(hb + 1) * HALF]
                        xl = x_lo[:, kt, hb * HALF:(hb + 1) * HALF]
                        for w, x in ((gu_hi, xs), (gu_hi, xl), (gu_lo, xs)):
                            last = mm(banks[2 * (j % 2) + g][:, 0:HALF], w[:, d, kt, m0:m0 + P], x, n == 0, n == 5)
                            n += 1
                    last.then_inc(S("gu_mm"), 1)

        def cnt_is_small(d, hb, j):
            return 12 * d + 6 * hb + j < 2

        def down_unit(i, d, hb, first):
            unit = 4 * i + (2 * d + hb)
            pe.wait_ge(*upto("hid_low", 6 * unit + 6))
            if not (first and 2 * d + hb < 2):
                pe.wait_ge(*upto("added", unit * 3 - 3))
            for tt in range(3):
                out = banks[4 + 2 * hb + tt // 2][:, (tt % 2) * D:(tt % 2 + 1) * D]
                n = 0
                for j in range(HT):
                    hs = hid_hi[:, hb, j, tt * P:(tt + 1) * P]
                    hl = hid_lo[:, hb, j, tt * P:(tt + 1) * P]
                    for w, x in ((d_hi, hs), (d_hi, hl), (d_lo, hs)):
                        last = mm(out, x, w[:, d, j, :], n == 0, n == 3 * HT - 1)
                        n += 1
                last.then_inc(S("down"), 1)

        def moe_iter(i, first):
            for d in range(2):
                pe.wait_ge(*upto(f"gu_split{d}", 2 * i + 2))
                for hb in range(2):
                    gate_up_unit(i, d, hb, first)
                    if d or hb:
                        pd, ph = (d, 0) if hb else (0, 1)
                        if ph == 0:
                            pe.wait_ge(*upto(f"d_split{pd}", 2 * i + 2))
                        down_unit(i, pd, ph, first)
            down_unit(i, 1, 1, first)

        moe_iter(0, True)
        with pe.Fori(1, EXPERTS // 2) as i:
            moe_iter(i, False)

        pe.wait_ge(*upto("hid_w", HT * 2 * EXPERTS))
        to_channels("a2", x_tok, "ln3_ln")
        pe.wait_ge(*upto("a2_xT", 3))
        qkv("l1", small["w_qkv"], xT, None)
        pe.wait_ge(*upto("l1_qkd", 8))
        vrows("l1", small["w_qkv"], small["b_qkv_row"], xT)
        pe.wait_ge(*upto("l1_vd", AT))
        for n in range(2 * AT + 2):
            if n < 2 * AT:
                a, hf = n // 2, n % 2
                pe.wait_ge(*upto("l1_blk", n + 1))
                if n >= 2:
                    pe.wait_ge(*upto("l1_sm", 2 * (n - 1)))
                for g in range(2):
                    mm(banks[2 * (n % 2) + g][0:HD, 0:3 * HD], qk[:, hf, a * HD:(a + 1) * HD],
                       blkd[:, n % 2, 3 * g:3 * g + 3, :]).then_inc(S("l1_s"), 1)
            if 1 <= n <= 2 * AT:
                m = n - 1
                pe.wait_ge(*upto("l1_exp", m + 1))
                for g in range(2):
                    if m >= 1:
                        pe.wait_ge(*upto("l1_pt", 2 * (m - 1) + g + 1))
                    for k in range(3):
                        last = nc.tensor.transpose(banks[6 + g][0:HD, k * HD:(k + 1) * HD], pr[:, m % 2, 3 * g + k, :],
                                                   ident[0:HD, 0:HD])
                    last.then_inc(S("l1_pT"), 1)
            if n >= 2:
                m = n - 2
                a, hf = m // 2, m % 2
                pe.wait_ge(*upto("l1_pt", 2 * (m + 1)))
                if a >= 2 and hf == 0:
                    pe.wait_ge(*upto("l1_o", a - 1))
                for hd in range(6):
                    c = (hf * 6 + hd) * (DH + 1)
                    last = mm(banks[4 + a % 2][0:HD, c:c + DH + 1], pt[:, m % 2, hd, :], vg[:, a, hf * 6 + hd, :])
                last.then_inc(S("l1_pv"), 1)
        pe.wait_ge(*upto("l1_o", AT))
        back("l1_oT")
        pe.wait_ge(*upto("l1_aT", 4))
        proj192("l1p", lambda tt: [xT[:, kt, tt * P:(tt + 1) * P] for kt in range(2)],
                [small["w_proj"][:, kt, :] for kt in range(2)], small["b_proj_row"][:, :])

        to_channels("f1", x_tok, "ln4_ln")
        pe.wait_ge(*upto("f1_xT", 3))
        xc = xT[:, :, :].rearrange("p k (b r) -> p k r b", r=12)
        for k in range(2):
            for i in range(6):
                for kt in range(2):
                    last = mm(banks[3 + k][0:HD, i * BATCH:(i + 1) * BATCH], small["G_W"][:, kt, i, k, :], xc[:, kt, i, :],
                              kt == 0, kt == 1)
            last.then_inc(S("glog"), 1)
        pe.wait_ge(*upto("x_lo2", 1))
        xh = x_hi.rearrange("p k (b r) -> p k r b", r=12)
        xl = x_lo[:, :, :].rearrange("p k (b r) -> p k r b", r=12)
        for u, cols, slots in UP:
            d = u % 2
            size = cols[2] * BATCH
            pe.wait_ge(*upto(f"gu_split{d}", EXPERTS + 2 * (u // 2 + 1)))
            for j in range(HT):
                cnt = 6 * u + j
                if cnt >= 2:
                    pe.wait_ge(*upto("up2_act", cnt - 1))
                n = 0
                for kt in range(2):
                    a, b = xh[:, kt, rng(cols), :], xl[:, kt, rng(cols), :]
                    for w, x in ((gu_hi, a), (gu_hi, b), (gu_lo, a)):
                        last = mm(banks[cnt % 2][:, 0:size], w[:, d, kt, j * P:(j + 1) * P], x, n == 0, n == 5)
                        n += 1
                last.then_inc(S("up2_mm"), 1)
        pe.wait_ge(*upto("glog_read", 2))
        for u, slots, direction, classes in DOWN:
            d = u % 2
            pe.wait_ge(*upto(f"d_split{d}", EXPERTS + 2 * (u // 2 + 1)))
            if u == 0:
                pe.wait_ge(*upto("up2_low", 6 * len(UP)))
            size = HALF if slots is None else slots[2] * BATCH
            for m in range(2):
                cnt = 2 * u + m
                if cnt >= 2:
                    pe.wait_ge(*upto("dn2_read", cnt - 1))
                n = 0
                for j in range(HT):
                    if slots is None:
                        a, b = hid_hi[:, 0, j, :], hid_lo[:, 0, j, :]
                    else:
                        a, b = hc_hi[:, j, rng(slots), :], hc_lo[:, j, rng(slots), :]
                    for w, x in ((d_hi, a), (d_hi, b), (d_lo, a)):
                        last = mm(banks[2 + cnt % 2][0:HD, 0:size], w[:, d, j, m * HD:(m + 1) * HD], x, n == 0,
                                  n == 3 * HT - 1)
                        n += 1
                last.then_inc(S("dn2_mm"), 1)
        pe.wait_ge(*upto("yT", 1))
        for tt in range(TT):
            for kt in range(2):
                last = nc.tensor.transpose(banks[4 + tt // 2][:, (tt % 2) * D + kt * HD:(tt % 2) * D + (kt + 1) * HD],
                                           yT[:, kt, tt * P:(tt + 1) * P], ident[0:HD, 0:HD])
            last.then_inc(S("y_tok"), 1)

    def act_prog(a):
        act = nc.scalar.activation

        def std(tag):
            a.wait_ge(*upto(tag + "_var", 1))
            act(sdv[:, :], mv[:, :, 1], ACT.Sqrt, bias=eps[:, :]).then_inc(S(tag + "_std"), 1)

        def evac_T(tag, dst):
            flat = dst[:, :, :].rearrange("p k n -> p (k n)")
            for c in range(3):
                a.wait_ge(*upto(tag + "_T", c + 1))
                act(flat[:, c * 512:(c + 1) * 512], banks[c][0:HD, :], ACT.Copy).then_inc(S(tag + "_xT"), 1)

        std("f")
        std("ln0")
        evac_T("a0", xT)
        std("ln1")
        for hf in range(2):
            a.wait_ge(*upto("hid_mm", hf + 1))
            act(hidT[:, hf * HALF:(hf + 1) * HALF], banks[3 + hf][:, 0:HALF], ACT.Silu).then_inc(S("hid_act"), 1)
        a.wait_ge(*upto("par_sb", 1))
        pv = par[:, :].rearrange("p (n f) -> p n f", f=5)
        act(gv[0][:, :], pv[:, :, 0], ACT.Tanh, scale=0.5).then_inc(S("gate_t"), 1)
        act(gv[1][:, :], pv[:, :, 1], ACT.Tanh).then_inc(S("gate_t"), 1)
        act(gv[2][:, :], pv[:, :, 2], ACT.Tanh, scale=0.5).then_inc(S("gate_t"), 1)
        act(gv[3][:, :], pv[:, :, 3], ACT.Tanh).then_inc(S("gate_t"), 1)
        a.wait_ge(*upto("gate_arg", 1))
        act(gv[1][:, :], gv[1][:, :], ACT.Sin).then_inc(S("gate_sin"), 1)
        a.wait_ge(*upto("gate_int", 1))
        act(gv[0][:, :], gv[0][:, :], ACT.Tanh).then_inc(S("gate_tanh"), 1)
        a.wait_ge(*upto("gate_int2", 1))
        act(gv[0][:, :], gv[0][:, :], ACT.Tanh, scale=0.5).then_inc(S("gate_tanh"), 1)
        for n in range(8):
            a.wait_ge(*upto("l0_qmin", n + 1))
            act(qe[:, n % 2, :], qe[:, n % 2, :], ACT.Exp).then_inc(S("l0_qexp"), 1)
        a.wait_ge(*upto("ovar", 1))
        act(ovar[:, :], ovar[:, :], ACT.Sqrt, bias=eps[0:HD, :], scale=1.0 / DH).then_inc(S("ostd"), 1)
        std("ln2")
        evac_T("f0", xT)
        a.wait_ge(*upto("logit", 1))
        act(score[:, :, :], logit[:, :, :], ACT.Exp).then_inc(S("score_exp"), 1)

        def split_hi(d, cnt, half=False):
            w = HID if half else 2 * HID
            a.wait_ge(*upto(f"gu_in{d}", 16 * cnt))
            act(gu_hi[:, d, :, 0:w], gu_raw[:, d, :, 0:w], ACT.Copy, scale=WS).then_inc(S(f"gu_split{d}"), 1)
            a.wait_ge(*upto(f"d_in{d}", 16 * cnt))
            act(d_hi[:, d, :, :], d_raw[:, d, :, :], ACT.Copy, scale=WS).then_inc(S(f"d_split{d}"), 1)

        def unit(i, d, hb):
            for j in range(HT):
                cnt = 24 * i + (12 * d + 6 * hb + j)
                a.wait_ge(*upto("gu_mm", 2 * cnt + 1))
                if not (type(i) is int and cnt < 2):
                    a.wait_ge(*upto("hid_w", cnt - 1))
                act(sg[:, j % 2, :], banks[2 * (j % 2)][:, 0:HALF], ACT.Silu, scale=1.0 / WS).then_inc(S("silu"), 1)

        def moe_iter(i, last):
            for d in range(2):
                for hb in range(2):
                    unit(i, d, hb)
                    if hb == 0 and not (type(i) is int and i == 0 and d == 0):
                        if d == 0:
                            a.wait_ge(*upto("down", 12 * i))
                            split_hi(1, i + 1)
                        elif not last:
                            a.wait_ge(*upto("down", 12 * i + 6))
                            split_hi(0, i + 2)

        split_hi(0, 1)
        split_hi(1, 1)
        moe_iter(0, False)
        with a.Fori(1, EXPERTS // 2 - 1) as i:
            moe_iter(i, False)
        moe_iter(EXPERTS // 2 - 1, True)

        std("ln3")
        evac_T("a2", xT)
        for n in range(2 * AT):
            a.wait_ge(*upto("l1_sub", n + 1))
            if n >= 2:
                a.wait_ge(*upto("l1_pT", 2 * (n - 1)))
            act(pr[:, n % 2, :, :], pr[:, n % 2, :, :], ACT.Exp, scale=SOFT_SCALE).then_inc(S("l1_exp"), 1)
            for g in range(2):
                a.wait_ge(*upto("l1_pT", 2 * n + g + 1))
                if n >= 2:
                    a.wait_ge(*upto("l1_pv", n - 1))
                act(pt[:, n % 2, 3 * g:3 * g + 3, :], banks[6 + g][0:HD, 0:3 * HD].rearrange("p (k n) -> p k n", k=3),
                    ACT.Copy).then_inc(S("l1_pt"), 1)
        std("ln4")
        evac_T("f1", xT)
        a.wait_ge(*upto("gsub", 1))
        act(gl[:, :, :, :], gl[:, :, :, :], ACT.Exp).then_inc(S("gexp"), 1)

        def split_hi2(u):
            d = u % 2
            n = EXPERTS // 2 + u // 2 + 1
            if u >= 2:
                a.wait_ge(*upto("up2_mm", 6 * (u - 1)))
            a.wait_ge(*upto(f"gu_in{d}", 16 * n))
            act(gu_hi[:, d, :, 0:HID], gu_raw[:, d, :, 0:HID], ACT.Copy, scale=WS).then_inc(S(f"gu_split{d}"), 1)

        def split_hi2d(u):
            d = u % 2
            n = EXPERTS // 2 + u // 2 + 1
            if u >= 2:
                a.wait_ge(*upto("dn2_mm", 2 * (u - 1)))
            a.wait_ge(*upto(f"d_in{d}", 16 * n))
            act(d_hi[:, d, :, :], d_raw[:, d, :, :], ACT.Copy, scale=WS).then_inc(S(f"d_split{d}"), 1)

        a.wait_ge(*upto("down", 6 * EXPERTS))
        split_hi2(0)
        split_hi2(1)
        split_hi2d(0)
        split_hi2d(1)
        for u, cols, slots in UP:
            size = cols[2] * BATCH
            for j in range(HT):
                cnt = 6 * u + j
                a.wait_ge(*upto("up2_mm", cnt + 1))
                src = banks[cnt % 2][:, 0:size].rearrange("p (r b) -> p r b", b=BATCH)
                dst = (hid[:, 0, j, :].rearrange("p (r b) -> p r b", b=BATCH) if slots is None
                       else hc[:, j, rng(slots), :])
                act(dst, src, ACT.Gelu, bias=small["b1"][:, u, j:j + 1], scale=1.0 / WS).then_inc(S("up2_act"), 1)
            if u + 2 < 6:
                split_hi2(u + 2)
        for u in range(2, 6):
            split_hi2d(u)

    def dve_prog(v):
        chain = [0]

        def link(ins):
            chain[0] += 1
            ins.then_inc(S("dve_chain"), 1)
            v.wait_ge(*upto("dve_chain", chain[0]))

        tt_ = nc.vector.tensor_tensor
        ts_ = nc.vector.tensor_scalar
        stt = nc.vector.scalar_tensor_tensor

        def layer_norm(tag, src, dst):
            for i in range(TT):
                nc.vector.bn_stats(st[:, i, :], src(i)).then_inc(S(tag + "_st"), 1)
            v.wait_ge(*upto(tag + "_st", TT))
            for i in range(TT):
                ins = nc.vector.bn_aggr(mv[:, i, :], st[:, i, :])
                if i == TT - 1:
                    ins.then_inc(S(tag + "_var"), 1)
            v.wait_ge(*upto(tag + "_std", 1))
            link(nc.vector.reciprocal(sdv[:, :], sdv[:, :]))
            for i in range(TT):
                ts_(dst(i), src(i), mv[:, i, 0:1], sdv[:, i:i + 1], ALU.subtract, ALU.mult).then_inc(S(tag + "_ln"), 1)

        def add_h(tag, first=False):
            for i in range(TT):
                v.wait_ge(*upto(tag + "_mm", i // 2 * 2 + 2))
                src = banks[4 + i // 2][:, (i % 2) * D:(i % 2 + 1) * D]
                if first:
                    link(nc.vector.tensor_copy(h[:, i, :], src))
                else:
                    link(tt_(h[:, i, :], src, h[:, i, :], ALU.add))

        nc.vector.memset(eps[:, :], EPS).then_inc(S("const_set"), 1)
        nc.vector.memset(one_row[:, :], 1.0).then_inc(S("const_set"), 1)
        v.wait_ge(t["small_in"], 16 * len(t["small"]))
        v.wait_ge(*upto("f_T", TT))
        layer_norm("f", lambda i: banks[i // 4][:, (i % 4) * P:(i % 4 + 1) * P], lambda i: xn_f[:, i, :])
        for c, (lo, hi) in enumerate(((0, 4), (4, 6))):
            v.wait_ge(*upto("f_T2", hi))
            ts_(nT[:, lo * P:hi * P], banks[2 + c][:, 0:(hi - lo) * P], small["fln"][:, 0:1], small["fln"][:, 1:2],
                ALU.mult, ALU.add).then_inc(S("f_nT"), 1)
        add_h("tok", True)
        layer_norm("ln0", lambda i: h[:, i, :], lambda i: x_tok[:, i, :])
        v.wait_ge(*upto("ln0_ln", TT))
        layer_norm("ln1", lambda i: x_tok[:, i, :], lambda i: x2_tok[:, i, :])
        flat = x2T[:, :, :].rearrange("p k n -> p (k n)")
        for c in range(3):
            v.wait_ge(*upto("a1_T", c + 1))
            for lo, hi in ((c * 512, min((c + 1) * 512, NTOK)), (max(c * 512, NTOK), (c + 1) * 512)):
                if lo >= hi:
                    continue
                kt = lo // NTOK
                ins = ts_(flat[:, lo:hi], banks[c][0:HD, lo - c * 512:hi - c * 512], small["ln_wb"][:, 0, kt:kt + 1],
                          small["ln_wb"][:, 1, kt:kt + 1], ALU.mult, ALU.add)
                if hi == (c + 1) * 512:
                    ins.then_inc(S("a1_xT"), 1)
        v.wait_ge(*upto("par_mm", 1))
        nc.vector.tensor_copy(par[:, :], banks[5][0:HD, 0:AT * 60]).then_inc(S("par_sb"), 1)
        link(ts_(tempc[:, :], small["temp"][0:HD, :], 0.1, 2.0, ALU.max, ALU.min))
        v.wait_ge(*upto("gate_t", 4))
        link(tt_(gv[1][:, :], gv[1][:, :], gv[3][:, :], ALU.subtract))
        link(ts_(gv[1][:, :], gv[1][:, :], PI_HALF, 3.1415925, ALU.mult, ALU.min))
        ts_(gv[1][:, :], gv[1][:, :], -3.1415925, None, ALU.max).then_inc(S("gate_arg"), 1)
        link(ts_(gv[0][:, :], gv[0][:, :], 0.5, 0.5, ALU.mult, ALU.add))
        link(ts_(gv[2][:, :], gv[2][:, :], 0.5, 0.5, ALU.mult, ALU.add))
        link(tt_(gv[0][:, :], gv[0][:, :], gv[2][:, :], ALU.mult))
        v.wait_ge(*upto("gate_sin", 1))
        link(tt_(gv[1][:, :], gv[1][:, :], gv[1][:, :], ALU.mult))
        link(ts_(gv[1][:, :], gv[1][:, :], -2.0, 1.0, ALU.mult, ALU.add))
        tt_(gv[0][:, :], gv[0][:, :], gv[1][:, :], ALU.mult).then_inc(S("gate_int"), 1)
        v.wait_ge(*upto("gate_tanh", 1))
        ts_(gv[0][:, :], gv[0][:, :], tempc[:, :], None, ALU.mult).then_inc(S("gate_int2"), 1)
        v.wait_ge(*upto("gate_tanh", 2))
        ts_(gv[4][:, :], gv[0][:, :], 0.5, 1.5, ALU.mult, ALU.add).then_inc(S("gates"), 1)
        nc.vector.memset(vg[:, :, :, DH:DH + 1], 1.0).then_inc(S("vones"), 1)
        for n in range(8):
            m, hf = n // 2, n % 2
            v.wait_ge(*upto("l0_qk", n + 1))
            src = banks[n % 2][0:HD, 0:HALF]
            b = small["bqkv"][:, m:m + 1]
            ts_(qe[:, n % 2, :], src, b, 0.0, ALU.add, ALU.min).then_inc(S("l0_qmin"), 1)
            ts_(qr[:, n % 2, :], src, b, 0.0, ALU.add, ALU.max).then_inc(S("l0_qkd"), 1)
            v.wait_ge(*upto("l0_qexp", n + 1))
            v.wait_ge(*upto("l0_qkd", n + 1))
            tt_(qk[:, m, hf * HALF:(hf + 1) * HALF], qe[:, n % 2, :], qr[:, n % 2, :], ALU.add).then_inc(S("l0_qf"), 1)
        v.wait_ge(*upto("gates", 1))
        gate1 = gv[4][:, :].rearrange("p (a n) -> p a n", a=AT)
        for a in range(AT):
            v.wait_ge(*upto("l0_v", a + 1))
            tt_(vg[:, a, :, 0:DH], banks[2 + a % 4][0:HD, 0:D].rearrange("p (n e) -> p n e", n=HEADS),
                gate1[:, a, :].unsqueeze(2).broadcast_to([HD, HEADS, DH]), ALU.mult).then_inc(S("l0_vd"), 1)

        def spread(n, row, tag, used):
            a, hf = n // 2, n % 2
            if n >= 2:
                v.wait_ge(*upto(used, 2 * (n - 1)))
            tt_(blkd[:, n % 2, :, :], qk[:, row + hf, a * HD:(a + 1) * HD].unsqueeze(1).broadcast_to([HD, 6, HD]),
                hm[:, :].unsqueeze(2).broadcast_to([HD, 6, HD]), ALU.mult).then_inc(S(tag), 1)

        v.wait_ge(*upto("l0_qf", 8))
        v.wait_ge(*upto("vones", 1))
        spread(0, 0, "l0_blk", None)
        causal = small["causal"][:, :].unsqueeze(1).broadcast_to([HD, 3, HD])
        for n in range(2 * AT):
            if n + 1 < 2 * AT:
                spread(n + 1, 0, "l0_blk", "l0_s")
            for g in range(2):
                v.wait_ge(*upto("l0_s", 2 * n + g + 1))
                if n >= 2:
                    v.wait_ge(*upto("l0_pv", n - 1))
                tt_(pr[:, n % 2, 3 * g:3 * g + 3, :],
                    banks[2 * (n % 2) + g][0:HD, 0:3 * HD].rearrange("p (k n) -> p k n", k=3), causal,
                    ALU.mult).then_inc(S("l0_p"), 1)
            if n % 2 == 1 and n > 1:
                o_norm0(v, n // 2 - 1, link, tt_, ts_)
        o_norm0(v, AT - 1, link, tt_, ts_)
        o3 = oa[:, :, :, :].rearrange("p a n e -> p (a n) e")
        q3 = osq[:, :, :, :].rearrange("p a n e -> p (a n) e")
        n3 = AT * HEADS
        v.wait_ge(*upto("l0_o", AT))
        link(nc.vector.reduce_sum(omean[:, :], o3, AX))
        link(ts_(omean[:, :], omean[:, :], 1.0 / DH, None, ALU.mult))
        link(tt_(o3, o3, omean[:, :].unsqueeze(2).broadcast_to([HD, n3, DH]), ALU.subtract))
        link(tt_(q3, o3, o3, ALU.mult))
        nc.vector.reduce_sum(ovar[:, :], q3, AX).then_inc(S("ovar"), 1)
        v.wait_ge(*upto("ostd", 1))
        link(nc.vector.reciprocal(ovar[:, :], ovar[:, :]))
        tt_(o3, o3, ovar[:, :].unsqueeze(2).broadcast_to([HD, n3, DH]), ALU.mult).then_inc(S("l0_oln"), 1)
        for c in range(4):
            v.wait_ge(*upto("l0_oT", c + 1))
            ts_(xT[:, c // 2, (c % 2) * HALF:(c % 2 + 1) * HALF], banks[c][0:HD, 0:HALF], small["mn"][:, 0:1],
                small["mn"][:, 1:2], ALU.mult, ALU.add).then_inc(S("l0_aT"), 1)
        add_h("l0p")

        layer_norm("ln2", lambda i: h[:, i, :], lambda i: x_tok[:, i, :])
        v.wait_ge(*upto("f0_xT", 3))
        tt_(x_lo[:, :, :], xT[:, :, :], x_hi, ALU.subtract).then_inc(S("x_lo"), 1)
        v.wait_ge(*upto("route", 1))
        lg = banks[3][:, 0:TT * 8].rearrange("p (t e) -> p t e", e=8)
        bc = lambda x: x[:, :].unsqueeze(2).broadcast_to([P, TT, 8])
        link(nc.vector.tensor_reduce(r1[0][:, :], lg, AX, ALU.max))
        tt_(logit[:, :, :], lg, bc(r1[0]), ALU.subtract).then_inc(S("logit"), 1)
        v.wait_ge(*upto("logit", 1))
        v.wait_ge(*upto("score_exp", 1))
        nc.vector.reduce_sum(r1[0][:, :], score[:, :, :], AX).then_inc(S("route_read"), 1)
        v.wait_ge(*upto("route_read", 1))
        link(nc.vector.reciprocal(r1[0][:, :], r1[0][:, :]))
        link(tt_(score[:, :, :], score[:, :, :], bc(r1[0]), ALU.mult))
        for i in range(TT):
            link(nc.vector.max(top8[:, i, :], score[:, i, :]))
            link(nc.vector.max_index(topi[:, i, :], top8[:, i, :], score[:, i, :]))
        link(nc.vector.tensor_copy(topf[:, :, :], topi[:, :, :]))
        iota = small["iota8"][:, :].unsqueeze(1).broadcast_to([P, TT, 8])
        link(tt_(r1[1][:, :], top8[:, :, 0], top8[:, :, 1], ALU.add))
        link(ts_(r1[1][:, :], r1[1][:, :], 1e-8, None, ALU.add))
        link(nc.vector.reciprocal(r1[1][:, :], r1[1][:, :]))
        link(ts_(r1[1][:, :], r1[1][:, :], 1.0 / WS, None, ALU.mult))
        for k in range(2):
            link(nc.vector.tensor_copy(r1[2][:, :], topf[:, :, k]))
            link(tt_(mk[k][:, :, :], iota, bc(r1[2]), ALU.is_equal))
            link(tt_(r1[2][:, :], top8[:, :, k], r1[1][:, :], ALU.mult))
            link(tt_(mk[k][:, :, :], mk[k][:, :, :], bc(r1[2]), ALU.mult))
        link(tt_(cw[:, 0:8, :], mk[0][:, :, :].rearrange("p t e -> p e t"), mk[1][:, :, :].rearrange("p t e -> p e t"),
                 ALU.add))
        link(nc.vector.memset(cw[:, 8:10, :], 0.5 / WS))

        def split_lo(d, cnt, half=False):
            w = HID if half else 2 * HID
            v.wait_ge(*upto(f"gu_split{d}", 2 * cnt - 1))
            stt(out=gu_lo[:, d, :, 0:w], in0=gu_raw[:, d, :, 0:w], scalar=WS, in1=gu_hi[:, d, :, 0:w], op0=ALU.mult,
                op1=ALU.subtract).then_inc(S(f"gu_split{d}"), 1)
            v.wait_ge(*upto(f"d_split{d}", 2 * cnt - 1))
            stt(out=d_lo[:, d, :, :], in0=d_raw[:, d, :, :], scalar=WS, in1=d_hi[:, d, :, :], op0=ALU.mult,
                op1=ALU.subtract).then_inc(S(f"d_split{d}"), 1)

        def unit(i, d, hb):
            for j in range(HT):
                cnt = 24 * i + (12 * d + 6 * hb + j)
                v.wait_ge(*upto("gu_mm", 2 * cnt + 2))
                v.wait_ge(*upto("silu", cnt + 1))
                stt(out=hid[:, hb, j, :], in0=banks[2 * (j % 2) + 1][:, 0:HALF], scalar=1.0 / WS, in1=sg[:, j % 2, :],
                    op0=ALU.mult, op1=ALU.mult).then_inc(S("hid_w"), 1)
                v.wait_ge(*upto("hid_w", cnt + 1))
                tt_(hid_lo[:, hb, j, :], hid[:, hb, j, :], hid_hi[:, hb, j, :], ALU.subtract).then_inc(S("hid_low"), 1)

        def add(i, d, hb):
            n0 = 12 * i + (6 * d + 3 * hb)
            for k in range(3):
                v.wait_ge(*upto("down", n0 + (2, 2, 3)[k]))
                src = banks[4 + 2 * hb + k // 2][:, (k % 2) * D:(k % 2 + 1) * D]
                tk = 3 * hb + k
                stt(out=h[:, tk, :], in0=src, scalar=cwc[:, d, tk:tk + 1], in1=h[:, tk, :], op0=ALU.mult,
                    op1=ALU.add).then_inc(S("added"), 1)

        def moe_iter(i, last):
            first = type(i) is int and i == 0
            if not first:
                v.wait_ge(*upto("added", 12 * i))
            nc.vector.tensor_copy(cwc[:, :, :], cw[:, bass.ds(2 * i, 2), :]).then_inc(S("cwc"), 1)
            v.wait_ge(*upto("cwc", i + 1))
            for d in range(2):
                for hb in range(2):
                    if not (first and d == 0):
                        v.wait_ge(*upto("down", 12 * i + (6 * d + 3 * hb - 3)))
                    unit(i, d, hb)
                    if hb == 0 and not (first and d == 0):
                        if d == 0:
                            split_lo(1, i + 1)
                        elif not last:
                            split_lo(0, i + 2)
                    if d or hb:
                        add(i, *((d, 0) if hb else (0, 1)))
            add(i, 1, 1)

        split_lo(0, 1)
        split_lo(1, 1)
        moe_iter(0, False)
        with v.Fori(1, EXPERTS // 2 - 1) as i:
            moe_iter(i, False)
        moe_iter(EXPERTS // 2 - 1, True)
        v.wait_ge(*upto("added", 6 * EXPERTS))

        layer_norm("ln3", lambda i: h[:, i, :], lambda i: x_tok[:, i, :])
        for n in range(8):
            m, hf = n // 2, n % 2
            v.wait_ge(*upto("l1_qk", n + 1))
            ts_(qk[:, m, hf * HALF:(hf + 1) * HALF], banks[n % 2][0:HD, 0:HALF], small["b_qkv"][:, m:m + 1], None,
                ALU.add).then_inc(S("l1_qkd"), 1)
        for a in range(AT):
            v.wait_ge(*upto("l1_v", a + 1))
            nc.vector.tensor_copy(vg[:, a, :, 0:DH],
                                  banks[2 + a % 4][0:HD, 0:D].rearrange("p (n e) -> p n e", n=HEADS)).then_inc(S("l1_vd"), 1)
        v.wait_ge(*upto("l1_qkd", 8))
        spread(0, 2, "l1_blk", None)
        same = small["same"][:, :].unsqueeze(1).broadcast_to([HD, 3, HD])
        for n in range(2 * AT):
            if n + 1 < 2 * AT:
                spread(n + 1, 2, "l1_blk", "l1_s")
            if n >= 2:
                v.wait_ge(*upto("l1_pT", 2 * (n - 1)))
            for g in range(2):
                v.wait_ge(*upto("l1_s", 2 * n + g + 1))
                tt_(pr[:, n % 2, 3 * g:3 * g + 3, :],
                    banks[2 * (n % 2) + g][0:HD, 0:3 * HD].rearrange("p (k n) -> p k n", k=3), same,
                    ALU.add).then_inc(S("l1_sm"), 1)
            v.wait_ge(*upto("l1_sm", 2 * n + 2))
            link(nc.vector.tensor_reduce(mxs[:, n % 2, :], pr[:, n % 2, :, :], AX, ALU.max))
            tt_(pr[:, n % 2, :, :], pr[:, n % 2, :, :], mxs[:, n % 2, :].unsqueeze(2).broadcast_to([HD, 6, HD]),
                ALU.subtract).then_inc(S("l1_sub"), 1)
            if n % 2 == 1 and n > 1:
                o_norm1(v, n // 2 - 1, link, tt_)
        o_norm1(v, AT - 1, link, tt_)
        for c in range(4):
            v.wait_ge(*upto("l1_oT", c + 1))
            nc.vector.tensor_copy(xT[:, c // 2, (c % 2) * HALF:(c % 2 + 1) * HALF],
                                  banks[c][0:HD, 0:HALF]).then_inc(S("l1_aT"), 1)
        add_h("l1p")

        layer_norm("ln4", lambda i: h[:, i, :], lambda i: x_tok[:, i, :])
        v.wait_ge(*upto("f1_xT", 3))
        tt_(x_lo[:, :, :], xT[:, :, :], x_hi, ALU.subtract).then_inc(S("x_lo2"), 1)
        v.wait_ge(*upto("glog", 2))
        l0 = banks[3][0:HD, 0:HALF].rearrange("p (i b) -> p i b", i=6)
        l1 = banks[4][0:HD, 0:HALF].rearrange("p (i b) -> p i b", i=6)
        link(nc.vector.tensor_copy(gq[1][:, :, :], l0))
        link(tt_(gq[0][:, :, :], l1, gq[1][:, :, :], ALU.max))
        tt_(gl[:, 0, :, :], l0, gq[0][:, :, :], ALU.subtract).then_inc(S("glog_read"), 1)
        tt_(gl[:, 1, :, :], l1, gq[0][:, :, :], ALU.subtract).then_inc(S("glog_read"), 1)
        v.wait_ge(*upto("glog_read", 2))
        nc.vector.memset(sdv[:, 0:1], 0.0).then_inc(S("gsub"), 1)
        v.wait_ge(*upto("gexp", 1))
        link(tt_(gq[0][:, :, :], gl[:, 0, :, :], gl[:, 1, :, :], ALU.add))
        link(nc.vector.reciprocal(gq[0][:, :, :], gq[0][:, :, :]))
        link(tt_(gl[:, 0, :, :], gl[:, 0, :, :], gq[0][:, :, :], ALU.mult))
        link(tt_(gl[:, 1, :, :], gl[:, 1, :, :], gq[0][:, :, :], ALU.mult))
        link(tt_(gq[0][:, :, :], gl[:, 0, :, :], gl[:, 1, :, :], ALU.min))
        for k in range(2):
            link(tt_(gq[1 + k][:, :, :], gl[:, k, :, :], gq[0][:, :, :], ALU.is_gt))
            link(tt_(gl[:, k, :, :], gl[:, k, :, :], gq[1 + k][:, :, :], ALU.mult))
        link(tt_(gq[0][:, :, :], gl[:, 0, :, :], gl[:, 1, :, :], ALU.add))
        link(ts_(gq[0][:, :, :], gq[0][:, :, :], 1e-6, None, ALU.max))
        link(nc.vector.reciprocal(gq[0][:, :, :], gq[0][:, :, :]))
        for k in range(2):
            link(tt_(gl[:, k, :, :], gl[:, k, :, :], gq[0][:, :, :], ALU.mult))

        def split_lo2(u):
            d, cnt = u % 2, EXPERTS // 2 + u // 2 + 1
            v.wait_ge(*upto(f"gu_split{d}", 2 * cnt - 1))
            stt(out=gu_lo[:, d, :, 0:HID], in0=gu_raw[:, d, :, 0:HID], scalar=WS, in1=gu_hi[:, d, :, 0:HID],
                op0=ALU.mult, op1=ALU.subtract).then_inc(S(f"gu_split{d}"), 1)

        def split_lo2d(u):
            d, cnt = u % 2, EXPERTS // 2 + u // 2 + 1
            v.wait_ge(*upto(f"d_split{d}", 2 * cnt - 1))
            stt(out=d_lo[:, d, :, :], in0=d_raw[:, d, :, :], scalar=WS, in1=d_hi[:, d, :, :], op0=ALU.mult,
                op1=ALU.subtract).then_inc(S(f"d_split{d}"), 1)

        split_lo2(0)
        split_lo2(1)
        split_lo2d(0)
        split_lo2d(1)
        for u, cols, slots in UP:
            for j in range(HT):
                v.wait_ge(*upto("up2_act", 6 * u + j + 1))
                if slots is None:
                    tt_(hid_lo[:, 0, j, :], hid[:, 0, j, :], hid_hi[:, 0, j, :], ALU.subtract).then_inc(S("up2_low"), 1)
                else:
                    tt_(hc_lo[:, j, rng(slots), :], hc[:, j, rng(slots), :], hc_hi[:, j, rng(slots), :],
                        ALU.subtract).then_inc(S("up2_low"), 1)
            if u + 2 < 6:
                split_lo2(u + 2)
        yr = yT[:, :, :].rearrange("p k (b r) -> p k r b", r=12)
        for u, slots, direction, classes in DOWN:
            for m in range(2):
                cnt = 2 * u + m
                v.wait_ge(*upto("dn2_mm", cnt + 1))
                if slots is None:
                    src = banks[2 + cnt % 2][0:HD, 0:HALF].rearrange("p (r b) -> p r b", b=BATCH)
                    dst = yr[:, m, 6:12, :]
                else:
                    src = banks[2 + cnt % 2][0:HD, 0:slots[2] * BATCH].rearrange("p (r b) -> p r b", b=BATCH)
                    dst = yd[:, direction, m, rng(classes), :]
                ts_(dst, src, 1.0 / WS, small["b2"][:, m, u:u + 1], ALU.mult, ALU.add).then_inc(S("dn2_read"), 1)
            if u + 2 < 6:
                split_lo2d(u + 2)
        v.wait_ge(*upto("dn2_read", 12))
        for m in range(2):
            for k in range(2):
                link(tt_(yd[:, k, m, :, :], yd[:, k, m, :, :], gl[:, k, :, :], ALU.mult))
            ins = tt_(yr[:, m, 0:6, :], yd[:, 0, m, :, :], yd[:, 1, m, :, :], ALU.add)
        ins.then_inc(S("yT"), 1)
        for i in range(TT):
            v.wait_ge(*upto("y_tok", i // 2 * 2 + 2))
            tt_(outb[:, i, :], banks[4 + i // 2][:, (i % 2) * D:(i % 2 + 1) * D], h[:, i, :],
                ALU.add).then_inc(S("out_ready"), 1)

    def o_norm0(v, a, link, tt_, ts_):
        v.wait_ge(*upto("l0_pv", 2 * a + 2))
        o = banks[4 + a % 2][0:HD, 0:HEADS * (DH + 1)].rearrange("p (n e) -> p n e", n=HEADS)
        r = rden[:, a * HEADS:(a + 1) * HEADS]
        link(ts_(r, o[:, :, DH], 1e-6, None, ALU.add))
        link(nc.vector.reciprocal(r, r))
        tt_(oa[:, a, :, :], o[:, :, 0:DH], r.unsqueeze(2).broadcast_to([HD, HEADS, DH]),
            ALU.mult).then_inc(S("l0_o"), 1)

    def o_norm1(v, a, link, tt_):
        v.wait_ge(*upto("l1_pv", 2 * a + 2))
        o = banks[4 + a % 2][0:HD, 0:HEADS * (DH + 1)].rearrange("p (n e) -> p n e", n=HEADS)
        r = rden[:, a * HEADS:(a + 1) * HEADS]
        link(nc.vector.reciprocal(r, o[:, :, DH]))
        tt_(oa[:, a, :, :], o[:, :, 0:DH], r.unsqueeze(2).broadcast_to([HD, HEADS, DH]),
            ALU.mult).then_inc(S("l1_o"), 1)

    return dict(sync=sync_prog, act=act_prog, pe=pe_prog, dve=dve_prog)


def halves(w):
    return w.reshape(2, HD, -1).transpose(1, 0, 2)


def rest_inputs(i):
    b12 = np.arange(HD) // 12
    same = b12[:, None] == b12[None, :]
    causal = same & (np.arange(HD)[:, None] <= np.arange(HD)[None, :])
    up1 = [np.concatenate([i[f"L0_ffn_{k}_gate"], i[f"L0_ffn_{k}_up"]], axis=1) for k in ("routed", "shared")]
    gu = np.concatenate(up1)
    dn = np.concatenate([i["L0_ffn_routed_down"], i["L0_ffn_shared_down"]])
    up2 = np.concatenate([i["L1_ffn_moe0_W1"][None], i["L1_ffn_A1_W"]])
    dn2 = np.concatenate([i["L1_ffn_moe0_W2"][None], i["L1_ffn_A2_W"]])
    b1 = np.concatenate([i["L1_ffn_moe0_b1"][None], i["L1_ffn_A1_b"]])
    b2 = np.concatenate([i["L1_ffn_moe0_b2"][None], i["L1_ffn_A2_b"]])
    small = {
        "fln": np.stack([i["L0_tok_fln_g"], i["L0_tok_fln_b"]], -1),
        "proj_w": i["L0_tok_proj_w"], "proj_b": i["L0_tok_proj_b"][None],
        "Wb1": halves(i["L0_attn_Wb1"]), "Wb2": i["L0_attn_Wb2"],
        "Wqkv": halves(i["L0_attn_Wqkv"]), "bqkv": i["L0_attn_bqkv"].reshape(6, HD).T,
        "bqkv_row": i["L0_attn_bqkv"][None],
        "ln_wb": np.stack([i["L0_attn_ln_w"].reshape(2, HD).T, i["L0_attn_ln_b"].reshape(2, HD).T], 1),
        "temp": np.broadcast_to(i["L0_attn_temperature"][None], (P, 1)),
        "mn": np.stack([np.tile(i["L0_attn_mn_w"], 6), np.tile(i["L0_attn_mn_b"], 6)], -1),
        "Wproj": halves(i["L0_attn_Wproj"]), "bproj_row": i["L0_attn_bproj"][None],
        "gate_w": halves(i["L0_ffn_gate_w"].T),
        "w_qkv": halves(i["L1_attn_w_qkv"]), "b_qkv": i["L1_attn_b_qkv"].reshape(6, HD).T,
        "b_qkv_row": i["L1_attn_b_qkv"][None],
        "w_proj": halves(i["L1_attn_w_proj"]), "b_proj_row": i["L1_attn_b_proj"][None],
        "G_W": np.broadcast_to(i["L1_ffn_G_W"].reshape(6, 2, HD, 2).transpose(2, 1, 0, 3)[..., None], (HD, 2, 6, 2, HD)),
        "b1": b1.reshape(6, HT, P).transpose(2, 0, 1), "b2": b2.reshape(6, 2, HD).transpose(2, 1, 0),
        "headmask": (np.arange(HD)[:, None] // DH == np.arange(6)[None]).astype(np.float32),
        "causal": causal.astype(np.float32), "same": np.where(same, 0.0, -1e30).astype(np.float32),
        "iota8": np.broadcast_to(np.arange(8, dtype=np.float32), (P, 8)),
    }
    large = {
        "gu": gu.transpose(0, 2, 1).reshape(EXPERTS, 2, HD, 2 * HID).transpose(0, 2, 1, 3),
        "dn": dn.transpose(0, 2, 1).reshape(EXPERTS, HT, P, D).transpose(0, 2, 1, 3),
        "up2": up2.reshape(6, 2, HD, HID).transpose(0, 2, 1, 3),
        "dn2": dn2.reshape(6, HT, P, D).transpose(0, 2, 1, 3),
    }
    return small, large


def build(nc, t, out):
    with ExitStack() as ctx, ExitStack() as conv_ctx:
        sb = lambda n, sh, dt: ctx.enter_context(nc.sbuf_tensor(n, sh, dt))
        conv_sb = lambda n, sh, dt: conv_ctx.enter_context(nc.sbuf_tensor(n, sh, dt))
        sem = lambda n: ctx.enter_context(nc.semaphore(n))
        banks = [ctx.enter_context(nc.psum_tensor(f"bank{i}", [P, 512], F32)) for i in range(8)]
        t["ident"] = sb("ident", [P, P], F32)
        t["scratch"] = nc.dram_tensor("scratch", (2, TAPS0, STREAM0), F16).ap()
        t["out"] = out.rearrange("b r d -> (b r) d").rearrange("(t p) d -> p t d", p=P)
        t["gu_flat"] = t["gu"].rearrange("e p k n -> (e p) (k n)")
        t["dn_flat"] = t["dn"].rearrange("e p k n -> (e p) (k n)")
        act6 = sb("act6", [P, NTOK], F32)
        t["small_sb"] = {n: sb("s_" + n, list(a.shape), F32) for n, a in t["small"].items()}
        t["small_in"] = sem("small_in")

        def load_small(sp):
            for n, a in t["small"].items():
                sp.dma_start(t["small_sb"][n][tuple(slice(None) for _ in a.shape)], a).then_inc(t["small_in"], 16)

        conv = build_conv(nc, conv_sb, lambda i: banks[i], sem, t, act6, load_small)
        conv_ctx.close()
        rest = build_rest(nc, sb, banks, sem, t, act6, conv)
        block = ctx.enter_context(nc.Block())

        @block.sync
        def _(sp):
            conv["sync"](sp)
            sp.wait_ge(conv["s"]["tail_act"], conv["tail"])
            rest["sync"](sp)

        @block.gpsimd
        def _(pool):
            conv["pool"](pool)

        @block.scalar
        def _(act):
            conv["act"](act)
            rest["act"](act)

        @block.tensor
        def _(pe):
            conv["pe"](pe)
            rest["pe"](pe)

        @block.vector
        def _(dve):
            conv["dve"](dve)
            dve.wait_ge(conv["s"]["tail_act"], conv["tail"])
            rest["dve"](dve)


def kernel(**inputs):
    import concourse.bacc as bacc
    from concourse.bass_utils import run_bass_kernel_spmd

    inputs = {k: np.asarray(v) for k, v in inputs.items()}
    small, large = rest_inputs(inputs)
    nc = bacc.Bacc("TRN2", target_bir_lowering=False, num_devices=1)
    arrays, t = {}, {"small": {}}
    for group, given in ((t, conv_inputs(inputs["x"], inputs)), (t["small"], small), (t, large)):
        for n, a in given.items():
            a = np.ascontiguousarray(a)
            arrays["in_" + n] = a
            group[n] = nc.dram_tensor("in_" + n, a.shape, mybir.dt.from_np(a.dtype), kind="ExternalInput").ap()
    out = nc.dram_tensor("out", (BATCH, 12, D), F32, kind="ExternalOutput").ap()
    build(nc, t, out)
    r = run_bass_kernel_spmd(nc, [arrays], core_ids=[0])
    return r.results[0]["out"]
```

```python
from contextlib import ExitStack

import numpy as np
import concourse.bass as bass
from concourse import mybir

F32 = mybir.dt.float32
F16 = mybir.dt.float16
BF16 = mybir.dt.bfloat16
U32 = mybir.dt.uint32
ALU = mybir.AluOpType
ACT = mybir.ActivationFunctionType
AX = mybir.AxisListType.X

P = 128
BATCH = 64
CH = 128
TAPS0, STRIDE0 = 10, 5
SLOTS0 = 800
STREAM0 = BATCH * SLOTS0
GROUPS = 8
FOLD = STREAM0 // GROUPS
WROWS = GROUPS * TAPS0
PIECE = 400
PIECES = FOLD // PIECE
CHUNK = 512
BODY0 = 2048
STEPS = STREAM0 // BODY0
WS = 256.0
EPS = 1e-5
TAPS = [3, 3, 3, 3, 2, 2]
TAP0 = [0, 3, 6, 9, 12, 14]
NTAPS = 16


def conv_tail_chunks():
    out = []
    for layer, tokens in ((3, 6400), (4, 3200), (5, 1600)):
        for c in range(0, tokens, CHUNK):
            n = min(CHUNK, tokens - c)
            out.append((layer, c, [min(P, n - t) for t in range(0, n, P)]))
    for r in range(0, 12, 4):
        out.append((6, r, [BATCH] * 4))
    return out


def build_conv(nc, sb, ps, sem, t, act6, load_small):
    scr = t["scratch"]

    tail_ctx = ExitStack()
    tail_sb = lambda n, sh, dt: tail_ctx.enter_context(nc.sbuf_tensor(n, sh, dt))
    act = {2: sb("act2", [P, 12802], F32), 3: sb("act3", [P, 6401], F32), 6: act6}
    low = {2: sb("low2", [P, 12802], F16), 3: sb("low3", [P, 6401], F16)}
    act[4], act[5] = tail_sb("act4", [P, 3200], F32), tail_sb("act5", [P, 1600], F32)
    low[4], low[5] = tail_sb("low4", [P, 3200], F16), tail_sb("low5", [P, 1600], F16)
    tail_ctx.close()
    act[0], act[1] = sb("act0", [P, 1 + BODY0], F32), sb("act1", [P, 1 + BODY0 // 2], F32)
    low[0], low[1] = sb("low0", [P, 1 + BODY0], F16), sb("low1", [P, 1 + BODY0 // 2], F16)
    wt = sb("wt", [64, 2, BODY0], F16)
    high = {l: act[l][:, :].bitcast(BF16).rearrange("p (n two) -> p n two", two=2)[:, :, 1] for l in range(6)}
    win = act[2][0:WROWS, 0:FOLD]
    win_hi = low[2][0:WROWS, 0:FOLD]
    win_lo = low[2][0:WROWS, FOLD:2 * FOLD]
    raw = act[3][:, 0:NTAPS * CH].rearrange("p (t n) -> p t n", t=NTAPS)
    raw0 = act[2][0:64, 2 * FOLD - 2 * CH:2 * FOLD - CH]
    g0rows = act[2][0:64, 2 * FOLD - CH:2 * FOLD]
    w_cen = act[3][:, NTAPS * CH:2 * NTAPS * CH].rearrange("p (t n) -> p t n", t=NTAPS)
    w_hi = sb("w_hi", [P, NTAPS, CH], F16)
    w_lo = sb("w_lo", [P, NTAPS, CH], F16)
    w_mean = sb("w_mean", [P, NTAPS], F32)
    w0_mean = sb("w0_mean", [64, 1], F32)
    w0st = sb("w0st", [64, CH], F16)
    w0hi = sb("w0hi", [64, CH], F16)
    wrep = sb("wrep", [P, WROWS], F32)
    wrepc = sb("wrepc", [P, WROWS], F32)
    gram = sb("gram", [WROWS, WROWS], F32)
    blk = sb("blk", [WROWS, WROWS], F32)
    f16_area = act[2][:, FOLD:FOLD + P + PIECES * WROWS // 2].bitcast(F16)
    pick = f16_area[0:WROWS, 0:2 * P - GROUPS]
    back = f16_area[:, 2 * P:2 * P + PIECES * WROWS].rearrange("p (c r) -> p c r", c=PIECES)
    cen = sb("cen", [P, P], F32)
    gt = act[1][0:WROWS, 1:1 + 2 * PIECE].rearrange("p (k n) -> p k n", k=2)
    odd = lambda x: x.bitcast(BF16).rearrange("p (n two) -> p n two", two=2)[:, :, 1]
    gt_hi = odd(act[1][0:WROWS, 1:1 + 2 * PIECE]).rearrange("p (k n) -> p k n", k=2)
    gt_lo = low[1][0:WROWS, 1:1 + 2 * PIECE].rearrange("p (k n) -> p k n", k=2)
    sd_lo = low[0][:, 1:1 + PIECE]
    sd = sb("sd", [P, PIECE], F32)
    xn0 = act[0][0:WROWS, 1:1 + 3 * PIECE].rearrange("p (k n) -> p k n", k=3)
    ident = t["ident"]
    gb = sb("gb", [P, 7, 2], F32)
    eps1 = sb("eps1", [P, 1], F32)
    expo = sb("expo", [P, 4], F32)
    st = sb("st", [P, 3, 4, 6], F32)
    sq = sb("sq", [P, 3, 4], F32)
    s2 = sb("s2", [P, 3, 4], F32)
    var = sb("var", [P, 3, 4], F32)
    rstd = sb("rstd", [P, 3, 4], F32)
    yn = sb("yn", [P, 3, 4, CH], F32)

    yb = [ps(i) for i in range(3)]
    zb = [ps(i + 3) for i in range(3)]
    z0 = [ps(6), ps(7)]

    names = ["loaded", "loaded2", "cen_ps", "cen_sb", "gram_ps", "gram_sb", "wsplit", "w0split", "gx_ps", "gx_sb", "gx_lo", "pick_ps",
             "var_sb", "std_sb", "rstd_sb", "rstd_ps", "xn_sb", "hi_sb", "lo_sb", "w_mean", "w_cen", "ch_v", "scr_out0",
             "scr_out", "win_part0", "win_part1", "win_part2", "win_part3", "conv0_ps", "act0_w", "low0_w", "halo0", "halo1",
             "zeroed", "zeroed_p", "expo_set", "tail_y", "tail_var", "tail_rstd", "tail_norm", "tail_z",
             "tail_act", "tail_low", "ch_p"]
    s = {n: sem("c_" + n) for n in names}
    s["win_in"] = [sem(f"c_win_in{i}") for i in range(2)]
    kinds = "ABC"
    q = {n: {k: sem(f"c_{n}{k}") for k in kinds} for n in
         ["y", "var", "rstd", "norm", "z", "act", "low"]}
    tail = conv_tail_chunks()
    tail_index = {}
    for n, (l, c, sizes) in enumerate(tail):
        tail_index[(l, c)] = n

    def need(n):
        l, c, sizes = tail[n]
        if l == 3:
            return 0
        if l == 6:
            return max(i for i, (ll, cc, ss) in enumerate(tail) if ll == 5) + 1
        end = 2 * (c + sum(sizes)) + (1 if l == 4 else 0)
        return max(i for i, (ll, cc, ss) in enumerate(tail) if ll == l - 1 and cc < end) + 1

    def sync_prog(sp):
        for dst, src in ((wrep[:, :], t["w0rep"]), (blk[:, :], t["blk"]), (cen[:, :], t["cen"]),
                         (pick, t["pick"])):
            sp.dma_start(dst, src).then_inc(s["loaded"], 16)
        for part in range(4):
            cols = slice(part * FOLD // 4, (part + 1) * FOLD // 4)
            sp.dma_start(win[:, cols], t["windows"][:, cols]).then_inc(s[f"win_part{part}"], 16)
        for dst, src in ((raw, t["conv_w"]), (gb[:, :, :], t["conv_gb"]), (ident[:, :], t["ident_d"]),
                         (back, t["back"])):
            sp.dma_start(dst, src).then_inc(s["loaded2"], 16)
        for h in range(2):
            sp.dma_start(raw0[32 * h:32 * h + 20, :], t["w0rows"]).then_inc(s["loaded2"], 16)
            sp.dma_start(g0rows[32 * h:32 * h + 20, :], t["g0rows"]).then_inc(s["loaded2"], 16)
        load_small(sp)
        sp.wait_ge(s["hi_sb"], PIECES)
        sp.wait_ge(s["lo_sb"], PIECES)
        for g in range(GROUPS):
            for h, src in enumerate((win_hi, win_lo)):
                sp.dma_start(scr[h, :, g * FOLD:(g + 1) * FOLD],
                             src[g * TAPS0:(g + 1) * TAPS0, :]).then_inc(s["scr_out" if g else "scr_out0"], 16)
        rows = scr.rearrange("h k n -> (h k) n")

        def load(i, par):
            for h in range(2):
                sp.dma_start(wt[32 * h:32 * h + 20, par, :],
                             rows[:, bass.ds(i * BODY0, BODY0)]).then_inc(s["win_in"][par], 16)

        sp.wait_ge(s["scr_out0"], 16 * 2)
        sp.wait_ge(s["zeroed"], 2)
        load(0, 0)
        load(1, 1)
        sp.wait_ge(s["scr_out"], 16 * 2 * (GROUPS - 1))
        with sp.Fori(0, (STEPS - 3) // 2) as j:
            sp.wait_ge(s["conv0_ps"], 8 * j + 4)
            load(2 * j + 2, 0)
            sp.wait_ge(s["conv0_ps"], 8 * j + 8)
            load(2 * j + 3, 1)
        sp.wait_ge(s["conv0_ps"], 4 * (STEPS - 2))
        load(STEPS - 1, 0)

    def pool_prog(pool):
        nc.gpsimd.memset(expo[:, :], -0.5).then_inc(s["expo_set"], 1)
        nc.gpsimd.memset(low[3][:, 6400:6401], 0.0).then_inc(s["zeroed_p"], 1)
        pool.wait_ge(s["expo_set"], 1)

        def power(k, slot, cnt):
            pool.wait_ge(q["var"][k], cnt)
            nc.gpsimd.tensor_tensor(rstd[:, slot, :], var[:, slot, :], expo[:, :], ALU.pow).then_inc(q["rstd"][k], 1)

        def lower(k, l, off, cnt):
            pool.wait_ge(q["act"][k], cnt)
            a = act[l][:, bass.ds(off, CHUNK)]
            nc.gpsimd.tensor_tensor(low[l][:, bass.ds(off, CHUNK)], a, high[l][:, bass.ds(off, CHUNK)],
                                    ALU.subtract).then_inc(q["low"][k], 1)

        def step(i, has_b, has_c, has_y=True):
            if has_y:
                power("A", 0, i + 1)
            if has_b:
                lower("B", 1, 1 + CHUNK, i)
            if has_y:
                power("B", 1, i + 1)
            if has_c:
                lower("C", 2, (i - 2) * CHUNK, i - 1)
            if has_b:
                power("C", 2, i)
            if has_y:
                lower("A", 1, 1, i + 1)

        step(0, False, False)
        step(1, True, False)
        with pool.Fori(2, STEPS) as i:
            step(i, True, True)
        lower("B", 1, 1 + CHUNK, STEPS)
        lower("C", 2, (STEPS - 2) * CHUNK, STEPS - 1)
        power("C", 2, STEPS)
        lower("C", 2, (STEPS - 1) * CHUNK, STEPS)

        def tail_power(n):
            pool.wait_ge(s["tail_var"], n + 1)
            l, c, sizes = tail[n]
            k, m = len(sizes), sizes[-1]
            nc.gpsimd.tensor_tensor(rstd[0:m, n % 3, 0:k], var[0:m, n % 3, 0:k], expo[0:m, 0:k],
                                    ALU.pow).then_inc(s["tail_rstd"], 1)

        def tail_lower(n):
            l, c, sizes = tail[n]
            pool.wait_ge(s["tail_act"], n + 1)
            if l < 6:
                m = sum(sizes)
                nc.gpsimd.tensor_tensor(low[l][:, c:c + m], act[l][:, c:c + m], high[l][:, c:c + m],
                                        ALU.subtract).then_inc(s["tail_low"], 1)

        for kind, m in tail_schedule:
            if kind == "conv":
                tail_power(m)
            else:
                tail_lower(m)

    tail_schedule = []
    done_t = 0
    for n in range(len(tail)):
        while done_t < need(n) or done_t < n - 2:
            tail_schedule.append(("turn", done_t))
            done_t += 1
        tail_schedule.append(("conv", n))
    while done_t < len(tail):
        tail_schedule.append(("turn", done_t))
        done_t += 1

    def act_prog(a):
        a.wait_ge(s["w_mean"], 1)
        for w in range(NTAPS):
            nc.scalar.activation(w_cen[:, w, :], raw[:, w, :], ACT.Identity, bias=w_mean[:, w:w + 1],
                                 scale=WS).then_inc(s["w_cen"], 1)
        a.wait_ge(s["w_cen"], NTAPS)
        nc.scalar.activation(w_hi[:, :, :], w_cen, ACT.Copy).then_inc(s["wsplit"], 1)
        a.wait_ge(s["var_sb"], 1)
        nc.scalar.activation(sd[:, :], sd[:, :], ACT.Sqrt, bias=eps1[:, :]).then_inc(s["std_sb"], 1)
        for c in range(PIECES):
            a.wait_ge(s["xn_sb"], c + 1)
            nc.scalar.activation(win_hi[:, c * PIECE:(c + 1) * PIECE], xn0[:, c % 3, :],
                                 ACT.Copy).then_inc(s["hi_sb"], 1)

        def gelu0(i, half, first):
            for c in range(2):
                a.wait_ge(s["conv0_ps"], 4 * i + (2 * half + c + 1))
                if not first:
                    a.wait_ge(q["y"]["B"], i)
                    if half == 1 and c == 1:
                        a.wait_ge(s["halo0"], 2 * i)
                if first and half == 0 and c == 0:
                    a.wait_ge(s["zeroed"], 4)
                off = 1 + half * 1024 + c * CHUNK
                nc.scalar.activation(act[0][:, off:off + CHUNK], z0[c][:, :], ACT.Gelu,
                                     bias=gb[:, 0, 1:2], scale=1.0 / WS).then_inc(s["act0_w"], 1)

        def gelu(k, slot, l, off, cnt):
            a.wait_ge(q["z"][k], cnt)
            nc.scalar.activation(act[l][:, bass.ds(off, CHUNK)], zb[slot][:, :], ACT.Gelu,
                                 bias=gb[:, l, 1:2], scale=gb[:, l, 0:1]).then_inc(q["act"][k], 1)

        def step(i, has_b, has_c, has_next, first=False):
            if has_b:
                if not first:
                    a.wait_ge(s["halo1"], 2 * (i - 1))
                gelu("B", 1, 1, 1 + CHUNK, i)
            if has_next:
                gelu0(i + 1, 0, False)
            if has_c:
                gelu("C", 2, 2, (i - 2) * CHUNK, i - 1)
            if has_next:
                gelu0(i + 1, 1, False)
            if has_b:
                a.wait_ge(q["y"]["C"], i)
                a.wait_ge(q["low"]["B"], i)
                for x in (act[1], low[1]):
                    nc.scalar.activation(x[:, 0:1], x[:, CHUNK * 2:CHUNK * 2 + 1], ACT.Copy).then_inc(s["halo1"], 1)
            gelu("A", 0, 1, 1, i + 1)

        gelu0(0, 0, True)
        gelu0(0, 1, True)
        step(0, False, False, True)
        step(1, True, False, True, first=True)
        with a.Fori(2, STEPS - 1) as i:
            step(i, True, True, True)
        step(STEPS - 1, True, True, False)
        a.wait_ge(s["halo1"], 2 * (STEPS - 1))
        gelu("B", 1, 1, 1 + CHUNK, STEPS)
        gelu("C", 2, 2, (STEPS - 2) * CHUNK, STEPS - 1)
        gelu("C", 2, 2, (STEPS - 1) * CHUNK, STEPS)
        for kind, n in tail_schedule:
            if kind == "turn":
                l, c, sizes = tail[n]
                m = sum(sizes)
                a.wait_ge(s["tail_z"], n + 1)
                if l == 6:
                    dst = act[6][:, :].rearrange("p (b r) -> p r b", b=BATCH)[:, c:c + 4, :]
                    src = zb[n % 3][:, 0:m].rearrange("p (r b) -> p r b", r=4)
                else:
                    dst, src = act[l][:, c:c + m], zb[n % 3][:, 0:m]
                nc.scalar.activation(dst, src, ACT.Gelu,
                                     bias=gb[:, l, 1:2], scale=gb[:, l, 0:1]).then_inc(s["tail_act"], 1)

    def pe_prog(pe):
        pe.wait_ge(s["loaded"], 4 * 16)
        nc.tensor.matmul(zb[0][:, 0:WROWS], cen[:, :], wrep[:, :], start=True, stop=True).then_inc(s["cen_ps"], 1)
        pe.wait_ge(s["cen_sb"], 1)
        nc.tensor.matmul(zb[1][0:WROWS, 0:WROWS], wrepc[:, :], wrepc[:, :], start=True,
                         stop=True).then_inc(s["gram_ps"], 1)
        pe.wait_ge(s["gram_sb"], 1)
        for c in range(PIECES + 1):
            if c < PIECES:
                if c * 4 % PIECES == 0:
                    pe.wait_ge(s[f"win_part{c * 4 // PIECES}"], 16)
                if c >= 2:
                    pe.wait_ge(s["gx_sb"], c - 1)
                nc.tensor.matmul(yb[c % 2][0:WROWS, 0:PIECE], gram[:, :], win[:, c * PIECE:(c + 1) * PIECE],
                                 start=True, stop=True).then_inc(s["gx_ps"], 1)
            if c >= 1:
                pe.wait_ge(s["gx_lo"], c)
                first = P - GROUPS - GROUPS * (c - 1)
                for n, part in enumerate((gt_hi, gt_lo)):
                    last = nc.tensor.matmul(yb[2][:, 0:PIECE], pick[:, first:first + P], part[:, (c - 1) % 2, :],
                                            start=(c == 1 and n == 0), stop=(c == PIECES and n == 1))
                last.then_inc(s["pick_ps"], 1)
        pe.wait_ge(s["loaded2"], 8 * 16)
        pe.wait_ge(s["rstd_sb"], 1)
        for c in range(PIECES):
            if c >= 3:
                pe.wait_ge(s["xn_sb"], c - 2)
            nc.tensor.matmul(zb[c % 3][0:WROWS, 0:PIECE], back[:, c, :], odd(sd[:, :]), start=True, stop=False)
            nc.tensor.matmul(zb[c % 3][0:WROWS, 0:PIECE], back[:, c, :], sd_lo, start=False,
                             stop=True).then_inc(s["rstd_ps"], 1)

        def conv0(i, half, parity, first=False):
            for c in range(2):
                off = half * 1024 + c * CHUNK
                if not first:
                    pe.wait_ge(s["act0_w"], 4 * i + 2 * half + c - 1)
                elif half == 1:
                    pe.wait_ge(s["act0_w"], c + 1)
                nc.tensor.matmul(z0[c][:, :], w0st[0:52, :], wt[0:52, parity, off:off + CHUNK],
                                 start=True, stop=True).then_inc(s["conv0_ps"], 1)

        def conv(bank, l, firsts, sizes):
            last = None
            for ti, (f, m) in enumerate(zip(firsts, sizes)):
                out = bank[0:m, ti * CH:(ti + 1) * CH]
                n, total = 0, 3 * TAPS[l - 1]
                for tap in range(TAPS[l - 1]):
                    hi, lo = f(tap)
                    w = TAP0[l - 1] + tap
                    for x, y in ((hi, w_hi), (hi, w_lo), (lo, w_hi)):
                        last = nc.tensor.matmul(out, x, y[:, w, :], start=(n == 0), stop=(n == total - 1))
                        n += 1
            return last

        def stream_conv(k, slot, l, off):
            fs = [lambda tap, o=off + 256 * j: [x[:, o + tap:o + tap + 255:2] for x in (high[l - 1], low[l - 1])]
                  for j in range(4)]
            conv(yb[slot], l, fs, [P] * 4).then_inc(q["y"][k], 1)

        def turn(k, slot, cnt, gelu_cnt):
            pe.wait_ge(q["norm"][k], cnt)
            if gelu_cnt is not None:
                pe.wait_ge(q["act"][k], gelu_cnt)
            for j in range(4):
                last = nc.tensor.transpose(zb[slot][:, j * P:(j + 1) * P], yn[:, slot, j, :], ident[:, :])
            last.then_inc(q["z"][k], 1)

        def step(i, has_b, has_c, has_next, parity=0, loads=0, z_used=True):
            pe.wait_ge(s["low0_w"], 4 * i + 2)
            pe.wait_ge(s["act0_w"], 4 * i + 2)
            if has_b:
                pe.wait_ge(s["halo0"], 2 * i)
                pe.wait_ge(q["norm"]["A"], i)
            stream_conv("A", 0, 1, 0)
            if has_b:
                turn("B", 1, i, i - 1 if z_used else None)
            pe.wait_ge(s["low0_w"], 4 * i + 4)
            if has_b:
                pe.wait_ge(q["norm"]["B"], i)
            stream_conv("B", 1, 1, 1024)
            if has_next:
                pe.wait_ge(s["win_in"][parity], loads)
                conv0(i + 1, 0, parity)
            if has_c:
                turn("C", 2, i - 1, i - 2 if z_used != "c" else None)
            if has_b:
                pe.wait_ge(q["low"]["A"], i)
                pe.wait_ge(q["low"]["B"], i)
                if has_c:
                    pe.wait_ge(s["halo1"], 2 * (i - 1))
                    pe.wait_ge(q["norm"]["C"], i - 1)
                stream_conv("C", 2, 2, 0)
            if has_next:
                conv0(i + 1, 1, parity)
            turn("A", 0, i + 1, i if has_b else None)

        pe.wait_ge(s["w0split"], 1)
        pe.wait_ge(s["win_in"][0], 32)
        conv0(0, 0, 0, True)
        conv0(0, 1, 0, True)
        pe.wait_ge(s["wsplit"], 2)
        loads = lambda i: 32 * (i // 2 + 1)
        step(0, False, False, True, 1, loads(1))
        step(1, True, False, True, 0, loads(2), z_used=False)
        step(2, True, True, True, 1, loads(3), z_used="c")
        with pe.Fori(0, (STEPS - 5) // 2) as j:
            for d in range(2):
                step(2 * j + (3 + d), True, True, True, d, 32 * j + loads(4 + d))
        step(STEPS - 2, True, True, True, (STEPS - 1) % 2, loads(STEPS - 1))
        step(STEPS - 1, True, True, False)
        turn("B", 1, STEPS, STEPS - 1)
        turn("C", 2, STEPS - 1, STEPS - 2)
        pe.wait_ge(q["low"]["A"], STEPS)
        pe.wait_ge(q["low"]["B"], STEPS)
        pe.wait_ge(s["halo1"], 2 * (STEPS - 1))
        pe.wait_ge(q["norm"]["C"], STEPS - 1)
        stream_conv("C", 2, 2, 0)
        turn("C", 2, STEPS, STEPS - 1)

        pe.wait_ge(q["low"]["C"], STEPS)
        pe.wait_ge(s["zeroed_p"], 1)
        for kind, n in tail_schedule:
            l, c, sizes = tail[n]
            if kind == "conv":
                if need(n):
                    pe.wait_ge(s["tail_low"], need(n))
                if n >= 3:
                    pe.wait_ge(s["tail_norm"], n - 2)
                fs = []
                for ti in range(len(sizes)):
                    if l == 6:
                        fs.append(lambda tap, r=c + ti: [x[:, 2 * r + tap:2 * r + tap + 25 * 63 + 1:25]
                                                         for x in (high[5], low[5])])
                    else:
                        o = 2 * (c + P * ti) + (1 if l == 3 else 0)
                        fs.append(lambda tap, o=o, m=sizes[ti]: [x[:, o + tap:o + tap + 2 * m - 1:2]
                                                              for x in (high[l - 1], low[l - 1])])
                conv(yb[n % 3], l, fs, sizes).then_inc(s["tail_y"], 1)
            else:
                pe.wait_ge(s["tail_norm"], n + 1)
                if n >= 3:
                    pe.wait_ge(s["tail_act"], n - 2)
                off = 0
                for ti, m in enumerate(sizes):
                    last = nc.tensor.transpose(zb[n % 3][:, off:off + m], yn[0:m, n % 3, ti, :], ident[0:m, 0:m])
                    off += m
                last.then_inc(s["tail_z"], 1)

    def dve_prog(v):
        chain = [0]

        def link(ins):
            chain[0] += 1
            ins.then_inc(s["ch_v"], 1)
            v.wait_ge(s["ch_v"], chain[0])

        nc.vector.memset(eps1[:, :], EPS).then_inc(s["zeroed"], 1)
        nc.vector.memset(wt[:, :, :], 0.0).then_inc(s["zeroed"], 1)
        nc.vector.memset(act[0][:, 0:1], 0.0).then_inc(s["zeroed"], 1)
        nc.vector.memset(low[0][:, 0:1], 0.0).then_inc(s["zeroed"], 1)
        link(nc.vector.memset(act[1][:, 0:1], 0.0))
        link(nc.vector.memset(low[1][:, 0:1], 0.0))
        link(nc.vector.memset(act[2][:, 12800:12802], 0.0))
        link(nc.vector.memset(low[2][:, 12800:12802], 0.0))
        link(nc.vector.memset(act[3][:, 6400:6401], 0.0))
        link(nc.vector.memset(w0st[:, :], 0.0))
        v.wait_ge(s["cen_ps"], 1)
        nc.vector.tensor_copy(wrepc[:, :], zb[0][:, 0:WROWS]).then_inc(s["cen_sb"], 1)
        v.wait_ge(s["gram_ps"], 1)
        nc.vector.scalar_tensor_tensor(out=gram[:, :], in0=zb[1][0:WROWS, 0:WROWS], scalar=1.0 / CH, in1=blk[:, :],
                                       op0=ALU.mult, op1=ALU.mult).then_inc(s["gram_sb"], 1)
        v.wait_ge(s["loaded2"], 8 * 16)
        link(nc.vector.reduce_sum(w_mean[:, :], raw, AX))
        nc.vector.tensor_scalar(w_mean[:, :], w_mean[:, :], -WS / CH, None, ALU.mult).then_inc(s["w_mean"], 1)
        for h in range(2):
            rows = slice(32 * h, 32 * h + 20)
            link(nc.vector.reduce_sum(w0_mean[rows, 0:1], raw0[rows, :], AX))
            link(nc.vector.tensor_scalar(w0_mean[rows, 0:1], w0_mean[rows, 0:1], 1.0 / CH, None, ALU.mult))
            link(nc.vector.tensor_scalar(raw0[rows, :], raw0[rows, :], w0_mean[rows, 0:1], WS / 4, ALU.subtract,
                                         ALU.mult))
            link(nc.vector.tensor_tensor(raw0[rows, :], raw0[rows, :], g0rows[rows, :], ALU.mult))
            link(nc.vector.tensor_copy(w0hi[rows, :], raw0[rows, :]))
            if h == 0:
                link(nc.vector.tensor_copy(w0st[rows, :], w0hi[rows, :]))
            else:
                nc.vector.tensor_tensor(w0st[rows, :], raw0[rows, :], w0hi[rows, :],
                                        ALU.subtract).then_inc(s["w0split"], 1)
        for c in range(PIECES):
            v.wait_ge(s["gx_ps"], c + 1)
            if c >= 2:
                v.wait_ge(s["pick_ps"], c - 1)
            nc.vector.tensor_tensor(gt[:, c % 2, :], yb[c % 2][0:WROWS, 0:PIECE],
                                    win[:, c * PIECE:(c + 1) * PIECE], ALU.mult).then_inc(s["gx_sb"], 1)
            v.wait_ge(s["gx_sb"], c + 1)
            nc.vector.tensor_tensor(gt_lo[:, c % 2, :], gt[:, c % 2, :], gt_hi[:, c % 2, :],
                                    ALU.subtract).then_inc(s["gx_lo"], 1)
            if c == PIECES - 2:
                v.wait_ge(s["wsplit"], 1)
                nc.vector.tensor_tensor(w_lo[:, :, :], w_cen, w_hi[:, :, :], ALU.subtract).then_inc(s["wsplit"], 1)
        v.wait_ge(s["pick_ps"], PIECES)
        nc.vector.tensor_scalar(sd[:, :], yb[2][:, 0:PIECE], 0.0, None, ALU.max).then_inc(s["var_sb"], 1)
        v.wait_ge(s["std_sb"], 1)
        link(nc.vector.reciprocal(sd[:, :], sd[:, :]))
        nc.vector.tensor_tensor(sd_lo, sd[:, :], odd(sd[:, :]), ALU.subtract).then_inc(s["rstd_sb"], 1)
        for c in range(PIECES + 1):
            if c < PIECES:
                v.wait_ge(s["rstd_ps"], c + 1)
                if c >= 3:
                    v.wait_ge(s["hi_sb"], c - 2)
                    v.wait_ge(s["lo_sb"], c - 2)
                nc.vector.scalar_tensor_tensor(out=xn0[:, c % 3, :], in0=win[:, c * PIECE:(c + 1) * PIECE], scalar=4.0,
                                               in1=zb[c % 3][0:WROWS, 0:PIECE], op0=ALU.mult,
                                               op1=ALU.mult).then_inc(s["xn_sb"], 1)
            if c >= 1:
                v.wait_ge(s["hi_sb"], c)
                cols = slice((c - 1) * PIECE, c * PIECE)
                nc.vector.tensor_tensor(win_lo[:, cols], xn0[:, (c - 1) % 3, :], win_hi[:, cols],
                                        ALU.subtract).then_inc(s["lo_sb"], 1)

        ch2 = s["ch_p"]

        def stats(bank, slot, sizes, done, base):
            k, m = len(sizes), sizes[-1]
            for j in range(k):
                nc.vector.bn_stats(st[0:sizes[j], slot, j, :], bank[0:sizes[j], j * CH:(j + 1) * CH]).then_inc(ch2, 1)
            v.wait_ge(ch2, base + k)
            nc.vector.tensor_tensor(sq[0:m, slot, 0:k], st[0:m, slot, 0:k, 1], st[0:m, slot, 0:k, 1],
                                    ALU.mult).then_inc(ch2, 1)
            nc.vector.tensor_tensor(s2[0:m, slot, 0:k], st[0:m, slot, 0:k, 2], st[0:m, slot, 0:k, 5],
                                    ALU.add).then_inc(ch2, 1)
            v.wait_ge(ch2, base + k + 2)
            nc.vector.scalar_tensor_tensor(out=s2[0:m, slot, 0:k], in0=s2[0:m, slot, 0:k], scalar=1.0 / CH,
                                           in1=sq[0:m, slot, 0:k], op0=ALU.mult, op1=ALU.add).then_inc(ch2, 1)
            v.wait_ge(ch2, base + k + 3)
            nc.vector.tensor_scalar(var[0:m, slot, 0:k], s2[0:m, slot, 0:k], EPS * WS * WS, None,
                                    ALU.add).then_inc(done, 1)

        def stream_stats(k, slot, cnt, base):
            v.wait_ge(q["y"][k], cnt)
            stats(yb[slot], slot, [P] * 4, q["var"][k], base)

        def norm(k, slot, cnt, reuse=True):
            v.wait_ge(q["rstd"][k], cnt)
            if reuse:
                v.wait_ge(q["z"][k], cnt - 1)
            nc.vector.tensor_tensor(yn[:, slot, :, :], yb[slot][:, :].rearrange("p (j n) -> p j n", j=4),
                                    rstd[:, slot, :].unsqueeze(2).broadcast_to([P, 4, CH]),
                                    ALU.mult).then_inc(q["norm"][k], 1)

        def low0(i, half):
            for c in range(2):
                v.wait_ge(s["act0_w"], 4 * i + 2 * half + c + 1)
                off = 1 + half * 1024 + c * CHUNK
                nc.vector.tensor_tensor(low[0][:, off:off + CHUNK], act[0][:, off:off + CHUNK],
                                        high[0][:, off:off + CHUNK], ALU.subtract).then_inc(s["low0_w"], 1)

        def step(i, has_b, has_c, has_next, base):
            n = 0
            stream_stats("A", 0, i + 1, base)
            n += 7
            if has_b:
                norm("C", 2, i - 1, has_c != "first") if has_c else None
            stream_stats("B", 1, i + 1, base + 7)
            n += 7
            norm("A", 0, i + 1, has_b)
            if has_next:
                v.wait_ge(s["low0_w"], 4 * i + 4)
                nc.vector.tensor_copy(act[0][:, 0:1], act[0][:, BODY0:BODY0 + 1]).then_inc(s["halo0"], 1)
                nc.vector.tensor_copy(low[0][:, 0:1], low[0][:, BODY0:BODY0 + 1]).then_inc(s["halo0"], 1)
                low0(i + 1, 0)
            norm("B", 1, i + 1, has_b)
            if has_b:
                stream_stats("C", 2, i, base + 14)
                n += 7
            if has_next:
                low0(i + 1, 1)
            return n

        low0(0, 0)
        low0(0, 1)
        base = step(0, False, False, True, 0)
        base += step(1, True, False, True, base)
        base += step(2, True, "first", True, base)
        with v.Fori(3, STEPS - 1) as i:
            step(i, True, True, True, 21 * i + (base - 63))
        base += 21 * (STEPS - 4)
        base += step(STEPS - 1, True, True, False, base)
        norm("C", 2, STEPS - 1)
        stream_stats("C", 2, STEPS, base)
        base += 7
        norm("C", 2, STEPS)

        def tail_norm(n):
            l, c, sizes = tail[n]
            k, m = len(sizes), sizes[-1]
            v.wait_ge(s["tail_rstd"], n + 1)
            if n >= 3:
                v.wait_ge(s["tail_z"], n - 2)
            nc.vector.tensor_tensor(yn[0:m, n % 3, 0:k, :], yb[n % 3][0:m, 0:k * CH].rearrange("p (j n) -> p j n", j=k),
                                    rstd[0:m, n % 3, 0:k].unsqueeze(2).broadcast_to([m, k, CH]),
                                    ALU.mult).then_inc(s["tail_norm"], 1)

        pending = None
        for kind, n in tail_schedule:
            if kind == "conv":
                l, c, sizes = tail[n]
                v.wait_ge(s["tail_y"], n + 1)
                stats(yb[n % 3], n % 3, sizes, s["tail_var"], base)
                base += len(sizes) + 3
                if pending is not None:
                    tail_norm(pending)
                pending = n
            elif kind == "turn" and pending == n:
                tail_norm(n)
                pending = None

    return dict(sync=sync_prog, pool=pool_prog, act=act_prog, pe=pe_prog, dve=dve_prog,
                tail=len(tail), s=s, gb=gb)


def conv_inputs(x, inputs):
    pad = np.zeros((BATCH, (SLOTS0 + 1) * STRIDE0), x.dtype)
    pad[:, :x.shape[1]] = x
    blocks = pad.reshape(BATCH, SLOTS0 + 1, STRIDE0)
    stream = np.concatenate([blocks[:, :-1], blocks[:, 1:]], axis=2).reshape(STREAM0, TAPS0)
    stream = np.concatenate([np.zeros((1, TAPS0), x.dtype), stream[:-1]])
    windows = stream.T.reshape(TAPS0, GROUPS, FOLD).transpose(1, 0, 2).reshape(WROWS, FOLD)
    w0 = inputs["L0_tok_conv_w0"][:, 0, :]
    pick = np.zeros((WROWS, 2 * P - GROUPS), np.float16)
    pick[np.arange(WROWS), P - GROUPS + np.arange(WROWS) // TAPS0] = 1
    return {
        "windows": windows,
        "w0rep": np.tile(w0, (1, GROUPS)),
        "w0rows": np.tile(w0.T, (2, 1)),
        "g0rows": np.broadcast_to(inputs["L0_tok_ln_g0"], (2 * TAPS0, CH)),
        "conv_w": np.concatenate([inputs[f"L0_tok_conv_w{l}"].transpose(1, 2, 0) for l in range(1, 7)], axis=1),
        "conv_gb": np.stack([np.stack([inputs[f"L0_tok_ln_g{l}"], inputs[f"L0_tok_ln_b{l}"]], -1)
                             for l in range(7)], axis=1),
        "blk": np.kron(np.eye(GROUPS), np.ones((TAPS0, TAPS0))).astype(np.float32),
        "pick": pick,
        "back": np.concatenate([pick[:, P - GROUPS - GROUPS * c:2 * P - GROUPS - GROUPS * c].T
                                for c in range(PIECES)], axis=1),
        "cen": (np.eye(P) - 1.0 / P).astype(np.float32),
        "ident_d": np.eye(P, dtype=np.float32),
    }


D = 192
HD = 96
NTOK = BATCH * 12
TT = NTOK // P
AT = 8
HEADS, DH = 12, 16
EXPERTS = 10
HID = 768
HT = HID // P
HALF = NTOK // 2
REST = D - P
SOFT_SCALE = DH ** -0.5
PI_HALF = float(np.float32(np.pi / 2))


def build_rest(nc, sb, banks, sem, t, act6, conv):
    sems = {}

    shared = {}

    def share(family, tags, signals):
        for name, n in signals.items():
            for k, tag in enumerate(tags):
                shared[tag + name] = (family + name, n * k)

    share("norm", ["f", "ln0", "ln1", "ln2", "ln3", "ln4"], {"_st": TT, "_var": 1, "_std": 1, "_ln": TT})
    share("turn", ["a0", "a1", "f0", "a2", "f1"], {"_T": 3, "_xT": 3})
    share("project", ["tok", "l0p", "l1p"], {"_mm": TT})
    share("att", ["l0", "l1"], {"_qk": 8, "_qkd": 8, "_v": AT, "_vd": AT, "_blk": 2 * AT, "_s": 4 * AT, "_pv": 2 * AT,
                         "_o": AT, "_oT": 4, "_aT": 4})
    for n, name in enumerate(("gate_t", "", "", "", "gate_sin", "gate_tanh")):
        shared[name] = ("gate_act", n)
    for n, name in enumerate(("gate_arg", "gate_int", "gate_int2")):
        shared[name] = ("gate_dve", n)
    for u in range(6):
        shared[f"dn2_in{u}"] = (f"d_in{u % 2}", 16 * (EXPERTS // 2 + u // 2))
        if u not in (2, 3):
            shared[f"up2_in{u}"] = (f"gu_in{u % 2}", 16 * (EXPERTS // 2 + u // 4))
    shared["x_lo2"] = ("x_lo", 1)

    def S(name):
        name = shared.get(name, (name, 0))[0]
        if name not in sems:
            sems[name] = sem("r_" + name)
        return sems[name]

    def upto(name, n):
        return S(name), shared.get(name, (name, 0))[1] + n

    ident = t["ident"]
    small = t["small_sb"]
    hm = small["headmask"]
    h = sb("h", [P, TT, D], F32)
    x_tok = sb("x_tok", [P, TT, 2 * P], F32)
    xT = sb("xT", [P, 2, NTOK], F32)
    xT_att = xT[0:HD, :, :]
    st = sb("r_st", [P, TT, 6], F32)
    mv = sb("r_mv", [P, TT, 2], F32)
    sdv = sb("r_sd", [P, TT], F32)
    eps = sb("r_eps", [P, 1], F32)
    one_row = sb("one_row", [1, P], F32)
    gu_raw = sb("gu_raw", [P, 2, 2, 2 * HID], F32)
    d_raw = sb("d_raw", [P, 2, HT, D], F32)
    gu_hi = sb("gu_hi", [P, 2, 2 * HID], F16)
    gu_lo = sb("gu_lo", [P, 2, 2 * HID], F16)
    gu_mix = sb("gu_mix", [P, 2, 2 * HID], F16)
    d_hi = sb("d_hi", [P, 2, HT, D], F16)
    d_lo = sb("d_lo", [P, 2, HT, D], F16)
    x_lo = sb("x_lo", [P, 2, NTOK], F16)
    x_hi = xT[:, :, :].bitcast(BF16).rearrange("p a (n two) -> p a n two", two=2)[:, :, :, 1]
    logit = sb("logit", [P, TT, 8], F32)
    score = sb("score", [P, TT, 8], F32)
    top8 = sb("top8", [P, TT, 8], F32)
    topi = sb("topi", [P, TT, 8], U32)
    topf = sb("topf", [P, TT, 8], F32)
    r1 = [sb(f"r1_{i}", [P, TT], F32) for i in range(3)]
    mk = [sb(f"mk{i}", [P, TT, 8], F32) for i in range(2)]
    cw = sb("cw", [P, EXPERTS, TT], F32)
    cwc = sb("cwc", [P, 2, TT], F32)
    attn_ctx = ExitStack()
    attn_sb = lambda n, sh, dt: attn_ctx.enter_context(nc.sbuf_tensor(n, sh, dt))
    x2_tok = attn_sb("x2_tok", [P, TT, D], F32)
    x2T = attn_sb("x2T", [HD, 2, NTOK], F32)
    xn_f = attn_sb("xn_f", [P, TT, CH], F32)
    nT = attn_sb("nT", [P, NTOK], F32)
    qk = attn_sb("qk", [HD, 4, NTOK], F32)
    qe = attn_sb("qe", [HD, 2, HALF], F32)
    qr = attn_sb("qr", [HD, 2, HALF], F32)
    hidT = attn_sb("hidT", [P, NTOK], F32)
    par = attn_sb("par", [HD, AT * HEADS * 5], F32)
    gv = [attn_sb(f"gv{i}", [HD, AT * HEADS], F32) for i in range(5)]
    tempc = attn_sb("tempc", [HD, 1], F32)
    vg = attn_sb("vg", [HD, AT, HEADS, DH + 1], F32)
    blkd = attn_sb("blkd", [HD, 2, 6, HD], F32)
    pr = attn_sb("pr", [HD, 2, 6, HD], F32)
    pt = attn_sb("pt", [HD, 2, 6, HD], F32)
    mxs = attn_sb("mxs", [HD, 2, 6], F32)
    oa = attn_sb("oa", [HD, AT, HEADS, DH], F32)
    osq = attn_sb("osq", [HD, AT, HEADS, DH], F32)
    rden = attn_sb("rden", [HD, AT * HEADS], F32)
    omean = attn_sb("omean", [HD, AT * HEADS], F32)
    ovar = attn_sb("ovar", [HD, AT * HEADS], F32)
    attn_ctx.close()
    hid = sb("hid", [P, 2, HT, HALF], F32)
    hid_hi = hid[:, :, :, :].bitcast(BF16).rearrange("p a j (n two) -> p a j n two", two=2)[:, :, :, :, 1]
    hid_lo = sb("hid_lo", [P, 2, HT, HALF], F16)
    sg = sb("sg", [P, 2, HALF], F32)
    hc = sb("hc", [P, HT, 12, BATCH], F32)
    hc_hi = hc[:, :, :, :].bitcast(BF16).rearrange("p j s (n two) -> p j s n two", two=2)[:, :, :, :, 1]
    hc_lo = sb("hc_lo", [P, HT, 12, BATCH], F16)
    yT = sb("yT", [HD, 2, NTOK], F32)
    yd = sb("yd", [HD, 2, 2, 6, BATCH], F32)
    gl = sb("gl", [HD, 2, 6, BATCH], F32)
    gq = [sb(f"gq{i}", [HD, 6, BATCH], F32) for i in range(3)]
    outb = x_tok
    spare = hid[:, 1, :, :].rearrange("p j n -> p (j n)").bitcast(F16).rearrange("p (k j n) -> p k j n", k=4, j=HT)
    dn2_hi = [d_hi[:, 0], d_hi[:, 1], spare[:, 0], spare[:, 1], d_hi[:, 0], d_hi[:, 1]]
    dn2_lo = [d_lo[:, 0], d_lo[:, 1], spare[:, 2], spare[:, 3], d_lo[:, 0], d_lo[:, 1]]
    up2_at = [(u % 2, HID * (u // 2 % 2)) for u in range(6)]

    UP = [(0, (6, 1, 6), None), (1, (0, 1, 2), (0, 1, 2)), (2, (2, 1, 2), (2, 1, 2)), (3, (4, 1, 2), (4, 1, 2)),
          (4, (0, 2, 3), (6, 2, 3)), (5, (1, 2, 3), (7, 2, 3))]
    DOWN = [(0, None, None, None), (1, (6, 1, 2), 1, (0, 1, 2)), (2, (8, 1, 2), 1, (2, 1, 2)),
            (3, (10, 1, 2), 1, (4, 1, 2)), (4, (0, 2, 3), 0, (0, 2, 3)), (5, (1, 2, 3), 0, (1, 2, 3))]

    def rng(r):
        return slice(r[0], r[0] + r[1] * (r[2] - 1) + 1, r[1])

    def sync_prog(sp):
        def load(dst, src, sig):
            sp.dma_start(dst, src).then_inc(sig, 16)

        load(gu_raw[:, 0, :, :], t["gu"][0], S("gu_in0"))
        load(d_raw[:, 0, :, :], t["dn"][0], S("d_in0"))
        load(gu_raw[:, 1, :, :], t["gu"][1], S("gu_in1"))
        load(d_raw[:, 1, :, :], t["dn"][1], S("d_in1"))
        with sp.Fori(0, EXPERTS // 2 - 1) as i:
            for d in range(2):
                sp.wait_ge(*upto(f"gu_low{d}", 4 * i + 4))
                load(gu_raw[:, d, :, :], t["gu_flat"][bass.ds((2 * i + (2 + d)) * P, P), :], S(f"gu_in{d}"))
                sp.wait_ge(*upto(f"d_low{d}", 2 * i + 2))
                load(d_raw[:, d, :, :], t["dn_flat"][bass.ds((2 * i + (2 + d)) * P, P), :], S(f"d_in{d}"))

        def load_up2(u):
            d, c = up2_at[u]
            load(gu_raw[:, d, :, c:c + HID], t["up2"][u], S(f"up2_in{u}"))

        for d in range(2):
            sp.wait_ge(*upto(f"gu_low{d}", 4 * (EXPERTS // 2)))
            load_up2(d)
            load_up2(d + 2)
            sp.wait_ge(*upto(f"d_low{d}", 2 * (EXPERTS // 2)))
            load(d_raw[:, d, :, :], t["dn2"][d], S(f"dn2_in{d}"))
        for u in range(2, 6):
            if u >= 4:
                sp.wait_ge(*upto("up2_wlow", 2 * (u - 3)))
                load_up2(u)
            sp.wait_ge(*upto("dn2_wlow", u - 1))
            load(d_raw[:, u % 2, :, :], t["dn2"][u], S(f"dn2_in{u}"))
        sp.wait_ge(*upto("out_ready", TT))
        sp.dma_start(t["out"], outb[:, :, 0:D]).then_inc(S("out_done"), 16)
        sp.wait_ge(*upto("out_done", 16))

    def pe_prog(pe):
        def mm(out, a, b, start=True, stop=True):
            return nc.tensor.matmul(out, a, b, start=start, stop=stop)

        def to_channels(tag, src, wait):
            for j in range(12):
                hf, tt = j // 6, j % 6
                pe.wait_ge(*upto(wait, tt + 1))
                last = nc.tensor.transpose(banks[j // 4][0:HD, (j % 4) * P:(j % 4 + 1) * P],
                                           src[:, tt, hf * HD:(hf + 1) * HD], ident[:, :])
                if j % 4 == 3:
                    last.then_inc(S(tag + "_T"), 1)

        def to_channels_packed(tag, src, wait):
            for j in range(12):
                k, tt = j // 6, j % 6
                pe.wait_ge(*upto(wait, tt + 1))
                last = nc.tensor.transpose(banks[j // 4][:, (j % 4) * P:(j % 4 + 1) * P],
                                           src[:, tt, k * P:(k + 1) * P], ident[:, :])
                if j % 4 == 3:
                    last.then_inc(S(tag + "_T"), 1)

        def split_products(hi, lo, mix, x):
            xh, xl = x(x_hi), x(x_lo[:, :, :])
            return ((hi, xh[:, 0]), (hi, xl[:, 0]), (lo, xh[:, 0]), (mix, xh[:, 1]), (mix[0:REST], xl[0:REST, 1]))

        def proj192(tag, lhs, rhs, bias, waits=None):
            for tt in range(TT):
                out = banks[4 + tt // 2][:, (tt % 2) * D:(tt % 2 + 1) * D]
                parts = lhs(tt)
                for i, (a, b) in enumerate(zip(parts, rhs)):
                    mm(out, a, b, start=(i == 0), stop=False)
                mm(out, one_row[:, :], bias, start=False).then_inc(S(tag + "_mm"), 1)

        pe.wait_ge(conv["s"]["tail_act"], conv["tail"])
        pe.wait_ge(t["small_in"], 16 * len(t["small"]))
        pe.wait_ge(*upto("const_set", 2))
        for tt in range(TT):
            nc.tensor.transpose(banks[tt // 4][:, (tt % 4) * P:(tt % 4 + 1) * P], act6[:, tt * P:(tt + 1) * P],
                                ident[:, :]).then_inc(S("f_T"), 1)
        for tt in range(TT):
            pe.wait_ge(*upto("f_ln", tt + 1))
            nc.tensor.transpose(banks[2 + tt // 4][:, (tt % 4) * P:(tt % 4 + 1) * P], xn_f[:, tt, :],
                                ident[:, :]).then_inc(S("f_T2"), 1)
        pe.wait_ge(*upto("f_nT", 2))
        proj192("tok", lambda tt: [nT[:, tt * P:(tt + 1) * P]], [small["proj_w"][:, :]], small["proj_b"][:, :])

        to_channels("a0", x_tok, "ln0_ln")
        pe.wait_ge(*upto("a0_xT", 3))
        to_channels("a1", x2_tok, "ln1_ln")
        for hf in range(2):
            for kt in range(2):
                last = mm(banks[3 + hf][:, 0:HALF], small["Wb1"][:, kt, :], xT_att[:, kt, hf * HALF:(hf + 1) * HALF],
                          kt == 0, kt == 1)
            last.then_inc(S("hid_mm"), 1)
        pe.wait_ge(*upto("hid_act", 2))
        for a in range(AT):
            last = mm(banks[5][0:HD, a * 60:(a + 1) * 60], hidT[:, a * HD:(a + 1) * HD], small["Wb2"][:, :])
        last.then_inc(S("par_mm"), 1)
        pe.wait_ge(*upto("a1_xT", 3))

        def qkv(tag, w, src, first_free):
            for m in range(4):
                for hf in range(2):
                    n = 2 * m + hf
                    if n >= 2:
                        pe.wait_ge(*upto(tag + "_qkd", n - 1))
                    for kt in range(2):
                        last = mm(banks[n % 2][0:HD, 0:HALF], w[:, kt, m * HD:(m + 1) * HD],
                                  src[:, kt, hf * HALF:(hf + 1) * HALF], kt == 0, kt == 1)
                    last.then_inc(S(tag + "_qk"), 1)

        def vrows(tag, w, bias, src):
            for a in range(AT):
                if a >= 4:
                    pe.wait_ge(*upto(tag + "_vd", a - 3))
                out = banks[2 + a % 4][0:HD, 0:D]
                for kt in range(2):
                    mm(out, src[:, kt, a * HD:(a + 1) * HD], w[:, kt, 2 * D:3 * D], kt == 0, False)
                mm(out, one_row[:, 0:HD], bias[:, 2 * D:3 * D], False).then_inc(S(tag + "_v"), 1)

        qkv("l0", small["Wqkv"], x2T, None)
        pe.wait_ge(*upto("gates", 1))
        vrows("l0", small["Wqkv"], small["bqkv_row"], x2T)
        pe.wait_ge(*upto("l0_vd", AT))
        for n in range(2 * AT + 1):
            if n < 2 * AT:
                a, hf = n // 2, n % 2
                pe.wait_ge(*upto("l0_blk", n + 1))
                if n >= 2:
                    pe.wait_ge(*upto("l0_p", 2 * (n - 1)))
                for g in range(2):
                    mm(banks[2 * (n % 2) + g][0:HD, 0:3 * HD], qk[:, 2 + hf, a * HD:(a + 1) * HD],
                       blkd[:, n % 2, 3 * g:3 * g + 3, :]).then_inc(S("l0_s"), 1)
            if n >= 1:
                m = n - 1
                a, hf = m // 2, m % 2
                pe.wait_ge(*upto("l0_p", 2 * (m + 1)))
                if a >= 2 and hf == 0:
                    pe.wait_ge(*upto("l0_o", a - 1))
                for hd in range(6):
                    c = (hf * 6 + hd) * (DH + 1)
                    last = mm(banks[4 + a % 2][0:HD, c:c + DH + 1], pr[:, m % 2, hd, :], vg[:, a, hf * 6 + hd, :])
                last.then_inc(S("l0_pv"), 1)

        def back(tag):
            for hf in range(2):
                for a in range(AT):
                    last = nc.tensor.transpose(banks[2 * hf + a // 4][0:HD, (a % 4) * HD:(a % 4 + 1) * HD],
                                               oa[:, a, 6 * hf:6 * hf + 6, :], ident[0:HD, 0:HD])
                    if a % 4 == 3:
                        last.then_inc(S(tag), 1)

        pe.wait_ge(*upto("l0_oln", 1))
        back("l0_oT")
        pe.wait_ge(*upto("l0_aT", 4))
        proj192("l0p", lambda tt: [xT_att[:, kt, tt * P:(tt + 1) * P] for kt in range(2)],
                [small["Wproj"][:, kt, :] for kt in range(2)], small["bproj_row"][:, :])

        to_channels_packed("f0", x_tok, "ln2_ln")
        pe.wait_ge(*upto("f0_xT", 3))
        for tt in range(TT):
            for kt, rows in ((0, P), (1, REST)):
                last = mm(banks[3][:, tt * 8:tt * 8 + 8], xT[0:rows, kt, tt * P:(tt + 1) * P],
                          small["gate_w"][0:rows, kt, :], kt == 0, kt == 1)
        last.then_inc(S("route"), 1)
        pe.wait_ge(*upto("x_lo", 1))
        pe.wait_ge(*upto("route_read", 1))

        def gate_up_unit(i, d, hb, first):
            for j in range(HT):
                cnt = 24 * i + (12 * d + 6 * hb + j)
                if not (first and cnt_is_small(d, hb, j)):
                    pe.wait_ge(*upto("hid_w", cnt - 1))
                for g in range(2):
                    m0 = g * HID + j * P
                    parts = split_products(*[w[:, d, m0:m0 + P] for w in (gu_hi, gu_lo, gu_mix)],
                                           lambda x: x[:, :, hb * HALF:(hb + 1) * HALF])
                    for n, (w, x) in enumerate(parts):
                        last = mm(banks[2 * (j % 2) + g][:, 0:HALF], w, x, n == 0, n == 4)
                    last.then_inc(S("gu_mm"), 1)

        def cnt_is_small(d, hb, j):
            return 12 * d + 6 * hb + j < 2

        def down_unit(i, d, hb, first):
            unit = 4 * i + (2 * d + hb)
            pe.wait_ge(*upto("hid_low", 6 * unit + 6))
            if not (first and 2 * d + hb < 2):
                pe.wait_ge(*upto("added", unit * 3 - 3))
            for tt in range(3):
                out = banks[4 + 2 * hb + tt // 2][:, (tt % 2) * D:(tt % 2 + 1) * D]
                n = 0
                for j in range(HT):
                    hs = hid_hi[:, hb, j, tt * P:(tt + 1) * P]
                    hl = hid_lo[:, hb, j, tt * P:(tt + 1) * P]
                    for w, x in ((d_hi, hs), (d_hi, hl), (d_lo, hs)):
                        last = mm(out, x, w[:, d, j, :], n == 0, n == 3 * HT - 1)
                        n += 1
                last.then_inc(S("down"), 1)

        def moe_iter(i, first):
            for d in range(2):
                pe.wait_ge(*upto(f"gu_low{d}", 4 * i + 4))
                gate_up_unit(i, d, 0, first)
                if d == 1:
                    down_unit(i, 0, 1, first)
                elif not first:
                    down_unit(i - 1, 1, 1, False)
                gate_up_unit(i, d, 1, first)
                pe.wait_ge(*upto(f"d_low{d}", 2 * i + 2))
                down_unit(i, d, 0, first)

        moe_iter(0, True)
        with pe.Fori(1, EXPERTS // 2) as i:
            moe_iter(i, False)
        down_unit(EXPERTS // 2 - 1, 1, 1, False)

        pe.wait_ge(*upto("hid_w", HT * 2 * EXPERTS))
        to_channels("a2", x_tok, "ln3_ln")
        pe.wait_ge(*upto("a2_xT", 3))
        qkv("l1", small["w_qkv"], xT_att, None)
        pe.wait_ge(*upto("l1_qkd", 8))
        vrows("l1", small["w_qkv"], small["b_qkv_row"], xT_att)
        pe.wait_ge(*upto("l1_vd", AT))
        for n in range(2 * AT + 2):
            if n < 2 * AT:
                a, hf = n // 2, n % 2
                pe.wait_ge(*upto("l1_blk", n + 1))
                if n >= 2:
                    pe.wait_ge(*upto("l1_sm", 2 * (n - 1)))
                for g in range(2):
                    mm(banks[2 * (n % 2) + g][0:HD, 0:3 * HD], qk[:, hf, a * HD:(a + 1) * HD],
                       blkd[:, n % 2, 3 * g:3 * g + 3, :]).then_inc(S("l1_s"), 1)
            if 1 <= n <= 2 * AT:
                m = n - 1
                pe.wait_ge(*upto("l1_exp", m + 1))
                for g in range(2):
                    if m >= 1:
                        pe.wait_ge(*upto("l1_pt", 2 * (m - 1) + g + 1))
                    for k in range(3):
                        last = nc.tensor.transpose(banks[6 + g][0:HD, k * HD:(k + 1) * HD], pr[:, m % 2, 3 * g + k, :],
                                                   ident[0:HD, 0:HD])
                    last.then_inc(S("l1_pT"), 1)
            if n >= 2:
                m = n - 2
                a, hf = m // 2, m % 2
                pe.wait_ge(*upto("l1_pt", 2 * (m + 1)))
                if a >= 2 and hf == 0:
                    pe.wait_ge(*upto("l1_o", a - 1))
                for hd in range(6):
                    c = (hf * 6 + hd) * (DH + 1)
                    last = mm(banks[4 + a % 2][0:HD, c:c + DH + 1], pt[:, m % 2, hd, :], vg[:, a, hf * 6 + hd, :])
                last.then_inc(S("l1_pv"), 1)
        pe.wait_ge(*upto("l1_o", AT))
        back("l1_oT")
        pe.wait_ge(*upto("l1_aT", 4))
        proj192("l1p", lambda tt: [xT_att[:, kt, tt * P:(tt + 1) * P] for kt in range(2)],
                [small["w_proj"][:, kt, :] for kt in range(2)], small["b_proj_row"][:, :])

        to_channels_packed("f1", x_tok, "ln4_ln")
        pe.wait_ge(*upto("f1_xT", 3))
        xc = xT[:, :, :].rearrange("p k (b r) -> p k r b", r=12)
        for k in range(2):
            for i in range(6):
                for kt, rows in ((0, P), (1, REST)):
                    last = mm(banks[3 + k][0:HD, i * BATCH:(i + 1) * BATCH], small["G_W"][0:rows, kt, i, k, :],
                              xc[0:rows, kt, i, :], kt == 0, kt == 1)
            last.then_inc(S("glog"), 1)
        pe.wait_ge(*upto("x_lo2", 1))
        for u, cols, slots in UP:
            d, c = up2_at[u]
            size = cols[2] * BATCH
            pe.wait_ge(*upto("up2_wlow", 2 * u + 2))
            for j in range(HT):
                cnt = 6 * u + j
                if cnt >= 2:
                    pe.wait_ge(*upto("up2_act", cnt - 1))
                m0 = c + j * P
                parts = split_products(*[w[:, d, m0:m0 + P] for w in (gu_hi, gu_lo, gu_mix)],
                                       lambda x: x.rearrange("p k (b r) -> p k r b", r=12)[:, :, rng(cols), :])
                for n, (w, x) in enumerate(parts):
                    last = mm(banks[cnt % 2][:, 0:size], w, x, n == 0, n == 4)
                last.then_inc(S("up2_mm"), 1)
        pe.wait_ge(*upto("glog_read", 2))
        for u, slots, direction, classes in DOWN:
            pe.wait_ge(*upto("dn2_wlow", u + 1))
            if u == 0:
                pe.wait_ge(*upto("up2_low", 6 * len(UP)))
            size = HALF if slots is None else slots[2] * BATCH
            for m in range(2):
                cnt = 2 * u + m
                if cnt >= 2:
                    pe.wait_ge(*upto("dn2_read", cnt - 1))
                n = 0
                for j in range(HT):
                    if slots is None:
                        a, b = hid_hi[:, 0, j, :], hid_lo[:, 0, j, :]
                    else:
                        a, b = hc_hi[:, j, rng(slots), :], hc_lo[:, j, rng(slots), :]
                    for w, x in ((dn2_hi[u], a), (dn2_hi[u], b), (dn2_lo[u], a)):
                        last = mm(banks[2 + cnt % 2][0:HD, 0:size], w[:, j, m * HD:(m + 1) * HD], x, n == 0,
                                  n == 3 * HT - 1)
                        n += 1
                last.then_inc(S("dn2_mm"), 1)
        pe.wait_ge(*upto("yT", 1))
        for tt in range(TT):
            for kt in range(2):
                last = nc.tensor.transpose(banks[4 + tt // 2][:, (tt % 2) * D + kt * HD:(tt % 2) * D + (kt + 1) * HD],
                                           yT[:, kt, tt * P:(tt + 1) * P], ident[0:HD, 0:HD])
            last.then_inc(S("y_tok"), 1)

    def act_prog(a):
        act = nc.scalar.activation

        def std(tag):
            a.wait_ge(*upto(tag + "_var", 1))
            act(sdv[:, :], mv[:, :, 1], ACT.Sqrt, bias=eps[:, :]).then_inc(S(tag + "_std"), 1)

        def evac_T(tag, dst):
            flat = dst.rearrange("p k n -> p (k n)")
            rows = dst.shape[0]
            for c in range(3):
                a.wait_ge(*upto(tag + "_T", c + 1))
                act(flat[:, c * 512:(c + 1) * 512], banks[c][0:rows, :], ACT.Copy).then_inc(S(tag + "_xT"), 1)

        def high_and_scaled(high, raw):
            act(high, raw, ACT.Copy, scale=WS)
            return act(raw, raw, ACT.Copy, scale=WS)

        def high_part(d, c, k):
            return high_and_scaled((gu_mix if k else gu_hi)[:, d, c:c + HID], gu_raw[:, d, k, c:c + HID])

        std("f")
        std("ln0")
        evac_T("a0", xT_att)
        std("ln1")
        for hf in range(2):
            a.wait_ge(*upto("hid_mm", hf + 1))
            act(hidT[:, hf * HALF:(hf + 1) * HALF], banks[3 + hf][:, 0:HALF], ACT.Silu).then_inc(S("hid_act"), 1)
        a.wait_ge(*upto("par_sb", 1))
        pv = par[:, :].rearrange("p (n f) -> p n f", f=5)
        act(gv[0][:, :], pv[:, :, 0], ACT.Tanh, scale=0.5).then_inc(S("gate_t"), 1)
        act(gv[1][:, :], pv[:, :, 1], ACT.Tanh).then_inc(S("gate_t"), 1)
        act(gv[2][:, :], pv[:, :, 2], ACT.Tanh, scale=0.5).then_inc(S("gate_t"), 1)
        act(gv[3][:, :], pv[:, :, 3], ACT.Tanh).then_inc(S("gate_t"), 1)
        a.wait_ge(*upto("gate_arg", 1))
        act(gv[1][:, :], gv[1][:, :], ACT.Sin).then_inc(S("gate_sin"), 1)
        a.wait_ge(*upto("gate_int", 1))
        act(gv[0][:, :], gv[0][:, :], ACT.Tanh).then_inc(S("gate_tanh"), 1)
        a.wait_ge(*upto("gate_int2", 1))
        act(gv[0][:, :], gv[0][:, :], ACT.Tanh, scale=0.5).then_inc(S("gate_tanh"), 1)
        for n in range(8):
            a.wait_ge(*upto("l0_qmin", n + 1))
            act(qe[:, n % 2, :], qe[:, n % 2, :], ACT.Exp).then_inc(S("l0_qexp"), 1)
        a.wait_ge(*upto("ovar", 1))
        act(ovar[:, :], ovar[:, :], ACT.Sqrt, bias=eps[0:HD, :], scale=1.0 / DH).then_inc(S("ostd"), 1)
        a.wait_ge(*upto("gu_in0", 16))
        for k in range(4):
            high_part(0, k % 2 * HID, k // 2).then_inc(S("gu_high0"), 1)
        a.wait_ge(*upto("d_in0", 16))
        for k in range(2):
            high_and_scaled(d_hi[:, 0, 3 * k:3 * k + 3, :],
                            d_raw[:, 0, 3 * k:3 * k + 3, :]).then_inc(S("d_high0"), 1)
        std("ln2")
        evac_T("f0", xT[:, :, :])
        a.wait_ge(*upto("logit", 1))
        act(score[:, :, :], logit[:, :, :], ACT.Exp).then_inc(S("score_exp"), 1)

        def unit(i, d, hb, splits):
            for j in range(HT):
                cnt = 24 * i + (12 * d + 6 * hb + j)
                a.wait_ge(*upto("gu_mm", 2 * cnt + 1))
                if not (type(i) is int and cnt < 2):
                    a.wait_ge(*upto("hid_w", cnt - 1))
                act(sg[:, j % 2, :], banks[2 * (j % 2)][:, 0:HALF], ACT.Silu, scale=1.0 / WS).then_inc(S("silu"), 1)
                if j in splits:
                    splits[j]()

        def expert(i, d, nxt):
            unit(i, d, 0, {1 + k: (lambda k=k: nxt("gu", k)) for k in range(4)} if nxt else {})
            unit(i, d, 1, {1 + 2 * k: (lambda k=k: nxt("d", k)) for k in range(2)} if nxt else {})

        def next_expert(i, d):
            def part(kind, k):
                if k == 0:
                    a.wait_ge(*upto(f"{kind}_in{d}", 16 * i + 16))
                if kind == "gu":
                    high_part(d, k % 2 * HID, k // 2).then_inc(S(f"gu_high{d}"), 1)
                else:
                    if k == 0 and not (type(i) is int and i == 0):
                        a.wait_ge(*upto("down", 12 * i + (6 * d - 6)))
                    high_and_scaled(d_hi[:, d, 3 * k:3 * k + 3, :],
                                    d_raw[:, d, 3 * k:3 * k + 3, :]).then_inc(S(f"d_high{d}"), 1)
            return part

        def up2_unit0(kind, k):
            if kind == "gu" and k < 2:
                if k == 0:
                    a.wait_ge(*upto("up2_in0", 16))
                up2_high(0, k)
            elif kind == "d" and k == 0:
                a.wait_ge(*upto("down", 6 * EXPERTS - 6))
                dn2_high(0)

        def up2_high(u, k):
            d, c = up2_at[u]
            high_part(d, c, k).then_inc(S("up2_whigh"), 1)

        def dn2_high(u):
            a.wait_ge(*upto(f"dn2_in{u}", 16))
            high_and_scaled(dn2_hi[u], d_raw[:, u % 2, :, :]).then_inc(S("dn2_whigh"), 1)

        last_pair = EXPERTS // 2 - 1
        expert(0, 0, next_expert(0, 1))
        expert(0, 1, next_expert(1, 0))
        with a.Fori(1, last_pair) as i:
            expert(i, 0, next_expert(i, 1))
            expert(i, 1, next_expert(i + 1, 0))
        expert(last_pair, 0, next_expert(last_pair, 1))
        expert(last_pair, 1, up2_unit0)

        std("ln3")
        evac_T("a2", xT_att)
        for u in (1, 2, 3):
            a.wait_ge(*upto(f"up2_in{u}", 16))
            for k in range(2):
                up2_high(u, k)
            if u == 1:
                a.wait_ge(*upto("down", 6 * EXPERTS))
                dn2_high(1)
        for n in range(2 * AT):
            a.wait_ge(*upto("l1_sub", n + 1))
            if n >= 2:
                a.wait_ge(*upto("l1_pT", 2 * (n - 1)))
            act(pr[:, n % 2, :, :], pr[:, n % 2, :, :], ACT.Exp, scale=SOFT_SCALE).then_inc(S("l1_exp"), 1)
            for g in range(2):
                a.wait_ge(*upto("l1_pT", 2 * n + g + 1))
                if n >= 2:
                    a.wait_ge(*upto("l1_pv", n - 1))
                act(pt[:, n % 2, 3 * g:3 * g + 3, :], banks[6 + g][0:HD, 0:3 * HD].rearrange("p (k n) -> p k n", k=3),
                    ACT.Copy).then_inc(S("l1_pt"), 1)
        std("ln4")
        evac_T("f1", xT[:, :, :])
        for u in (2, 3):
            dn2_high(u)
        for u, cols, slots in UP:
            size = cols[2] * BATCH
            if u == 1:
                a.wait_ge(*upto("gsub", 1))
                act(gl[:, :, :, :], gl[:, :, :, :], ACT.Exp).then_inc(S("gexp"), 1)
            for j in range(HT):
                cnt = 6 * u + j
                a.wait_ge(*upto("up2_mm", cnt + 1))
                src = banks[cnt % 2][:, 0:size].rearrange("p (r b) -> p r b", b=BATCH)
                dst = (hid[:, 0, j, :].rearrange("p (r b) -> p r b", b=BATCH) if slots is None
                       else hc[:, j, rng(slots), :])
                act(dst, src, ACT.Gelu, bias=small["b1"][:, u, j:j + 1], scale=1.0 / WS).then_inc(S("up2_act"), 1)
            if u < 2:
                a.wait_ge(*upto(f"up2_in{u + 4}", 16))
                for k in range(2):
                    up2_high(u + 4, k)
        for u in (4, 5):
            a.wait_ge(*upto("dn2_mm", 2 * (u - 3)))
            dn2_high(u)

    def pool_prog(pool):
        def less_high(dst, raw, high):
            return nc.gpsimd.tensor_tensor(dst, raw, high, ALU.subtract)

        def low_part(d, c, k):
            if k == 0:
                return less_high(gu_lo[:, d, c:c + HID], gu_raw[:, d, 0, c:c + HID], gu_hi[:, d, c:c + HID])
            return less_high(gu_mix[REST:P, d, c:c + HID], gu_raw[REST:P, d, 1, c:c + HID],
                             gu_mix[REST:P, d, c:c + HID])

        def expert(i, d):
            for k in range(4):
                pool.wait_ge(*upto(f"gu_high{d}", 4 * i + (k + 1)))
                if k == 2:
                    pool.wait_ge(*upto(f"gu_low{d}", 4 * i + 2))
                low_part(d, k % 2 * HID, k // 2).then_inc(S(f"gu_low{d}"), 1)
            pool.wait_ge(*upto(f"gu_low{d}", 4 * i + 4))
            for k in range(2):
                pool.wait_ge(*upto(f"d_high{d}", 2 * i + (k + 1)))
                less_high(d_lo[:, d, 3 * k:3 * k + 3, :], d_raw[:, d, 3 * k:3 * k + 3, :],
                          d_hi[:, d, 3 * k:3 * k + 3, :]).then_inc(S(f"d_low{d}"), 1)

        def up2(u):
            for k in range(2):
                pool.wait_ge(*upto("up2_whigh", 2 * u + k + 1))
                if 2 * u + k > 0:
                    pool.wait_ge(*upto("up2_wlow", 2 * u + k))
                low_part(*up2_at[u], k).then_inc(S("up2_wlow"), 1)

        def dn2(u, ups):
            pool.wait_ge(*upto("dn2_whigh", u + 1))
            pool.wait_ge(*upto("up2_wlow", 2 * ups))
            less_high(dn2_lo[u], d_raw[:, u % 2, :, :], dn2_hi[u]).then_inc(S("dn2_wlow"), 1)

        with pool.Fori(0, EXPERTS // 2) as i:
            for d in range(2):
                expert(i, d)
        up2(0)
        dn2(0, 1)
        up2(1)
        dn2(1, 2)
        up2(2)
        up2(3)
        dn2(2, 4)
        dn2(3, 4)
        up2(4)
        up2(5)
        dn2(4, 6)
        dn2(5, 6)

    def dve_prog(v):
        chain = [0]

        def link(ins):
            chain[0] += 1
            ins.then_inc(S("dve_chain"), 1)
            v.wait_ge(*upto("dve_chain", chain[0]))

        tt_ = nc.vector.tensor_tensor
        ts_ = nc.vector.tensor_scalar
        stt = nc.vector.scalar_tensor_tensor

        def layer_norm(tag, src, dst, packed=False):
            for i in range(TT):
                nc.vector.bn_stats(st[:, i, :], src(i)).then_inc(S(tag + "_st"), 1)
            v.wait_ge(*upto(tag + "_st", TT))
            for i in range(TT):
                ins = nc.vector.bn_aggr(mv[:, i, :], st[:, i, :])
                if i == TT - 1:
                    ins.then_inc(S(tag + "_var"), 1)
            v.wait_ge(*upto(tag + "_std", 1))
            link(nc.vector.reciprocal(sdv[:, :], sdv[:, :]))
            for i in range(TT):
                if packed:
                    ts_(x_tok[:, i, D:2 * P], src(i)[:, P:D], mv[:, i, 0:1], sdv[:, i:i + 1], ALU.subtract, ALU.mult)
                ts_(dst(i), src(i), mv[:, i, 0:1], sdv[:, i:i + 1], ALU.subtract, ALU.mult).then_inc(S(tag + "_ln"), 1)

        def add_h(tag, first=False):
            for i in range(TT):
                v.wait_ge(*upto(tag + "_mm", i // 2 * 2 + 2))
                src = banks[4 + i // 2][:, (i % 2) * D:(i % 2 + 1) * D]
                if first:
                    link(nc.vector.tensor_copy(h[:, i, :], src))
                else:
                    link(tt_(h[:, i, :], src, h[:, i, :], ALU.add))

        nc.vector.memset(eps[:, :], EPS).then_inc(S("const_set"), 1)
        nc.vector.memset(one_row[:, :], 1.0).then_inc(S("const_set"), 1)
        v.wait_ge(t["small_in"], 16 * len(t["small"]))
        v.wait_ge(*upto("f_T", TT))
        layer_norm("f", lambda i: banks[i // 4][:, (i % 4) * P:(i % 4 + 1) * P], lambda i: xn_f[:, i, :])
        for c, (lo, hi) in enumerate(((0, 4), (4, 6))):
            v.wait_ge(*upto("f_T2", hi))
            ts_(nT[:, lo * P:hi * P], banks[2 + c][:, 0:(hi - lo) * P], small["fln"][:, 0:1], small["fln"][:, 1:2],
                ALU.mult, ALU.add).then_inc(S("f_nT"), 1)
        add_h("tok", True)
        layer_norm("ln0", lambda i: h[:, i, :], lambda i: x_tok[:, i, 0:D])
        v.wait_ge(*upto("ln0_ln", TT))
        layer_norm("ln1", lambda i: x_tok[:, i, 0:D], lambda i: x2_tok[:, i, :])
        flat = x2T[:, :, :].rearrange("p k n -> p (k n)")
        for c in range(3):
            v.wait_ge(*upto("a1_T", c + 1))
            for lo, hi in ((c * 512, min((c + 1) * 512, NTOK)), (max(c * 512, NTOK), (c + 1) * 512)):
                if lo >= hi:
                    continue
                kt = lo // NTOK
                ins = ts_(flat[:, lo:hi], banks[c][0:HD, lo - c * 512:hi - c * 512], small["ln_wb"][:, 0, kt:kt + 1],
                          small["ln_wb"][:, 1, kt:kt + 1], ALU.mult, ALU.add)
                if hi == (c + 1) * 512:
                    ins.then_inc(S("a1_xT"), 1)
        v.wait_ge(*upto("par_mm", 1))
        nc.vector.tensor_copy(par[:, :], banks[5][0:HD, 0:AT * 60]).then_inc(S("par_sb"), 1)
        link(ts_(tempc[:, :], small["temp"][0:HD, :], 0.1, 2.0, ALU.max, ALU.min))
        v.wait_ge(*upto("gate_t", 4))
        link(tt_(gv[1][:, :], gv[1][:, :], gv[3][:, :], ALU.subtract))
        link(ts_(gv[1][:, :], gv[1][:, :], PI_HALF, 3.1415925, ALU.mult, ALU.min))
        ts_(gv[1][:, :], gv[1][:, :], -3.1415925, None, ALU.max).then_inc(S("gate_arg"), 1)
        link(ts_(gv[0][:, :], gv[0][:, :], 0.5, 0.5, ALU.mult, ALU.add))
        link(ts_(gv[2][:, :], gv[2][:, :], 0.5, 0.5, ALU.mult, ALU.add))
        link(tt_(gv[0][:, :], gv[0][:, :], gv[2][:, :], ALU.mult))
        v.wait_ge(*upto("gate_sin", 1))
        link(tt_(gv[1][:, :], gv[1][:, :], gv[1][:, :], ALU.mult))
        link(ts_(gv[1][:, :], gv[1][:, :], -2.0, 1.0, ALU.mult, ALU.add))
        tt_(gv[0][:, :], gv[0][:, :], gv[1][:, :], ALU.mult).then_inc(S("gate_int"), 1)
        v.wait_ge(*upto("gate_tanh", 1))
        ts_(gv[0][:, :], gv[0][:, :], tempc[:, :], None, ALU.mult).then_inc(S("gate_int2"), 1)
        v.wait_ge(*upto("gate_tanh", 2))
        ts_(gv[4][:, :], gv[0][:, :], 0.5, 1.5, ALU.mult, ALU.add).then_inc(S("gates"), 1)
        nc.vector.memset(vg[:, :, :, DH:DH + 1], 1.0).then_inc(S("vones"), 1)
        for n in range(8):
            m, hf = n // 2, n % 2
            v.wait_ge(*upto("l0_qk", n + 1))
            src = banks[n % 2][0:HD, 0:HALF]
            b = small["bqkv"][:, m:m + 1]
            ts_(qe[:, n % 2, :], src, b, 0.0, ALU.add, ALU.min).then_inc(S("l0_qmin"), 1)
            ts_(qr[:, n % 2, :], src, b, 0.0, ALU.add, ALU.max).then_inc(S("l0_qkd"), 1)
            v.wait_ge(*upto("l0_qexp", n + 1))
            v.wait_ge(*upto("l0_qkd", n + 1))
            tt_(qk[:, m, hf * HALF:(hf + 1) * HALF], qe[:, n % 2, :], qr[:, n % 2, :], ALU.add).then_inc(S("l0_qf"), 1)
        v.wait_ge(*upto("gates", 1))
        gate1 = gv[4][:, :].rearrange("p (a n) -> p a n", a=AT)
        for a in range(AT):
            v.wait_ge(*upto("l0_v", a + 1))
            tt_(vg[:, a, :, 0:DH], banks[2 + a % 4][0:HD, 0:D].rearrange("p (n e) -> p n e", n=HEADS),
                gate1[:, a, :].unsqueeze(2).broadcast_to([HD, HEADS, DH]), ALU.mult).then_inc(S("l0_vd"), 1)

        def spread(n, row, tag, used):
            a, hf = n // 2, n % 2
            if n >= 2:
                v.wait_ge(*upto(used, 2 * (n - 1)))
            tt_(blkd[:, n % 2, :, :], qk[:, row + hf, a * HD:(a + 1) * HD].unsqueeze(1).broadcast_to([HD, 6, HD]),
                hm[:, :].unsqueeze(2).broadcast_to([HD, 6, HD]), ALU.mult).then_inc(S(tag), 1)

        v.wait_ge(*upto("l0_qf", 8))
        v.wait_ge(*upto("vones", 1))
        spread(0, 0, "l0_blk", None)
        causal = small["causal"][:, :].unsqueeze(1).broadcast_to([HD, 3, HD])
        for n in range(2 * AT):
            if n + 1 < 2 * AT:
                spread(n + 1, 0, "l0_blk", "l0_s")
            for g in range(2):
                v.wait_ge(*upto("l0_s", 2 * n + g + 1))
                if n >= 2:
                    v.wait_ge(*upto("l0_pv", n - 1))
                tt_(pr[:, n % 2, 3 * g:3 * g + 3, :],
                    banks[2 * (n % 2) + g][0:HD, 0:3 * HD].rearrange("p (k n) -> p k n", k=3), causal,
                    ALU.mult).then_inc(S("l0_p"), 1)
            if n % 2 == 1 and n > 1:
                o_norm0(v, n // 2 - 1, link, tt_, ts_)
        o_norm0(v, AT - 1, link, tt_, ts_)
        o3 = oa[:, :, :, :].rearrange("p a n e -> p (a n) e")
        q3 = osq[:, :, :, :].rearrange("p a n e -> p (a n) e")
        n3 = AT * HEADS
        v.wait_ge(*upto("l0_o", AT))
        link(nc.vector.reduce_sum(omean[:, :], o3, AX))
        link(ts_(omean[:, :], omean[:, :], 1.0 / DH, None, ALU.mult))
        link(tt_(o3, o3, omean[:, :].unsqueeze(2).broadcast_to([HD, n3, DH]), ALU.subtract))
        link(tt_(q3, o3, o3, ALU.mult))
        nc.vector.reduce_sum(ovar[:, :], q3, AX).then_inc(S("ovar"), 1)
        v.wait_ge(*upto("ostd", 1))
        link(nc.vector.reciprocal(ovar[:, :], ovar[:, :]))
        tt_(o3, o3, ovar[:, :].unsqueeze(2).broadcast_to([HD, n3, DH]), ALU.mult).then_inc(S("l0_oln"), 1)
        for c in range(4):
            v.wait_ge(*upto("l0_oT", c + 1))
            ts_(xT_att[:, c // 2, (c % 2) * HALF:(c % 2 + 1) * HALF], banks[c][0:HD, 0:HALF], small["mn"][:, 0:1],
                small["mn"][:, 1:2], ALU.mult, ALU.add).then_inc(S("l0_aT"), 1)
        add_h("l0p")

        layer_norm("ln2", lambda i: h[:, i, :], lambda i: x_tok[:, i, 0:D], packed=True)
        v.wait_ge(*upto("f0_xT", 3))
        tt_(x_lo[:, :, :], xT[:, :, :], x_hi, ALU.subtract).then_inc(S("x_lo"), 1)
        v.wait_ge(*upto("route", 1))
        lg = banks[3][:, 0:TT * 8].rearrange("p (t e) -> p t e", e=8)
        bc = lambda x: x[:, :].unsqueeze(2).broadcast_to([P, TT, 8])
        link(nc.vector.tensor_reduce(r1[0][:, :], lg, AX, ALU.max))
        tt_(logit[:, :, :], lg, bc(r1[0]), ALU.subtract).then_inc(S("logit"), 1)
        v.wait_ge(*upto("logit", 1))
        v.wait_ge(*upto("score_exp", 1))
        nc.vector.reduce_sum(r1[0][:, :], score[:, :, :], AX).then_inc(S("route_read"), 1)
        v.wait_ge(*upto("route_read", 1))
        link(nc.vector.reciprocal(r1[0][:, :], r1[0][:, :]))
        link(tt_(score[:, :, :], score[:, :, :], bc(r1[0]), ALU.mult))
        for i in range(TT):
            link(nc.vector.max(top8[:, i, :], score[:, i, :]))
            link(nc.vector.max_index(topi[:, i, :], top8[:, i, :], score[:, i, :]))
        link(nc.vector.tensor_copy(topf[:, :, :], topi[:, :, :]))
        iota = small["iota8"][:, :].unsqueeze(1).broadcast_to([P, TT, 8])
        link(tt_(r1[1][:, :], top8[:, :, 0], top8[:, :, 1], ALU.add))
        link(ts_(r1[1][:, :], r1[1][:, :], 1e-8, None, ALU.add))
        link(nc.vector.reciprocal(r1[1][:, :], r1[1][:, :]))
        link(ts_(r1[1][:, :], r1[1][:, :], 1.0 / WS, None, ALU.mult))
        for k in range(2):
            link(nc.vector.tensor_copy(r1[2][:, :], topf[:, :, k]))
            link(tt_(mk[k][:, :, :], iota, bc(r1[2]), ALU.is_equal))
            link(tt_(r1[2][:, :], top8[:, :, k], r1[1][:, :], ALU.mult))
            link(tt_(mk[k][:, :, :], mk[k][:, :, :], bc(r1[2]), ALU.mult))
        link(tt_(cw[:, 0:8, :], mk[0][:, :, :].rearrange("p t e -> p e t"), mk[1][:, :, :].rearrange("p t e -> p e t"),
                 ALU.add))
        link(nc.vector.memset(cw[:, 8:10, :], 0.5 / WS))

        def unit(i, d, hb):
            for j in range(HT):
                cnt = 24 * i + (12 * d + 6 * hb + j)
                v.wait_ge(*upto("gu_mm", 2 * cnt + 2))
                v.wait_ge(*upto("silu", cnt + 1))
                stt(out=hid[:, hb, j, :], in0=banks[2 * (j % 2) + 1][:, 0:HALF], scalar=1.0 / WS, in1=sg[:, j % 2, :],
                    op0=ALU.mult, op1=ALU.mult).then_inc(S("hid_w"), 1)
                v.wait_ge(*upto("hid_w", cnt + 1))
                tt_(hid_lo[:, hb, j, :], hid[:, hb, j, :], hid_hi[:, hb, j, :], ALU.subtract).then_inc(S("hid_low"), 1)

        def add(i, d, hb):
            n0 = 12 * i + (6 * d + 3 * hb)
            for k in range(3):
                v.wait_ge(*upto("down", n0 + (2, 2, 3)[k]))
                src = banks[4 + 2 * hb + k // 2][:, (k % 2) * D:(k % 2 + 1) * D]
                tk = 3 * hb + k
                stt(out=h[:, tk, :], in0=src, scalar=cwc[:, d, tk:tk + 1], in1=h[:, tk, :], op0=ALU.mult,
                    op1=ALU.add).then_inc(S("added"), 1)

        def moe_iter(i, first):
            for d in range(2):
                unit(i, d, 0)
                if d == 1:
                    add(i, 0, 1)
                else:
                    if not first:
                        add(i - 1, 1, 1)
                        v.wait_ge(*upto("added", 12 * i))
                    nc.vector.tensor_copy(cwc[:, :, :], cw[:, bass.ds(2 * i, 2), :]).then_inc(S("cwc"), 1)
                    v.wait_ge(*upto("cwc", i + 1))
                unit(i, d, 1)
                add(i, d, 0)

        moe_iter(0, True)
        with v.Fori(1, EXPERTS // 2) as i:
            moe_iter(i, False)
        add(EXPERTS // 2 - 1, 1, 1)
        v.wait_ge(*upto("added", 6 * EXPERTS))

        layer_norm("ln3", lambda i: h[:, i, :], lambda i: x_tok[:, i, 0:D])
        for n in range(8):
            m, hf = n // 2, n % 2
            v.wait_ge(*upto("l1_qk", n + 1))
            ts_(qk[:, m, hf * HALF:(hf + 1) * HALF], banks[n % 2][0:HD, 0:HALF], small["b_qkv"][:, m:m + 1], None,
                ALU.add).then_inc(S("l1_qkd"), 1)
        for a in range(AT):
            v.wait_ge(*upto("l1_v", a + 1))
            nc.vector.tensor_copy(vg[:, a, :, 0:DH],
                                  banks[2 + a % 4][0:HD, 0:D].rearrange("p (n e) -> p n e", n=HEADS)).then_inc(S("l1_vd"), 1)
        v.wait_ge(*upto("l1_qkd", 8))
        spread(0, 2, "l1_blk", None)
        same = small["same"][:, :].unsqueeze(1).broadcast_to([HD, 3, HD])
        for n in range(2 * AT):
            if n + 1 < 2 * AT:
                spread(n + 1, 2, "l1_blk", "l1_s")
            if n >= 2:
                v.wait_ge(*upto("l1_pT", 2 * (n - 1)))
            for g in range(2):
                v.wait_ge(*upto("l1_s", 2 * n + g + 1))
                tt_(pr[:, n % 2, 3 * g:3 * g + 3, :],
                    banks[2 * (n % 2) + g][0:HD, 0:3 * HD].rearrange("p (k n) -> p k n", k=3), same,
                    ALU.add).then_inc(S("l1_sm"), 1)
            v.wait_ge(*upto("l1_sm", 2 * n + 2))
            link(nc.vector.tensor_reduce(mxs[:, n % 2, :], pr[:, n % 2, :, :], AX, ALU.max))
            tt_(pr[:, n % 2, :, :], pr[:, n % 2, :, :], mxs[:, n % 2, :].unsqueeze(2).broadcast_to([HD, 6, HD]),
                ALU.subtract).then_inc(S("l1_sub"), 1)
            if n % 2 == 1 and n > 1:
                o_norm1(v, n // 2 - 1, link, tt_)
        o_norm1(v, AT - 1, link, tt_)
        for c in range(4):
            v.wait_ge(*upto("l1_oT", c + 1))
            nc.vector.tensor_copy(xT_att[:, c // 2, (c % 2) * HALF:(c % 2 + 1) * HALF],
                                  banks[c][0:HD, 0:HALF]).then_inc(S("l1_aT"), 1)
        add_h("l1p")

        layer_norm("ln4", lambda i: h[:, i, :], lambda i: x_tok[:, i, 0:D], packed=True)
        v.wait_ge(*upto("f1_xT", 3))
        tt_(x_lo[:, :, :], xT[:, :, :], x_hi, ALU.subtract).then_inc(S("x_lo2"), 1)
        def gate_logits():
            v.wait_ge(*upto("glog", 2))
            l0 = banks[3][0:HD, 0:HALF].rearrange("p (i b) -> p i b", i=6)
            l1 = banks[4][0:HD, 0:HALF].rearrange("p (i b) -> p i b", i=6)
            link(nc.vector.tensor_copy(gq[1][:, :, :], l0))
            link(tt_(gq[0][:, :, :], l1, gq[1][:, :, :], ALU.max))
            tt_(gl[:, 0, :, :], l0, gq[0][:, :, :], ALU.subtract).then_inc(S("glog_read"), 1)
            tt_(gl[:, 1, :, :], l1, gq[0][:, :, :], ALU.subtract).then_inc(S("glog_read"), 1)
            v.wait_ge(*upto("glog_read", 2))
            nc.vector.memset(sdv[:, 0:1], 0.0).then_inc(S("gsub"), 1)

        def gate_shares():
            v.wait_ge(*upto("gexp", 1))
            link(tt_(gq[0][:, :, :], gl[:, 0, :, :], gl[:, 1, :, :], ALU.add))
            link(nc.vector.reciprocal(gq[0][:, :, :], gq[0][:, :, :]))
            link(tt_(gl[:, 0, :, :], gl[:, 0, :, :], gq[0][:, :, :], ALU.mult))
            link(tt_(gl[:, 1, :, :], gl[:, 1, :, :], gq[0][:, :, :], ALU.mult))
            link(tt_(gq[0][:, :, :], gl[:, 0, :, :], gl[:, 1, :, :], ALU.min))
            for k in range(2):
                link(tt_(gq[1 + k][:, :, :], gl[:, k, :, :], gq[0][:, :, :], ALU.is_gt))
                link(tt_(gl[:, k, :, :], gl[:, k, :, :], gq[1 + k][:, :, :], ALU.mult))
            link(tt_(gq[0][:, :, :], gl[:, 0, :, :], gl[:, 1, :, :], ALU.add))
            link(ts_(gq[0][:, :, :], gq[0][:, :, :], 1e-6, None, ALU.max))
            link(nc.vector.reciprocal(gq[0][:, :, :], gq[0][:, :, :]))
            for k in range(2):
                link(tt_(gl[:, k, :, :], gl[:, k, :, :], gq[0][:, :, :], ALU.mult))

        gates = (gate_logits, gate_shares)
        for u, cols, slots in UP:
            for j in range(HT):
                v.wait_ge(*upto("up2_act", 6 * u + j + 1))
                if slots is None:
                    tt_(hid_lo[:, 0, j, :], hid[:, 0, j, :], hid_hi[:, 0, j, :], ALU.subtract).then_inc(S("up2_low"), 1)
                else:
                    tt_(hc_lo[:, j, rng(slots), :], hc[:, j, rng(slots), :], hc_hi[:, j, rng(slots), :],
                        ALU.subtract).then_inc(S("up2_low"), 1)
            if u in (0, 1):
                gates[u]()
        yr = yT[:, :, :].rearrange("p k (b r) -> p k r b", r=12)
        for u, slots, direction, classes in DOWN:
            for m in range(2):
                cnt = 2 * u + m
                v.wait_ge(*upto("dn2_mm", cnt + 1))
                if slots is None:
                    src = banks[2 + cnt % 2][0:HD, 0:HALF].rearrange("p (r b) -> p r b", b=BATCH)
                    dst = yr[:, m, 6:12, :]
                else:
                    src = banks[2 + cnt % 2][0:HD, 0:slots[2] * BATCH].rearrange("p (r b) -> p r b", b=BATCH)
                    dst = yd[:, direction, m, rng(classes), :]
                ts_(dst, src, 1.0 / WS, small["b2"][:, m, u:u + 1], ALU.mult, ALU.add).then_inc(S("dn2_read"), 1)
        v.wait_ge(*upto("dn2_read", 12))
        for m in range(2):
            for k in range(2):
                link(tt_(yd[:, k, m, :, :], yd[:, k, m, :, :], gl[:, k, :, :], ALU.mult))
            ins = tt_(yr[:, m, 0:6, :], yd[:, 0, m, :, :], yd[:, 1, m, :, :], ALU.add)
        ins.then_inc(S("yT"), 1)
        for i in range(TT):
            v.wait_ge(*upto("y_tok", i // 2 * 2 + 2))
            tt_(outb[:, i, 0:D], banks[4 + i // 2][:, (i % 2) * D:(i % 2 + 1) * D], h[:, i, :],
                ALU.add).then_inc(S("out_ready"), 1)

    def o_norm0(v, a, link, tt_, ts_):
        v.wait_ge(*upto("l0_pv", 2 * a + 2))
        o = banks[4 + a % 2][0:HD, 0:HEADS * (DH + 1)].rearrange("p (n e) -> p n e", n=HEADS)
        r = rden[:, a * HEADS:(a + 1) * HEADS]
        link(ts_(r, o[:, :, DH], 1e-6, None, ALU.add))
        link(nc.vector.reciprocal(r, r))
        tt_(oa[:, a, :, :], o[:, :, 0:DH], r.unsqueeze(2).broadcast_to([HD, HEADS, DH]),
            ALU.mult).then_inc(S("l0_o"), 1)

    def o_norm1(v, a, link, tt_):
        v.wait_ge(*upto("l1_pv", 2 * a + 2))
        o = banks[4 + a % 2][0:HD, 0:HEADS * (DH + 1)].rearrange("p (n e) -> p n e", n=HEADS)
        r = rden[:, a * HEADS:(a + 1) * HEADS]
        link(nc.vector.reciprocal(r, o[:, :, DH]))
        tt_(oa[:, a, :, :], o[:, :, 0:DH], r.unsqueeze(2).broadcast_to([HD, HEADS, DH]),
            ALU.mult).then_inc(S("l1_o"), 1)

    return dict(sync=sync_prog, pool=pool_prog, act=act_prog, pe=pe_prog, dve=dve_prog)


def halves(w):
    return w.reshape(2, HD, -1).transpose(1, 0, 2)


def packed(w):
    return np.stack([w[..., 0:P, :], np.concatenate([w[..., P:D, :], w[..., P:D, :]], axis=-2)], axis=-2)


def rest_inputs(i):
    b12 = np.arange(HD) // 12
    same = b12[:, None] == b12[None, :]
    causal = same & (np.arange(HD)[:, None] <= np.arange(HD)[None, :])
    up1 = [np.concatenate([i[f"L0_ffn_{k}_gate"], i[f"L0_ffn_{k}_up"]], axis=1) for k in ("routed", "shared")]
    gu = np.concatenate(up1)
    dn = np.concatenate([i["L0_ffn_routed_down"], i["L0_ffn_shared_down"]])
    up2 = np.concatenate([i["L1_ffn_moe0_W1"][None], i["L1_ffn_A1_W"]])
    dn2 = np.concatenate([i["L1_ffn_moe0_W2"][None], i["L1_ffn_A2_W"]])
    b1 = np.concatenate([i["L1_ffn_moe0_b1"][None], i["L1_ffn_A1_b"]])
    b2 = np.concatenate([i["L1_ffn_moe0_b2"][None], i["L1_ffn_A2_b"]])
    small = {
        "fln": np.stack([i["L0_tok_fln_g"], i["L0_tok_fln_b"]], -1),
        "proj_w": i["L0_tok_proj_w"], "proj_b": i["L0_tok_proj_b"][None],
        "Wb1": halves(i["L0_attn_Wb1"]), "Wb2": i["L0_attn_Wb2"],
        "Wqkv": halves(i["L0_attn_Wqkv"]), "bqkv": i["L0_attn_bqkv"].reshape(6, HD).T,
        "bqkv_row": i["L0_attn_bqkv"][None],
        "ln_wb": np.stack([i["L0_attn_ln_w"].reshape(2, HD).T, i["L0_attn_ln_b"].reshape(2, HD).T], 1),
        "temp": np.broadcast_to(i["L0_attn_temperature"][None], (P, 1)),
        "mn": np.stack([np.tile(i["L0_attn_mn_w"], 6), np.tile(i["L0_attn_mn_b"], 6)], -1),
        "Wproj": halves(i["L0_attn_Wproj"]), "bproj_row": i["L0_attn_bproj"][None],
        "gate_w": packed(i["L0_ffn_gate_w"].T),
        "w_qkv": halves(i["L1_attn_w_qkv"]), "b_qkv": i["L1_attn_b_qkv"].reshape(6, HD).T,
        "b_qkv_row": i["L1_attn_b_qkv"][None],
        "w_proj": halves(i["L1_attn_w_proj"]), "b_proj_row": i["L1_attn_b_proj"][None],
        "G_W": np.broadcast_to(packed(i["L1_ffn_G_W"].transpose(1, 0, 2).reshape(D, 12)).reshape(P, 2, 6, 2, 1),
                               (P, 2, 6, 2, HD)),
        "b1": b1.reshape(6, HT, P).transpose(2, 0, 1), "b2": b2.reshape(6, 2, HD).transpose(2, 1, 0),
        "headmask": (np.arange(HD)[:, None] // DH == np.arange(6)[None]).astype(np.float32),
        "causal": causal.astype(np.float32), "same": np.where(same, 0.0, -1e30).astype(np.float32),
        "iota8": np.broadcast_to(np.arange(8, dtype=np.float32), (P, 8)),
    }
    large = {
        "gu": packed(gu.transpose(0, 2, 1)),
        "dn": dn.transpose(0, 2, 1).reshape(EXPERTS, HT, P, D).transpose(0, 2, 1, 3),
        "up2": packed(up2),
        "dn2": dn2.reshape(6, HT, P, D).transpose(0, 2, 1, 3),
    }
    return small, large


def build(nc, t, out):
    with ExitStack() as ctx, ExitStack() as conv_ctx:
        sb = lambda n, sh, dt: ctx.enter_context(nc.sbuf_tensor(n, sh, dt))
        conv_sb = lambda n, sh, dt: conv_ctx.enter_context(nc.sbuf_tensor(n, sh, dt))
        sem = lambda n: ctx.enter_context(nc.semaphore(n))
        banks = [ctx.enter_context(nc.psum_tensor(f"bank{i}", [P, 512], F32)) for i in range(8)]
        t["ident"] = sb("ident", [P, P], F32)
        t["scratch"] = nc.dram_tensor("scratch", (2, TAPS0, STREAM0), F16).ap()
        t["out"] = out.rearrange("b r d -> (b r) d").rearrange("(t p) d -> p t d", p=P)
        t["gu_flat"] = t["gu"].rearrange("e p k n -> (e p) (k n)")
        t["dn_flat"] = t["dn"].rearrange("e p k n -> (e p) (k n)")
        act6 = sb("act6", [P, NTOK], F32)
        t["small_sb"] = {n: sb("s_" + n, list(a.shape), F32) for n, a in t["small"].items()}
        t["small_in"] = sem("small_in")

        def load_small(sp):
            for n, a in t["small"].items():
                sp.dma_start(t["small_sb"][n][tuple(slice(None) for _ in a.shape)], a).then_inc(t["small_in"], 16)

        conv = build_conv(nc, conv_sb, lambda i: banks[i], sem, t, act6, load_small)
        conv_ctx.close()
        rest = build_rest(nc, sb, banks, sem, t, act6, conv)
        block = ctx.enter_context(nc.Block())

        @block.sync
        def _(sp):
            conv["sync"](sp)
            sp.wait_ge(conv["s"]["tail_act"], conv["tail"])
            rest["sync"](sp)

        @block.gpsimd
        def _(pool):
            conv["pool"](pool)
            rest["pool"](pool)

        @block.scalar
        def _(act):
            conv["act"](act)
            rest["act"](act)

        @block.tensor
        def _(pe):
            conv["pe"](pe)
            rest["pe"](pe)

        @block.vector
        def _(dve):
            conv["dve"](dve)
            dve.wait_ge(conv["s"]["tail_act"], conv["tail"])
            rest["dve"](dve)


def kernel(**inputs):
    import concourse.bacc as bacc
    from concourse.bass_utils import run_bass_kernel_spmd

    inputs = {k: np.asarray(v) for k, v in inputs.items()}
    small, large = rest_inputs(inputs)
    nc = bacc.Bacc("TRN2", target_bir_lowering=False, num_devices=1)
    arrays, t = {}, {"small": {}}
    for group, given in ((t, conv_inputs(inputs["x"], inputs)), (t["small"], small), (t, large)):
        for n, a in given.items():
            a = np.ascontiguousarray(a)
            arrays["in_" + n] = a
            group[n] = nc.dram_tensor("in_" + n, a.shape, mybir.dt.from_np(a.dtype), kind="ExternalInput").ap()
    out = nc.dram_tensor("out", (BATCH, 12, D), F32, kind="ExternalOutput").ap()
    build(nc, t, out)
    r = run_bass_kernel_spmd(nc, [arrays], core_ids=[0])
    return r.results[0]["out"]
```

```python
from contextlib import ExitStack

import numpy as np
import concourse.bass as bass
from concourse import mybir

F32 = mybir.dt.float32
F16 = mybir.dt.float16
BF16 = mybir.dt.bfloat16
U32 = mybir.dt.uint32
ALU = mybir.AluOpType
ACT = mybir.ActivationFunctionType
AX = mybir.AxisListType.X

P = 128
BATCH = 64
CH = 128
TAPS0, STRIDE0 = 10, 5
SLOTS0 = 800
STREAM0 = BATCH * SLOTS0
GROUPS = 8
FOLD = STREAM0 // GROUPS
WROWS = GROUPS * TAPS0
PIECE = 400
PIECES = FOLD // PIECE
CHUNK = 512
BODY0 = 2048
STEPS = STREAM0 // BODY0
WS = 256.0
GS = 256.0
EPS = 1e-5
SUMS = PIECES // 2 + 1


def vector_lows(pieces):
    return (pieces + 2) // 3


TAPS = [3, 3, 3, 3, 2, 2]
TAP0 = [0, 3, 6, 9, 12, 14]
NTAPS = 16


def conv_tail_chunks():
    out = []
    for layer, tokens in ((3, 6400), (4, 3200), (5, 1600)):
        for c in range(0, tokens, CHUNK):
            n = min(CHUNK, tokens - c)
            out.append((layer, c, [min(P, n - t) for t in range(0, n, P)]))
    for r in range(0, 12, 4):
        out.append((6, r, [BATCH] * 4))
    return out


def build_conv(nc, sb, ps, sem, t, act6, load_small):
    scr = t["scratch"]

    tail_ctx = ExitStack()
    tail_sb = lambda n, sh, dt: tail_ctx.enter_context(nc.sbuf_tensor(n, sh, dt))
    act = {2: sb("act2", [P, 12802], F32), 3: sb("act3", [P, 6401], F32), 6: act6}
    low = {2: sb("low2", [P, 12802], F16), 3: sb("low3", [P, 6401], F16)}
    act[4], act[5] = tail_sb("act4", [P, 3200], F32), tail_sb("act5", [P, 1600], F32)
    low[4], low[5] = tail_sb("low4", [P, 3200], F16), tail_sb("low5", [P, 1600], F16)
    tail_ctx.close()
    act[0], act[1] = sb("act0", [P, 1 + BODY0], F32), sb("act1", [P, 1 + BODY0 // 2], F32)
    low[0], low[1] = sb("low0", [P, 1 + BODY0], F16), sb("low1", [P, 1 + BODY0 // 2], F16)
    wt = sb("wt", [64, 2, BODY0], F16)
    high = {l: act[l][:, :].bitcast(BF16).rearrange("p (n two) -> p n two", two=2)[:, :, 1] for l in range(6)}
    win = act[2][:, 0:FOLD]
    win_hi = low[2][0:WROWS, 0:FOLD]
    win_lo = low[2][0:WROWS, FOLD:2 * FOLD]
    raw = act[3][:, 0:NTAPS * CH].rearrange("p (t n) -> p t n", t=NTAPS)
    raw0 = act[2][0:64, 2 * FOLD - 2 * CH:2 * FOLD - CH]
    g0rows = act[2][0:64, 2 * FOLD - CH:2 * FOLD]
    w_cen = act[3][:, NTAPS * CH:2 * NTAPS * CH].rearrange("p (t n) -> p t n", t=NTAPS)
    w_hi = sb("w_hi", [P, NTAPS, CH], F16)
    w_lo = sb("w_lo", [P, NTAPS, CH], F16)
    w_mean = sb("w_mean", [P, NTAPS], F32)
    w0_mean = sb("w0_mean", [64, 1], F32)
    w0st = sb("w0st", [64, CH], F16)
    w0hi = sb("w0hi", [64, CH], F16)
    wrep = sb("wrep", [P, WROWS], F32)
    wrepc = sb("wrepc", [P, WROWS], F32)
    gram = sb("gram", [P, P], F32)
    blk = sb("blk", [WROWS, WROWS], F32)
    f16_area = act[2][:, FOLD:FOLD + P + PIECES * WROWS // 2].bitcast(F16)
    pick = f16_area[:, 0:2 * P - GROUPS]
    back = f16_area[:, 2 * P:2 * P + PIECES * WROWS].rearrange("p (c r) -> p c r", c=PIECES)
    cen = sb("cen", [P, P], F32)
    odd = lambda x: x.bitcast(BF16).rearrange("p (n two) -> p n two", two=2)[:, :, 1]
    gt_area = act[3][:, 2 * NTAPS * CH:2 * NTAPS * CH + 3 * PIECE]
    gt = gt_area.rearrange("p (k n) -> p k n", k=3)
    gt_hi = odd(gt_area).rearrange("p (k n) -> p k n", k=3)
    gt_lo = low[3][:, 0:3 * PIECE].rearrange("p (k n) -> p k n", k=3)
    sd_lo = low[0][:, 1:1 + PIECE]
    sd = sb("sd", [P, PIECE], F32)
    xn0 = act[3][0:WROWS, 2 * NTAPS * CH:2 * NTAPS * CH + 4 * PIECE].rearrange("p (k n) -> p k n", k=4)
    ident = t["ident"]
    gb = sb("gb", [P, 7, 2], F32)
    eps1 = sb("eps1", [P, 1], F32)
    unused = sb("unused", [P, 1], F32)
    expo = sb("expo", [P, 4], F32)
    st = sb("st", [P, 3, 4, 6], F32)
    sq = sb("sq", [P, 3, 4], F32)
    s2 = sb("s2", [P, 3, 4], F32)
    var = sb("var", [P, 3, 4], F32)
    rstd = sb("rstd", [P, 3, 4], F32)
    yn = sb("yn", [P, 3, 4, CH], F32)

    yb = [ps(i) for i in range(3)]
    zb = [ps(i + 3) for i in range(3)]
    z0 = [ps(6), ps(7)]
    gx = [yb[0], yb[1], zb[0]]

    names = ["loaded", "loaded2", "cen_ps", "cen_sb", "gram_ps", "gram_sb", "wsplit", "w0split",
             "gx_ps", "gx_sb", "gx_lo", "gx_lo_v",
             "pick_ps", "var_sb", "std_sb", "w_loaded", "rstd_sb", "rstd_ps", "xn_sb", "hi_sb", "lo_sb", "lo_sb_p", "w_mean", "w_cen",
             "ch_v", "scr_out", "win_part0", "win_part1", "win_part2", "win_part3",
             "conv0_ps", "act0_w", "low0_w", "halo0", "halo1",
             "zeroed", "expo_set", "tail_y", "tail_var", "tail_rstd", "tail_norm", "tail_z",
             "tail_act", "tail_low", "ch_p"]
    s = {n: sem("c_" + n) for n in names}
    s["win_in"] = [sem(f"c_win_in{i}") for i in range(2)]
    kinds = "ABC"
    q = {n: {k: sem(f"c_{n}{k}") for k in kinds} for n in
         ["y", "var", "rstd", "norm", "z", "act", "low"]}
    tail = conv_tail_chunks()
    tail_index = {}
    for n, (l, c, sizes) in enumerate(tail):
        tail_index[(l, c)] = n

    def need(n):
        l, c, sizes = tail[n]
        if l == 3:
            return 0
        if l == 6:
            return max(i for i, (ll, cc, ss) in enumerate(tail) if ll == 5) + 1
        end = 2 * (c + sum(sizes)) + (1 if l == 4 else 0)
        return max(i for i, (ll, cc, ss) in enumerate(tail) if ll == l - 1 and cc < end) + 1

    def sync_prog(sp):
        for dst, src in ((wrep[:, :], t["w0rep"]), (blk[:, :], t["blk"]), (cen[:, :], t["cen"]),
                         (pick, t["pick"])):
            sp.dma_start(dst, src).then_inc(s["loaded"], 16)
        for part in range(4):
            cols = slice(part * FOLD // 4, (part + 1) * FOLD // 4)
            sp.dma_start(win[:, cols], t["windows"][:, cols]).then_inc(s[f"win_part{part}"], 16)
        sp.dma_start(raw, t["conv_w"]).then_inc(s["w_loaded"], 16)
        for dst, src in ((gb[:, :, :], t["conv_gb"]), (ident[:, :], t["ident_d"]),
                         (back, t["back"])):
            sp.dma_start(dst, src).then_inc(s["loaded2"], 16)
        sp.wait_ge(s["zeroed"], 4)
        for h in range(2):
            sp.dma_start(raw0[32 * h:32 * h + 20, :], t["w0rows"]).then_inc(s["loaded2"], 16)
            sp.dma_start(g0rows[32 * h:32 * h + 20, :], t["g0rows"]).then_inc(s["loaded2"], 16)
        load_small(sp)
        sp.wait_ge(s["zeroed"], 2)
        for i in range(2):
            pieces = -(-(i + 1) * BODY0 // PIECE)
            sp.wait_ge(s["hi_sb"], pieces)
            sp.wait_ge(s["lo_sb"], vector_lows(pieces))
            sp.wait_ge(s["lo_sb_p"], pieces - vector_lows(pieces))
            for h in range(2):
                for k, src in enumerate((win_hi, win_lo)):
                    first = 32 * h + TAPS0 * k
                    sp.dma_start(wt[first:first + TAPS0, i, :],
                                 src[0:TAPS0, i * BODY0:(i + 1) * BODY0]).then_inc(s["win_in"][i], 16)
        sp.wait_ge(s["hi_sb"], PIECES)
        sp.wait_ge(s["lo_sb"], vector_lows(PIECES))
        sp.wait_ge(s["lo_sb_p"], PIECES - vector_lows(PIECES))
        for g in range(GROUPS):
            for h, src in enumerate((win_hi, win_lo)):
                sp.dma_start(scr[h, :, g * FOLD:(g + 1) * FOLD],
                             src[g * TAPS0:(g + 1) * TAPS0, :]).then_inc(s["scr_out"], 16)
        rows = scr.rearrange("h k n -> (h k) n")

        def load(i, par):
            for h in range(2):
                sp.dma_start(wt[32 * h:32 * h + 20, par, :],
                             rows[:, bass.ds(i * BODY0, BODY0)]).then_inc(s["win_in"][par], 16)

        sp.wait_ge(s["scr_out"], 16 * 2 * GROUPS)
        with sp.Fori(0, (STEPS - 3) // 2) as j:
            sp.wait_ge(s["conv0_ps"], 8 * j + 4)
            load(2 * j + 2, 0)
            sp.wait_ge(s["conv0_ps"], 8 * j + 8)
            load(2 * j + 3, 1)
        sp.wait_ge(s["conv0_ps"], 4 * (STEPS - 2))
        load(STEPS - 1, 0)

    def pool_prog(pool):
        nc.gpsimd.memset(expo[:, :], -0.5).then_inc(s["expo_set"], 1)
        nc.gpsimd.memset(low[3][:, 6400:6401], 0.0).then_inc(s["expo_set"], 1)
        pool.wait_ge(s["expo_set"], 2)
        for c in range(PIECES):
            if c % 4 == 3:
                continue
            pool.wait_ge(s["gx_sb"], c + 1)
            if c >= 3:
                pool.wait_ge(s["pick_ps"], c - 2)
            nc.gpsimd.tensor_tensor(gt_lo[:, c % 3, :], gt[:, c % 3, :], gt_hi[:, c % 3, :],
                                    ALU.subtract).then_inc(s["gx_lo"], 1)
        pool.wait_ge(s["wsplit"], 1)
        nc.gpsimd.tensor_tensor(w_lo[:, :, :], w_cen, w_hi[:, :, :], ALU.subtract).then_inc(s["wsplit"], 1)
        pool.wait_ge(s["wsplit"], 2)
        for c in range(PIECES):
            if c % 3 == 0:
                continue
            pool.wait_ge(s["hi_sb"], c + 1)
            cols = slice(c * PIECE, (c + 1) * PIECE)
            nc.gpsimd.tensor_tensor(win_lo[:, cols], xn0[:, c % 4, :], win_hi[:, cols],
                                    ALU.subtract).then_inc(s["lo_sb_p"], 1)
        pool.wait_ge(s["lo_sb_p"], PIECES - vector_lows(PIECES))

        def power(k, slot, cnt):
            pool.wait_ge(q["var"][k], cnt)
            nc.gpsimd.tensor_tensor(rstd[:, slot, :], var[:, slot, :], expo[:, :], ALU.pow).then_inc(q["rstd"][k], 1)

        def lower(k, l, off, cnt):
            pool.wait_ge(q["act"][k], cnt)
            a = act[l][:, bass.ds(off, CHUNK)]
            nc.gpsimd.tensor_tensor(low[l][:, bass.ds(off, CHUNK)], a, high[l][:, bass.ds(off, CHUNK)],
                                    ALU.subtract).then_inc(q["low"][k], 1)

        def step(i, has_b, has_c):
            if has_b:
                lower("B", 1, 1 + CHUNK, i)
            power("A", 0, i + 1)
            power("B", 1, i + 1)
            if has_c:
                lower("C", 2, (i - 2) * CHUNK, i - 1)
            if has_b:
                power("C", 2, i)
            lower("A", 1, 1, i + 1)

        step(0, False, False)
        step(1, True, False)
        with pool.Fori(2, STEPS) as i:
            step(i, True, True)

        def tail_power(n):
            pool.wait_ge(s["tail_var"], n + 1)
            l, c, sizes = tail[n]
            k, m = len(sizes), sizes[-1]
            nc.gpsimd.tensor_tensor(rstd[0:m, n % 3, 0:k], var[0:m, n % 3, 0:k], expo[0:m, 0:k],
                                    ALU.pow).then_inc(s["tail_rstd"], 1)

        def tail_lower(n):
            l, c, sizes = tail[n]
            pool.wait_ge(s["tail_act"], n + 1)
            if l < 6:
                m = sum(sizes)
                nc.gpsimd.tensor_tensor(low[l][:, c:c + m], act[l][:, c:c + m], high[l][:, c:c + m],
                                        ALU.subtract).then_inc(s["tail_low"], 1)

        lower("B", 1, 1 + CHUNK, STEPS)
        tail_power(0)
        lower("C", 2, (STEPS - 2) * CHUNK, STEPS - 1)
        power("C", 2, STEPS)
        tail_power(1)
        lower("C", 2, (STEPS - 1) * CHUNK, STEPS)
        for kind, m in tail_schedule[2:]:
            if kind == "conv":
                tail_power(m)
            else:
                tail_lower(m)

    tail_schedule = []
    done_t = 0
    for n in range(len(tail)):
        while done_t < need(n) or done_t < n - 2:
            tail_schedule.append(("turn", done_t))
            done_t += 1
        tail_schedule.append(("conv", n))
    while done_t < len(tail):
        tail_schedule.append(("turn", done_t))
        done_t += 1

    def act_prog(a):
        a.wait_ge(s["zeroed"], 1)
        nc.scalar.activation(unused[:, :], eps1[:, :], ACT.Sqrt)
        for w in range(NTAPS):
            if w * 4 % NTAPS == 0:
                a.wait_ge(s["w_mean"], w * 4 // NTAPS + 1)
            nc.scalar.activation(w_cen[:, w, :], raw[:, w, :], ACT.Identity, bias=w_mean[:, w:w + 1],
                                 scale=WS).then_inc(s["w_cen"], 1)
        a.wait_ge(s["w_cen"], NTAPS)
        nc.scalar.activation(w_hi[:, :, :], w_cen, ACT.Copy).then_inc(s["wsplit"], 1)
        a.wait_ge(s["var_sb"], 1)
        nc.scalar.activation(sd[:, :], sd[:, :], ACT.Sqrt, bias=eps1[:, :],
                             scale=1.0 / GS).then_inc(s["std_sb"], 1)
        nc.scalar.activation(unused[:, :], eps1[:, :], ACT.Gelu)
        for c in range(PIECES):
            a.wait_ge(s["xn_sb"], c + 1)
            nc.scalar.activation(win_hi[:, c * PIECE:(c + 1) * PIECE], xn0[:, c % 4, :],
                                 ACT.Copy).then_inc(s["hi_sb"], 1)

        def gelu0(i, half, first):
            for c in range(2):
                a.wait_ge(s["conv0_ps"], 4 * i + (2 * half + c + 1))
                if not first:
                    a.wait_ge(q["y"]["B"], i)
                    if half == 1 and c == 1:
                        a.wait_ge(s["halo0"], 2 * i)
                if first and half == 0 and c == 0:
                    a.wait_ge(s["zeroed"], 6)
                off = 1 + half * 1024 + c * CHUNK
                nc.scalar.activation(act[0][:, off:off + CHUNK], z0[c][:, :], ACT.Gelu,
                                     bias=gb[:, 0, 1:2], scale=1.0 / WS).then_inc(s["act0_w"], 1)

        def gelu(k, slot, l, off, cnt):
            a.wait_ge(q["z"][k], cnt)
            nc.scalar.activation(act[l][:, bass.ds(off, CHUNK)], zb[slot][:, :], ACT.Gelu,
                                 bias=gb[:, l, 1:2], scale=gb[:, l, 0:1]).then_inc(q["act"][k], 1)

        def step(i, has_b, has_c, has_next, first=False):
            if has_b:
                if not first:
                    a.wait_ge(s["halo1"], 2 * (i - 1))
                gelu("B", 1, 1, 1 + CHUNK, i)
            if has_next:
                gelu0(i + 1, 0, False)
            if has_c:
                gelu("C", 2, 2, (i - 2) * CHUNK, i - 1)
            if has_next:
                gelu0(i + 1, 1, False)
            if has_b:
                a.wait_ge(q["y"]["C"], i)
                a.wait_ge(q["low"]["B"], i)
                for x in (act[1], low[1]):
                    nc.scalar.activation(x[:, 0:1], x[:, CHUNK * 2:CHUNK * 2 + 1], ACT.Copy).then_inc(s["halo1"], 1)
            gelu("A", 0, 1, 1, i + 1)

        gelu0(0, 0, True)
        gelu0(0, 1, True)
        step(0, False, False, True)
        step(1, True, False, True, first=True)
        with a.Fori(2, STEPS - 1) as i:
            step(i, True, True, True)
        step(STEPS - 1, True, True, False)
        a.wait_ge(s["halo1"], 2 * (STEPS - 1))
        gelu("B", 1, 1, 1 + CHUNK, STEPS)
        gelu("C", 2, 2, (STEPS - 2) * CHUNK, STEPS - 1)
        gelu("C", 2, 2, (STEPS - 1) * CHUNK, STEPS)
        for kind, n in tail_schedule:
            if kind == "turn":
                l, c, sizes = tail[n]
                m = sum(sizes)
                a.wait_ge(s["tail_z"], n + 1)
                if l == 6:
                    dst = act[6][:, :].rearrange("p (b r) -> p r b", b=BATCH)[:, c:c + 4, :]
                    src = zb[n % 3][:, 0:m].rearrange("p (r b) -> p r b", r=4)
                else:
                    dst, src = act[l][:, c:c + m], zb[n % 3][:, 0:m]
                nc.scalar.activation(dst, src, ACT.Gelu,
                                     bias=gb[:, l, 1:2], scale=gb[:, l, 0:1]).then_inc(s["tail_act"], 1)

    def pe_prog(pe):
        pe.wait_ge(s["loaded"], 4 * 16)
        nc.tensor.matmul(zb[0][:, 0:WROWS], cen[:, :], wrep[:, :], start=True, stop=True).then_inc(s["cen_ps"], 1)
        pe.wait_ge(s["cen_sb"], 1)
        nc.tensor.matmul(zb[1][0:WROWS, 0:WROWS], wrepc[:, :], wrepc[:, :], start=True,
                         stop=True).then_inc(s["gram_ps"], 1)
        pe.wait_ge(s["gram_sb"], 1)
        for c in range(PIECES + 2):
            if c < PIECES:
                if c * 4 % PIECES == 0:
                    pe.wait_ge(s[f"win_part{c * 4 // PIECES}"], 16)
                if c >= 3:
                    pe.wait_ge(s["gx_sb"], c - 2)
                nc.tensor.matmul(gx[c % 3][:, 0:PIECE], gram[:, :], win[:, c * PIECE:(c + 1) * PIECE], start=True,
                                 stop=True).then_inc(s["gx_ps"], 1)
            if c >= 2:
                if (c - 2) % 4 == 3:
                    pe.wait_ge(s["gx_lo_v"], (c - 1) // 4)
                else:
                    pe.wait_ge(s["gx_lo"], c - 1 - (c - 1) // 4)
                first = P - GROUPS - GROUPS * (c - 2)
                for n, part in enumerate((gt_hi, gt_lo)):
                    last = nc.tensor.matmul(yb[2][:, 0:PIECE], pick[:, first:first + P], part[:, (c - 2) % 3, :],
                                            start=(c == 2 and n == 0), stop=(c == PIECES + 1 and n == 1))
                last.then_inc(s["pick_ps"], 1)
        pe.wait_ge(s["loaded2"], 7 * 16)
        pe.wait_ge(s["rstd_sb"], 1)
        for c in range(PIECES):
            if c >= 3:
                pe.wait_ge(s["xn_sb"], c - 2)
            nc.tensor.matmul(zb[c % 3][0:WROWS, 0:PIECE], back[:, c, :], odd(sd[:, :]), start=True, stop=False)
            nc.tensor.matmul(zb[c % 3][0:WROWS, 0:PIECE], back[:, c, :], sd_lo, start=False,
                             stop=True).then_inc(s["rstd_ps"], 1)

        def conv0(i, half, parity, first=False):
            for c in range(2):
                off = half * 1024 + c * CHUNK
                if not first:
                    pe.wait_ge(s["act0_w"], 4 * i + 2 * half + c - 1)
                elif half == 1:
                    pe.wait_ge(s["act0_w"], c + 1)
                nc.tensor.matmul(z0[c][:, :], w0st[0:52, :], wt[0:52, parity, off:off + CHUNK],
                                 start=True, stop=True).then_inc(s["conv0_ps"], 1)

        def conv(bank, l, firsts, sizes):
            last = None
            for ti, (f, m) in enumerate(zip(firsts, sizes)):
                out = bank[0:m, ti * CH:(ti + 1) * CH]
                n, total = 0, 3 * TAPS[l - 1]
                for tap in range(TAPS[l - 1]):
                    hi, lo = f(tap)
                    w = TAP0[l - 1] + tap
                    for x, y in ((hi, w_hi), (hi, w_lo), (lo, w_hi)):
                        last = nc.tensor.matmul(out, x, y[:, w, :], start=(n == 0), stop=(n == total - 1))
                        n += 1
            return last

        def stream_conv(k, slot, l, off):
            fs = [lambda tap, o=off + 256 * j: [x[:, o + tap:o + tap + 255:2] for x in (high[l - 1], low[l - 1])]
                  for j in range(4)]
            conv(yb[slot], l, fs, [P] * 4).then_inc(q["y"][k], 1)

        def turn(k, slot, cnt, gelu_cnt):
            pe.wait_ge(q["norm"][k], cnt)
            if gelu_cnt is not None:
                pe.wait_ge(q["act"][k], gelu_cnt)
            for j in range(4):
                last = nc.tensor.transpose(zb[slot][:, j * P:(j + 1) * P], yn[:, slot, j, :], ident[:, :])
            last.then_inc(q["z"][k], 1)

        def step(i, has_b, has_c, has_next, parity=0, loads=0, z_used=True):
            pe.wait_ge(s["low0_w"], 4 * i + 2)
            pe.wait_ge(s["act0_w"], 4 * i + 2)
            if has_b:
                pe.wait_ge(s["halo0"], 2 * i)
                pe.wait_ge(q["norm"]["A"], i)
            stream_conv("A", 0, 1, 0)
            if has_b:
                turn("B", 1, i, i - 1 if z_used else None)
            pe.wait_ge(s["low0_w"], 4 * i + 4)
            if has_b:
                pe.wait_ge(q["norm"]["B"], i)
            stream_conv("B", 1, 1, 1024)
            if has_next:
                pe.wait_ge(s["win_in"][parity], loads)
                conv0(i + 1, 0, parity)
            if has_c:
                turn("C", 2, i - 1, i - 2 if z_used != "c" else None)
            if has_b:
                pe.wait_ge(q["low"]["A"], i)
                pe.wait_ge(q["low"]["B"], i)
                if has_c:
                    pe.wait_ge(s["halo1"], 2 * (i - 1))
                    pe.wait_ge(q["norm"]["C"], i - 1)
                stream_conv("C", 2, 2, 0)
            if has_next:
                conv0(i + 1, 1, parity)
            turn("A", 0, i + 1, i if has_b else None)

        pe.wait_ge(s["w0split"], 1)
        pe.wait_ge(s["win_in"][0], 64)
        conv0(0, 0, 0, True)
        conv0(0, 1, 0, True)
        pe.wait_ge(s["wsplit"], 2)
        loads = lambda i: 32 * (i // 2 + 2)
        step(0, False, False, True, 1, loads(1))
        step(1, True, False, True, 0, loads(2), z_used=False)
        step(2, True, True, True, 1, loads(3), z_used="c")
        with pe.Fori(0, (STEPS - 5) // 2) as j:
            for d in range(2):
                step(2 * j + (3 + d), True, True, True, d, 32 * j + loads(4 + d))
        step(STEPS - 2, True, True, True, (STEPS - 1) % 2, loads(STEPS - 1))
        step(STEPS - 1, True, True, False)
        turn("B", 1, STEPS, STEPS - 1)

        def tail_conv(n):
            l, c, sizes = tail[n]
            if l == 3:
                pe.wait_ge(q["low"]["C"], min(STEPS, 2 * n + 3))
            if need(n):
                pe.wait_ge(s["tail_low"], need(n))
            if n >= 3:
                pe.wait_ge(s["tail_norm"], n - 2)
            else:
                pe.wait_ge(q["norm"][kinds[n]], STEPS)
            fs = []
            for ti in range(len(sizes)):
                if l == 6:
                    fs.append(lambda tap, r=c + ti: [x[:, 2 * r + tap:2 * r + tap + 25 * 63 + 1:25]
                                                     for x in (high[5], low[5])])
                else:
                    o = 2 * (c + P * ti) + (1 if l == 3 else 0)
                    fs.append(lambda tap, o=o, m=sizes[ti]: [x[:, o + tap:o + tap + 2 * m - 1:2]
                                                          for x in (high[l - 1], low[l - 1])])
            conv(yb[n % 3], l, fs, sizes).then_inc(s["tail_y"], 1)

        tail_conv(0)
        turn("C", 2, STEPS - 1, STEPS - 2)
        pe.wait_ge(q["low"]["A"], STEPS)
        pe.wait_ge(q["low"]["B"], STEPS)
        pe.wait_ge(s["halo1"], 2 * (STEPS - 1))
        pe.wait_ge(q["norm"]["C"], STEPS - 1)
        stream_conv("C", 2, 2, 0)
        pe.wait_ge(s["expo_set"], 2)
        tail_conv(1)
        turn("C", 2, STEPS, STEPS - 1)
        for kind, n in tail_schedule[2:]:
            l, c, sizes = tail[n]
            if kind == "conv":
                tail_conv(n)
            else:
                pe.wait_ge(s["tail_norm"], n + 1)
                if n >= 3:
                    pe.wait_ge(s["tail_act"], n - 2)
                else:
                    pe.wait_ge(q["act"][kinds[n]], STEPS)
                off = 0
                for ti, m in enumerate(sizes):
                    last = nc.tensor.transpose(zb[n % 3][:, off:off + m], yn[0:m, n % 3, ti, :], ident[0:m, 0:m])
                    off += m
                last.then_inc(s["tail_z"], 1)

    def dve_prog(v):
        chain = [0]

        def link(ins):
            chain[0] += 1
            ins.then_inc(s["ch_v"], 1)
            v.wait_ge(s["ch_v"], chain[0])

        nc.vector.memset(eps1[:, :], EPS).then_inc(s["zeroed"], 1)
        nc.vector.memset(wt[:, :, :], 0.0).then_inc(s["zeroed"], 1)
        nc.vector.memset(raw0[:, :], 0.0).then_inc(s["zeroed"], 1)
        nc.vector.memset(g0rows[:, :], 0.0).then_inc(s["zeroed"], 1)
        nc.vector.memset(act[0][:, 0:1], 0.0).then_inc(s["zeroed"], 1)
        nc.vector.memset(low[0][:, 0:1], 0.0).then_inc(s["zeroed"], 1)
        link(nc.vector.memset(act[1][:, 0:1], 0.0))
        link(nc.vector.memset(low[1][:, 0:1], 0.0))
        link(nc.vector.memset(act[2][:, 12800:12802], 0.0))
        link(nc.vector.memset(low[2][:, 12800:12802], 0.0))
        link(nc.vector.memset(act[3][:, 6400:6401], 0.0))
        link(nc.vector.memset(w0st[:, :], 0.0))
        link(nc.vector.memset(gram[:, :], 0.0))
        v.wait_ge(s["cen_ps"], 1)
        nc.vector.tensor_copy(wrepc[:, :], zb[0][:, 0:WROWS]).then_inc(s["cen_sb"], 1)
        v.wait_ge(s["gram_ps"], 1)
        nc.vector.scalar_tensor_tensor(out=gram[0:WROWS, 0:WROWS], in0=zb[1][0:WROWS, 0:WROWS], scalar=GS / CH,
                                       in1=blk[:, :], op0=ALU.mult, op1=ALU.mult).then_inc(s["gram_sb"], 1)

        def weight_means(part):
            v.wait_ge(s["w_loaded"], 16)
            taps = slice(part * NTAPS // 4, (part + 1) * NTAPS // 4)
            link(nc.vector.reduce_sum(w_mean[:, taps], raw[:, taps, :], AX))
            nc.vector.tensor_scalar(w_mean[:, taps], w_mean[:, taps], -WS / CH, None,
                                    ALU.mult).then_inc(s["w_mean"], 1)

        def first_weights():
            rows = slice(0, 52)
            v.wait_ge(s["loaded2"], 7 * 16)
            link(nc.vector.reduce_sum(w0_mean[rows, 0:1], raw0[rows, :], AX))
            link(nc.vector.tensor_scalar(w0_mean[rows, 0:1], w0_mean[rows, 0:1], 1.0 / CH, None, ALU.mult))
            link(nc.vector.tensor_scalar(raw0[rows, :], raw0[rows, :], w0_mean[rows, 0:1], WS / 4, ALU.subtract,
                                         ALU.mult))
            link(nc.vector.tensor_tensor(raw0[rows, :], raw0[rows, :], g0rows[rows, :], ALU.mult))
            link(nc.vector.tensor_copy(w0hi[rows, :], raw0[rows, :]))
            link(nc.vector.tensor_copy(w0st[0:20, :], w0hi[0:20, :]))
            nc.vector.tensor_tensor(w0st[32:52, :], raw0[32:52, :], w0hi[32:52, :],
                                    ALU.subtract).then_inc(s["w0split"], 1)

        for c in range(PIECES):
            v.wait_ge(s["gx_ps"], c + 1)
            if c >= 3:
                v.wait_ge(s["pick_ps"], c - 2)
            nc.vector.tensor_tensor(gt[:, c % 3, :], gx[c % 3][:, 0:PIECE],
                                    win[:, c * PIECE:(c + 1) * PIECE], ALU.mult).then_inc(s["gx_sb"], 1)
            if c % 4 == 3:
                v.wait_ge(s["gx_sb"], c + 1)
                nc.vector.tensor_tensor(gt_lo[:, c % 3, :], gt[:, c % 3, :], gt_hi[:, c % 3, :],
                                        ALU.subtract).then_inc(s["gx_lo_v"], 1)
            if SUMS <= c < SUMS + 4:
                weight_means(c - SUMS)
        v.wait_ge(s["pick_ps"], PIECES)
        nc.vector.tensor_scalar(sd[:, :], yb[2][:, 0:PIECE], 0.0, None, ALU.max).then_inc(s["var_sb"], 1)
        v.wait_ge(s["std_sb"], 1)
        link(nc.vector.reciprocal(sd[:, :], sd[:, :]))
        nc.vector.tensor_tensor(sd_lo, sd[:, :], odd(sd[:, :]), ALU.subtract).then_inc(s["rstd_sb"], 1)
        first_weights()
        for c in range(PIECES + 1):
            if c < PIECES:
                v.wait_ge(s["rstd_ps"], c + 1)
                if c >= 4:
                    v.wait_ge(s["hi_sb"], c - 3)
                    if (c - 4) % 3 == 0:
                        v.wait_ge(s["lo_sb"], vector_lows(c - 3))
                    else:
                        v.wait_ge(s["lo_sb_p"], c - 3 - vector_lows(c - 3))
                cols = slice(c * PIECE, (c + 1) * PIECE)
                nc.vector.scalar_tensor_tensor(out=xn0[:, c % 4, :], in0=win[0:WROWS, cols], scalar=4.0,
                                               in1=zb[c % 3][0:WROWS, 0:PIECE], op0=ALU.mult,
                                               op1=ALU.mult).then_inc(s["xn_sb"], 1)
            if c % 3 == 1:
                v.wait_ge(s["hi_sb"], c)
                cols = slice((c - 1) * PIECE, c * PIECE)
                nc.vector.tensor_tensor(win_lo[:, cols], xn0[:, (c - 1) % 4, :], win_hi[:, cols],
                                        ALU.subtract).then_inc(s["lo_sb"], 1)

        ch2 = s["ch_p"]

        def stats(bank, slot, sizes, done, base):
            k, m = len(sizes), sizes[-1]
            for j in range(k):
                nc.vector.bn_stats(st[0:sizes[j], slot, j, :], bank[0:sizes[j], j * CH:(j + 1) * CH]).then_inc(ch2, 1)
            v.wait_ge(ch2, base + k)
            nc.vector.tensor_tensor(sq[0:m, slot, 0:k], st[0:m, slot, 0:k, 1], st[0:m, slot, 0:k, 1],
                                    ALU.mult).then_inc(ch2, 1)
            nc.vector.scalar_tensor_tensor(out=s2[0:m, slot, 0:k], in0=st[0:m, slot, 0:k, 2],
                                           scalar=EPS * WS * WS * CH, in1=st[0:m, slot, 0:k, 5], op0=ALU.add,
                                           op1=ALU.add).then_inc(ch2, 1)
            v.wait_ge(ch2, base + k + 2)
            nc.vector.scalar_tensor_tensor(out=var[0:m, slot, 0:k], in0=s2[0:m, slot, 0:k], scalar=1.0 / CH,
                                           in1=sq[0:m, slot, 0:k], op0=ALU.mult, op1=ALU.add).then_inc(done, 1)

        def stream_stats(k, slot, cnt, base):
            v.wait_ge(q["y"][k], cnt)
            stats(yb[slot], slot, [P] * 4, q["var"][k], base)

        def norm(k, slot, cnt, reuse=True):
            v.wait_ge(q["rstd"][k], cnt)
            if reuse:
                v.wait_ge(q["z"][k], cnt - 1)
            nc.vector.tensor_tensor(yn[:, slot, :, :], yb[slot][:, :].rearrange("p (j n) -> p j n", j=4),
                                    rstd[:, slot, :].unsqueeze(2).broadcast_to([P, 4, CH]),
                                    ALU.mult).then_inc(q["norm"][k], 1)

        def low0(i, half):
            for c in range(2):
                v.wait_ge(s["act0_w"], 4 * i + 2 * half + c + 1)
                off = 1 + half * 1024 + c * CHUNK
                nc.vector.tensor_tensor(low[0][:, off:off + CHUNK], act[0][:, off:off + CHUNK],
                                        high[0][:, off:off + CHUNK], ALU.subtract).then_inc(s["low0_w"], 1)

        def step(i, has_b, has_c, has_next, base):
            n = 0
            stream_stats("A", 0, i + 1, base)
            n += 6
            if has_b:
                norm("C", 2, i - 1, has_c != "first") if has_c else None
            stream_stats("B", 1, i + 1, base + 6)
            n += 6
            norm("A", 0, i + 1, has_b)
            if has_next:
                v.wait_ge(s["low0_w"], 4 * i + 4)
                nc.vector.tensor_copy(act[0][:, 0:1], act[0][:, BODY0:BODY0 + 1]).then_inc(s["halo0"], 1)
                nc.vector.tensor_copy(low[0][:, 0:1], low[0][:, BODY0:BODY0 + 1]).then_inc(s["halo0"], 1)
                low0(i + 1, 0)
            norm("B", 1, i + 1, has_b)
            if has_b:
                stream_stats("C", 2, i, base + 12)
                n += 6
            if has_next:
                low0(i + 1, 1)
            return n

        low0(0, 0)
        low0(0, 1)
        base = step(0, False, False, True, 0)
        base += step(1, True, False, True, base)
        base += step(2, True, "first", True, base)
        with v.Fori(3, STEPS - 1) as i:
            step(i, True, True, True, 18 * i + (base - 54))
        base += 18 * (STEPS - 4)
        base += step(STEPS - 1, True, True, False, base)
        norm("C", 2, STEPS - 1)
        def tail_norm(n):
            l, c, sizes = tail[n]
            k, m = len(sizes), sizes[-1]
            v.wait_ge(s["tail_rstd"], n + 1)
            if n >= 3:
                v.wait_ge(s["tail_z"], n - 2)
            nc.vector.tensor_tensor(yn[0:m, n % 3, 0:k, :], yb[n % 3][0:m, 0:k * CH].rearrange("p (j n) -> p j n", j=k),
                                    rstd[0:m, n % 3, 0:k].unsqueeze(2).broadcast_to([m, k, CH]),
                                    ALU.mult).then_inc(s["tail_norm"], 1)

        def tail_stats(n, base):
            l, c, sizes = tail[n]
            v.wait_ge(s["tail_y"], n + 1)
            stats(yb[n % 3], n % 3, sizes, s["tail_var"], base)
            return base + len(sizes) + 2

        base = tail_stats(0, base)
        stream_stats("C", 2, STEPS, base)
        v.wait_ge(q["z"]["A"], STEPS)
        tail_norm(0)
        base = tail_stats(1, base + 6)
        norm("C", 2, STEPS)
        pending = 1
        for kind, n in tail_schedule[2:]:
            if kind == "conv":
                base = tail_stats(n, base)
                if pending is not None:
                    if pending < 3:
                        v.wait_ge(q["z"][kinds[pending]], STEPS)
                    tail_norm(pending)
                pending = n
            elif kind == "turn" and pending == n:
                tail_norm(n)
                pending = None

    return dict(sync=sync_prog, pool=pool_prog, act=act_prog, pe=pe_prog, dve=dve_prog,
                tail=len(tail), s=s, gb=gb)


def conv_inputs(x, inputs):
    pad = np.zeros((BATCH, (SLOTS0 + 1) * STRIDE0), x.dtype)
    pad[:, :x.shape[1]] = x
    blocks = pad.reshape(BATCH, SLOTS0 + 1, STRIDE0)
    stream = np.concatenate([blocks[:, :-1], blocks[:, 1:]], axis=2).reshape(STREAM0, TAPS0)
    stream = np.concatenate([np.zeros((1, TAPS0), x.dtype), stream[:-1]])
    windows = stream.T.reshape(TAPS0, GROUPS, FOLD).transpose(1, 0, 2).reshape(WROWS, FOLD)
    windows = np.concatenate([windows, np.zeros((P - WROWS, FOLD), x.dtype)])
    w0 = inputs["L0_tok_conv_w0"][:, 0, :]
    pick = np.zeros((P, 2 * P - GROUPS), np.float16)
    pick[np.arange(WROWS), P - GROUPS + np.arange(WROWS) // TAPS0] = 1
    return {
        "windows": windows,
        "w0rep": np.tile(w0, (1, GROUPS)),
        "w0rows": np.tile(w0.T, (2, 1)),
        "g0rows": np.broadcast_to(inputs["L0_tok_ln_g0"], (2 * TAPS0, CH)),
        "conv_w": np.concatenate([inputs[f"L0_tok_conv_w{l}"].transpose(1, 2, 0) for l in range(1, 7)], axis=1),
        "conv_gb": np.stack([np.stack([inputs[f"L0_tok_ln_g{l}"], inputs[f"L0_tok_ln_b{l}"]], -1)
                             for l in range(7)], axis=1),
        "blk": np.kron(np.eye(GROUPS), np.ones((TAPS0, TAPS0))).astype(np.float32),
        "pick": pick,
        "back": np.concatenate([pick[:, P - GROUPS - GROUPS * c:2 * P - GROUPS - GROUPS * c][0:WROWS].T
                                for c in range(PIECES)], axis=1),
        "cen": (np.eye(P) - 1.0 / P).astype(np.float32),
        "ident_d": np.eye(P, dtype=np.float32),
    }


D = 192
HD = 96
NTOK = BATCH * 12
TT = NTOK // P
AT = 8
HB = HD + 1
HEADS, DH = 12, 16
EXPERTS = 10
HID = 768
HT = HID // P
HALF = NTOK // 2
REST = D - P
SOFT_SCALE = DH ** -0.5
PI_HALF = float(np.float32(np.pi / 2))


def build_rest(nc, sb, banks, sem, t, act6, conv):
    sems = {}

    shared = {}

    def share(family, tags, signals):
        for name, n in signals.items():
            for k, tag in enumerate(tags):
                shared[tag + name] = (family + name, n * k)

    share("norm", ["f", "ln0", "ln2", "ln3", "ln4"], {"_st": TT, "_var": TT, "_vare": 2, "_std": 2, "_ln": TT})
    for k, tag in enumerate(("tok", "l0p", "l1p")):
        shared["h_add" + tag] = ("h_add", TT * k)
    share("turn", ["a0", "a1", "f0", "a2", "f1"], {"_T": 3, "_xT": 3})
    share("project", ["tok", "l0p", "l1p"], {"_mm": TT})
    share("att", ["l0", "l1"], {"_qk": 8, "_qkd": 8, "_v": AT, "_vd": AT, "_blk": 2 * AT, "_s": 4 * AT, "_pv": 2 * AT,
                         "_o": AT, "_oT": 4, "_aT": 4})
    for n, name in enumerate(("gate_t", "", "", "", "gate_sin", "gate_tanh")):
        shared[name] = ("gate_act", n)
    for n, name in enumerate(("gate_arg", "gate_int", "gate_int2")):
        shared[name] = ("gate_dve", n)
    for u in range(6):
        shared[f"dn2_in{u}"] = (f"d_in{u % 2}", 16 * (EXPERTS // 2 + u // 2))
        if u not in (2, 3):
            shared[f"up2_in{u}"] = (f"gu_in{u % 2}", 16 * (EXPERTS // 2 + u // 4))
    shared["vones"], shared["gdiag"] = ("const_set", 1), ("top", 2 * TT)
    shared["out_done"] = ("mask_in", 32)
    shared["weighed"] = ("cwc", EXPERTS // 2)
    shared["glog"], shared["gsub"], shared["gexp"] = ("route", 1), ("logit", 1), ("score_exp", 1)
    shared["x_lo2"] = ("x_lo", 1)

    def S(name):
        name = shared.get(name, (name, 0))[0]
        if name not in sems:
            sems[name] = sem("r_" + name)
        return sems[name]

    def upto(name, n):
        return S(name), shared.get(name, (name, 0))[1] + n

    ident = t["ident"]
    small = t["small_sb"]
    hm = small["headmask"]
    h = sb("h", [P, TT, D], F32)
    x_tok = sb("x_tok", [P, TT, 2 * P], F32)
    xT = sb("xT", [P, 2, NTOK], F32)
    xT_att = xT[0:HD, :, :]
    st = sb("r_st", [P, TT, 6], F32)
    mv = sb("r_mv", [P, TT, 2], F32)
    sdv = sb("r_sd", [P, TT], F32)
    var = sb("r_var", [P, TT], F32)
    minus_half = sb("minus_half", [P, TT], F32)
    eps = sb("r_eps", [P, 1], F32)
    gu_raw = sb("gu_raw", [P, 2, 2, 2 * HID], F32)
    d_raw = sb("d_raw", [P, 2, HT, D], F32)
    gu_hi = sb("gu_hi", [P, 2, 2 * HID], F16)
    gu_lo = sb("gu_lo", [P, 2, 2 * HID], F16)
    gu_mix = sb("gu_mix", [P, 2, 2 * HID], F16)
    d_hi = sb("d_hi", [P, 2, HT, D], F16)
    d_lo = sb("d_lo", [P, 2, HT, D], F16)
    x_lo = sb("x_lo", [P, 2, NTOK], F16)
    x_hi = xT[:, :, :].bitcast(BF16).rearrange("p a (n two) -> p a n two", two=2)[:, :, :, 1]
    logit = sb("logit", [P, TT, 8], F32)
    score = sb("score", [P, TT, 8], F32)
    top8 = sb("top8", [P, TT, 8], F32)
    topi = sb("topi", [P, TT, 8], U32)
    topf = sb("topf", [P, TT, 8], F32)
    r1 = [sb(f"r1_{i}", [P, TT], F32) for i in range(3)]
    mk = [sb(f"mk{i}", [P, TT, 8], F32) for i in range(2)]
    cw = sb("cw", [P, EXPERTS, TT], F32)
    cwc = sb("cwc", [P, 2, TT], F32)
    attn_ctx = ExitStack()
    attn_sb = lambda n, sh, dt: attn_ctx.enter_context(nc.sbuf_tensor(n, sh, dt))
    x2_tok = attn_sb("x2_tok", [P, TT, D], F32)
    x2T = attn_sb("x2T", [HB, 2, NTOK], F32)
    xn_f = attn_sb("xn_f", [P, TT, CH], F32)
    nT = attn_sb("nT", [P, NTOK], F32)
    qk = attn_sb("qk", [HD + AT, 4, NTOK], F32)
    qe = attn_sb("qe", [HD, 2, HALF], F32)
    qr = attn_sb("qr", [HD, 2, HALF], F32)
    hidT = attn_sb("hidT", [P, NTOK], F32)
    par = attn_sb("par", [HD, AT * HEADS * 5], F32)
    gv = [attn_sb(f"gv{i}", [HD, AT * HEADS], F32) for i in range(5)]
    tempc = attn_sb("tempc", [HD, 1], F32)
    vg = attn_sb("vg", [HD, AT, HEADS, DH + 1], F32)
    blkd = attn_sb("blkd", [HD + AT, 2, 6, HD], F32)
    pr = attn_sb("pr", [HD, 2, 6, HD], F32)
    pt = attn_sb("pt", [HD, 2, 6, HD], F32)
    mxs = attn_sb("mxs", [HD, 2, 6], F32)
    oa = attn_sb("oa", [HD, AT, HEADS, DH], F32)
    osq = attn_sb("osq", [HD, AT, HEADS, DH], F32)
    rden = attn_sb("rden", [HD, AT * HEADS], F32)
    ovar = attn_sb("ovar", [HD, AT * HEADS], F32)
    vmean = attn_sb("vmean", [HB, 2, HEADS], F32)
    attn_ctx.close()
    hid = sb("hid", [P, 2, HT, HALF], F32)
    hid_hi = hid[:, :, :, :].bitcast(BF16).rearrange("p a j (n two) -> p a j n two", two=2)[:, :, :, :, 1]
    hid_lo = sb("hid_lo", [P, 2, HT, HALF], F16)
    sg = sb("sg", [P, 2, HALF], F32)
    hc = sb("hc", [P, HT, 12, BATCH], F32)
    hc_hi = hc[:, :, :, :].bitcast(BF16).rearrange("p j s (n two) -> p j s n two", two=2)[:, :, :, :, 1]
    hc_lo = sb("hc_lo", [P, HT, 12, BATCH], F16)
    yT = sb("yT", [HD, 2, NTOK], F32)
    yd = sb("yd", [HD, 2, 2, 6, BATCH], F32)
    gl = sb("gl", [BATCH, 6, 2], F32)
    gkeep = sb("gkeep", [BATCH, 6, 2], F32)
    gr = sb("gr", [BATCH, 6], F32)
    gdiag = sb("gdiag", [BATCH, 2, 6, BATCH], F32)
    outb = x_tok
    spare = hid[:, 1, :, :].rearrange("p j n -> p (j n)").bitcast(F16).rearrange("p (k j n) -> p k j n", k=4, j=HT)
    dn2_hi = [d_hi[:, 0], d_hi[:, 1], spare[:, 0], spare[:, 1], d_hi[:, 0], d_hi[:, 1]]
    dn2_lo = [d_lo[:, 0], d_lo[:, 1], spare[:, 2], spare[:, 3], d_lo[:, 0], d_lo[:, 1]]
    up2_at = [(u % 2, HID * (u // 2 % 2)) for u in range(6)]

    UP = [(0, (6, 1, 6), None), (1, (0, 1, 2), (0, 1, 2)), (2, (2, 1, 2), (2, 1, 2)), (3, (4, 1, 2), (4, 1, 2)),
          (4, (0, 2, 3), (6, 2, 3)), (5, (1, 2, 3), (7, 2, 3))]
    DOWN = [(0, None, None, None), (1, (0, 2, 3), 0, (0, 2, 3)), (2, (1, 2, 3), 0, (1, 2, 3)),
            (3, (6, 1, 2), 1, (0, 1, 2)), (4, (8, 1, 2), 1, (2, 1, 2)), (5, (10, 1, 2), 1, (4, 1, 2))]

    ORDER = [("up", 0), ("up", 1), ("up", 2), ("gates", 0), ("down", 0), ("up", 3), ("up", 4), ("down", 1), ("up", 5),
             ("down", 2), ("down", 3), ("down", 4), ("down", 5)]
    UP_BANKS = (0, 1, 4, 5)
    HIDDEN_OF = (1, 4, 4, 6, 6, 6)

    def rng(r):
        return slice(r[0], r[0] + r[1] * (r[2] - 1) + 1, r[1])

    def sync_prog(sp):
        def load(dst, src, sig):
            sp.dma_start(dst, src).then_inc(sig, 16)

        load(gu_raw[:, 0, :, :], t["gu"][0], S("gu_in0"))
        load(d_raw[:, 0, :, :], t["dn"][0], S("d_in0"))
        load(gu_raw[:, 1, :, :], t["gu"][1], S("gu_in1"))
        load(d_raw[:, 1, :, :], t["dn"][1], S("d_in1"))
        with sp.Fori(0, EXPERTS // 2 - 1) as i:
            for d in range(2):
                sp.wait_ge(*upto(f"gu_low{d}", 4 * i + 4))
                load(gu_raw[:, d, :, :], t["gu_flat"][bass.ds((2 * i + (2 + d)) * P, P), :], S(f"gu_in{d}"))
                sp.wait_ge(*upto(f"d_low{d}", 2 * i + 2))
                load(d_raw[:, d, :, :], t["dn_flat"][bass.ds((2 * i + (2 + d)) * P, P), :], S(f"d_in{d}"))

        def load_up2(u):
            d, c = up2_at[u]
            load(gu_raw[:, d, :, c:c + HID], t["up2"][u], S(f"up2_in{u}"))

        for d in range(2):
            sp.wait_ge(*upto(f"gu_low{d}", 4 * (EXPERTS // 2)))
            load_up2(d)
            load_up2(d + 2)
            sp.wait_ge(*upto(f"d_low{d}", 2 * (EXPERTS // 2)))
            load(d_raw[:, d, :, :], t["dn2"][d], S(f"dn2_in{d}"))
        def load_dn2(u):
            sp.wait_ge(*upto("dn2_wlow", u - 1))
            load(d_raw[:, u % 2, :, :], t["dn2"][u], S(f"dn2_in{u}"))

        load_dn2(2)
        sp.wait_ge(*upto("added", 6 * EXPERTS))
        load(qk[HD:HD + AT, 0:2, :], t["row_of"], S("mask_in"))
        load(blkd[HD:HD + AT, :, :, :], t["apart"], S("mask_in"))
        load_dn2(3)
        for u in (4, 5):
            sp.wait_ge(*upto("up2_wlow", 2 * (u - 3)))
            load_up2(u)
        load_dn2(4)
        load_dn2(5)
        sp.wait_ge(*upto("out_ready", TT))
        sp.dma_start(t["out"], outb[:, :, 0:D]).then_inc(S("out_done"), 16)
        sp.wait_ge(*upto("out_done", 16))

    def pe_prog(pe):
        halves_rows = ((0, HB), (1, HD))

        def mm(out, a, b, start=True, stop=True):
            return nc.tensor.matmul(out, a, b, start=start, stop=stop)

        warm = ident[:, :].bitcast(BF16)

        def keep_warm(n):
            for _ in range(n):
                mm(banks[7][:, 0:2 * P], warm[:, 0:P], warm)

        def to_channels(tag, src, wait):
            for j in range(12):
                hf, tt = j // 6, j % 6
                pe.wait_ge(*upto(wait, tt + 1))
                last = nc.tensor.transpose(banks[j // 4][0:HD, (j % 4) * P:(j % 4 + 1) * P],
                                           src[:, tt, hf * HD:(hf + 1) * HD], ident[:, :])
                if j < TT:
                    keep_warm(1)
                if j % 4 == 3:
                    last.then_inc(S(tag + "_T"), 1)
            keep_warm(4)

        def to_channels_packed(tag, src, wait):
            for j in range(12):
                k, tt = j // 6, j % 6
                pe.wait_ge(*upto(wait, tt + 1))
                last = nc.tensor.transpose(banks[j // 4][:, (j % 4) * P:(j % 4 + 1) * P],
                                           src[:, tt, k * P:(k + 1) * P], ident[:, :])
                if j < TT:
                    keep_warm(1)
                if j % 4 == 3:
                    last.then_inc(S(tag + "_T"), 1)
            keep_warm(4)

        def split_products(hi, lo, mix, x):
            xh, xl = x(x_hi), x(x_lo[:, :, :])
            return ((hi, xh[:, 0]), (hi, xl[:, 0]), (lo, xh[:, 0]), (mix, xh[:, 1]), (mix[0:REST], xl[0:REST, 1]))

        def proj192(tag, lhs, rhs):
            for tt in range(TT):
                out = banks[4 + tt // 2][:, (tt % 2) * D:(tt % 2 + 1) * D]
                parts = lhs(tt)
                for i, (a, b) in enumerate(zip(parts, rhs)):
                    last = mm(out, a, b, start=(i == 0), stop=(i == len(rhs) - 1))
                last.then_inc(S(tag + "_mm"), 1)

        pe.wait_ge(conv["s"]["tail_act"], conv["tail"])
        pe.wait_ge(t["small_in"], 16 * len(t["small"]))
        pe.wait_ge(*upto("const_set", 1))
        for tt in range(TT):
            nc.tensor.transpose(banks[tt // 4][:, (tt % 4) * P:(tt % 4 + 1) * P], act6[:, tt * P:(tt + 1) * P],
                                ident[:, :]).then_inc(S("f_T"), 1)
        keep_warm(20)
        for tt in range(TT):
            pe.wait_ge(*upto("f_ln", tt + 1))
            nc.tensor.transpose(banks[2 + tt // 4][:, (tt % 4) * P:(tt % 4 + 1) * P], xn_f[:, tt, :],
                                ident[:, :]).then_inc(S("f_T2"), 1)
        pe.wait_ge(*upto("f_nT", 2))
        proj192("tok", lambda tt: [nT[:, tt * P:(tt + 1) * P]], [small["proj_w"][:, :]])

        keep_warm(20)
        to_channels("a0", x_tok, "ln0_ln")
        keep_warm(10)
        pe.wait_ge(*upto("a0_xT", 3))
        to_channels("a1", x2_tok, "ln1_ln")
        for hf in range(2):
            for kt in range(2):
                last = mm(banks[3 + hf][:, 0:HALF], small["Wb1"][:, kt, :], xT_att[:, kt, hf * HALF:(hf + 1) * HALF],
                          kt == 0, kt == 1)
            last.then_inc(S("hid_mm"), 1)
        pe.wait_ge(*upto("hid_act", 2))
        for a in range(AT):
            last = mm(banks[6][0:HD, a * 60:(a + 1) * 60], hidT[:, a * HD:(a + 1) * HD], small["Wb2"][:, :])
        last.then_inc(S("par_mm"), 1)
        pe.wait_ge(*upto("a1_xT", 3))

        def qkv(tag, w, src):
            for m in range(4):
                for hf in range(2):
                    n = 2 * m + hf
                    if n >= 2:
                        pe.wait_ge(*upto(tag + "_qkd", n - 1))
                    for kt in range(2):
                        last = mm(banks[n % 2][0:HD, 0:HALF], w[0:HD, kt, m * HD:(m + 1) * HD],
                                  src[0:HD, kt, hf * HALF:(hf + 1) * HALF], kt == 0, kt == 1)
                    last.then_inc(S(tag + "_qk"), 1)

        def vrows(tag, w, src, tiles=range(AT)):
            for a in tiles:
                if a >= 4:
                    pe.wait_ge(*upto(tag + "_vd", a - 3))
                out = banks[2 + a % 4][0:HD, 0:D]
                for kt, rows in halves_rows:
                    last = mm(out, src[0:rows, kt, a * HD:(a + 1) * HD], w[0:rows, kt, 2 * D:3 * D], kt == 0, kt == 1)
                last.then_inc(S(tag + "_v"), 1)

        pe.wait_ge(*upto("l0_wv", 1))
        pe.wait_ge(*upto("half_set", 3))
        vrows("l0", small["Wqkv"], x2T, range(4))
        qkv("l0", small["Wqkv"], x2T)
        vrows("l0", small["Wqkv"], x2T, range(4, AT))
        pe.wait_ge(*upto("l0_vd", AT))
        for n in range(2 * AT + 1):
            if n < 2 * AT:
                a, hf = n // 2, n % 2
                pe.wait_ge(*upto("l0_blk", n + 1))
                if n >= 2:
                    pe.wait_ge(*upto("l0_p", 2 * (n - 1)))
                for g in range(2):
                    mm(banks[2 * (n % 2) + g][0:HD, 0:3 * HD], qk[0:HD, 2 + hf, a * HD:(a + 1) * HD],
                       blkd[0:HD, n % 2, 3 * g:3 * g + 3, :]).then_inc(S("l0_s"), 1)
            if n >= 1:
                m = n - 1
                a, hf = m // 2, m % 2
                pe.wait_ge(*upto("l0_p", 2 * (m + 1)))
                if a >= 2 and hf == 0:
                    pe.wait_ge(*upto("l0_o", a - 1))
                for hd in range(6):
                    c = (hf * 6 + hd) * (DH + 1)
                    last = mm(banks[4 + a % 2][0:HD, c:c + DH + 1], pr[:, m % 2, hd, :], vg[:, a, hf * 6 + hd, :])
                last.then_inc(S("l0_pv"), 1)

        def back(tag):
            for hf in range(2):
                for a in range(AT):
                    last = nc.tensor.transpose(banks[2 * hf + a // 4][0:HD, (a % 4) * HD:(a % 4 + 1) * HD],
                                               oa[:, a, 6 * hf:6 * hf + 6, :], ident[0:HD, 0:HD])
                    if a % 4 == 3:
                        last.then_inc(S(tag), 1)

        keep_warm(10)
        pe.wait_ge(*upto("l0_oln", 4))
        back("l0_oT")
        pe.wait_ge(*upto("l0_aT", 4))
        proj192("l0p", lambda tt: [xT[0:rows, kt, tt * P:(tt + 1) * P] for kt, rows in halves_rows],
                [small["Wproj"][0:rows, kt, :] for kt, rows in halves_rows])

        keep_warm(20)
        to_channels_packed("f0", x_tok, "ln2_ln")
        pe.wait_ge(*upto("f0_xT", 3))
        for tt in range(TT):
            for kt, rows in ((0, P), (1, REST)):
                last = mm(banks[7][:, tt * 8:tt * 8 + 8], xT[0:rows, kt, tt * P:(tt + 1) * P],
                          small["gate_w"][0:rows, kt, :], kt == 0, kt == 1)
        last.then_inc(S("route"), 1)
        pe.wait_ge(*upto("x_lo", 1))

        def gate_up_unit(i, d, hb, first):
            for j in range(HT):
                cnt = 24 * i + (12 * d + 6 * hb + j)
                if not (first and cnt_is_small(d, hb, j)):
                    pe.wait_ge(*upto("hid_w", cnt - 1))
                for g in range(2):
                    m0 = g * HID + j * P
                    parts = split_products(*[w[:, d, m0:m0 + P] for w in (gu_hi, gu_lo, gu_mix)],
                                           lambda x: x[:, :, hb * HALF:(hb + 1) * HALF])
                    for n, (w, x) in enumerate(parts):
                        last = mm(banks[2 * (j % 2) + g][:, 0:HALF], w, x, n == 0, n == 4)
                    last.then_inc(S("gu_mm"), 1)

        def cnt_is_small(d, hb, j):
            return 12 * d + 6 * hb + j < 2

        def down_unit(i, d, hb, first):
            unit = 4 * i + (2 * d + hb)
            pe.wait_ge(*upto("hid_low", 6 * unit + 6))
            if not (first and 2 * d + hb < 2):
                pe.wait_ge(*upto("added", unit * 3 - 3))
            if first and d == 0 and hb == 1:
                pe.wait_ge(*upto("route_read", 1))
            for tt in range(3):
                out = banks[4 + 2 * hb + tt // 2][:, (tt % 2) * D:(tt % 2 + 1) * D]
                n = 0
                for j in range(HT):
                    hs = hid_hi[:, hb, j, tt * P:(tt + 1) * P]
                    hl = hid_lo[:, hb, j, tt * P:(tt + 1) * P]
                    for w, x in ((d_hi, hs), (d_hi, hl), (d_lo, hs)):
                        last = mm(out, x, w[:, d, j, :], n == 0, n == 3 * HT - 1)
                        n += 1
                last.then_inc(S("down"), 1)

        def moe_iter(i, first):
            for d in range(2):
                pe.wait_ge(*upto(f"gu_low{d}", 4 * i + 4))
                gate_up_unit(i, d, 0, first)
                if d == 1:
                    down_unit(i, 0, 1, first)
                elif not first:
                    down_unit(i - 1, 1, 1, False)
                gate_up_unit(i, d, 1, first)
                pe.wait_ge(*upto(f"d_low{d}", 2 * i + 2))
                down_unit(i, d, 0, first)

        moe_iter(0, True)
        with pe.Fori(1, EXPERTS // 2) as i:
            moe_iter(i, False)
        down_unit(EXPERTS // 2 - 1, 1, 1, False)

        pe.wait_ge(*upto("hid_w", HT * 2 * EXPERTS))
        pe.wait_ge(*upto("added", 6 * EXPERTS))
        keep_warm(20)
        pe.wait_ge(*upto("half_set", 4))
        to_channels("a2", x_tok, "ln3_ln")
        pe.wait_ge(*upto("a2_xT", 3))
        qkv("l1", small["w_qkv"], xT_att)
        pe.wait_ge(*upto("l1_qkd", 8))
        vrows("l1", small["w_qkv"], xT)
        pe.wait_ge(*upto("l1_vd", AT))
        pe.wait_ge(*upto("mask_in", 32))
        for n in range(2 * AT + 2):
            if n < 2 * AT:
                a, hf = n // 2, n % 2
                pe.wait_ge(*upto("l1_blk", n + 1))
                if n >= 2:
                    pe.wait_ge(*upto("l1_sub", 2 * (n - 1)))
                for g in range(2):
                    out = banks[2 * (n % 2) + g][0:HD, 0:3 * HD]
                    mm(out, qk[:, hf, a * HD:(a + 1) * HD],
                       blkd[:, n % 2, 3 * g:3 * g + 3, :]).then_inc(S("l1_s"), 1)
            if 1 <= n <= 2 * AT:
                m = n - 1
                pe.wait_ge(*upto("l1_exp", m + 1))
                for g in range(2):
                    if m >= 1:
                        pe.wait_ge(*upto("l1_pt", 2 * (m - 1) + g + 1))
                    for k in range(3):
                        last = nc.tensor.transpose(banks[6 + g][0:HD, k * HD:(k + 1) * HD], pr[:, m % 2, 3 * g + k, :],
                                                   ident[0:HD, 0:HD])
                    last.then_inc(S("l1_pT"), 1)
            if n >= 2:
                m = n - 2
                a, hf = m // 2, m % 2
                pe.wait_ge(*upto("l1_pt", 2 * (m + 1)))
                if a >= 2 and hf == 0:
                    pe.wait_ge(*upto("l1_o", a - 1))
                for hd in range(6):
                    c = (hf * 6 + hd) * (DH + 1)
                    last = mm(banks[4 + a % 2][0:HD, c:c + DH + 1], pt[:, m % 2, hd, :], vg[:, a, hf * 6 + hd, :])
                last.then_inc(S("l1_pv"), 1)
        pe.wait_ge(*upto("l1_o", AT))
        back("l1_oT")
        pe.wait_ge(*upto("l1_aT", 4))
        proj192("l1p", lambda tt: [xT[0:rows, kt, tt * P:(tt + 1) * P] for kt, rows in halves_rows],
                [small["w_proj"][0:rows, kt, :] for kt, rows in halves_rows])

        keep_warm(20)
        to_channels_packed("f1", x_tok, "ln4_ln")
        pe.wait_ge(*upto("f1_xT", 3))
        for i in range(6):
            for kt, rows in ((0, P), (1, REST)):
                last = mm(banks[7][0:BATCH, 2 * i:2 * i + 2], xT[0:rows, kt, i::12], small["G_W"][0:rows, kt, i, :],
                          kt == 0, kt == 1)
        last.then_inc(S("glog"), 1)
        pe.wait_ge(*upto("x_lo2", 1))

        def up_unit(u, cols, slots):
            d, c = up2_at[u]
            size = cols[2] * BATCH
            pe.wait_ge(*upto("up2_wlow", 2 * u + 2))
            for j in range(HT):
                cnt = 6 * u + j
                if cnt >= 4:
                    pe.wait_ge(*upto("up2_act", cnt - 3))
                m0 = c + j * P
                parts = split_products(*[w[:, d, m0:m0 + P] for w in (gu_hi, gu_lo, gu_mix)],
                                       lambda x: x.rearrange("p k (b r) -> p k r b", r=12)[:, :, rng(cols), :])
                for n, (w, x) in enumerate(parts):
                    last = mm(banks[UP_BANKS[cnt % 4]][:, 0:size], w, x, n == 0, n == 4)
                last.then_inc(S("up2_mm"), 1)

        def spread_shares():
            pe.wait_ge(*upto("gdiag", 1))
            for k in range(2):
                mm(banks[6 + k][0:HD, 0:HALF], small["ones"][:, :], gdiag[:, k, :, :]).then_inc(S("gall"), 1)

        def down_unit2(u, slots, direction, classes):
            pe.wait_ge(*upto("dn2_wlow", u + 1))
            pe.wait_ge(*upto("up2_low", HT * HIDDEN_OF[u]))
            size = HALF if slots is None else slots[2] * BATCH
            for m in range(2):
                cnt = 2 * u + m
                if cnt >= 2:
                    pe.wait_ge(*upto("dn2_read", cnt - 1))
                n = 0
                for j in range(HT):
                    if slots is None:
                        a, b = hid_hi[:, 0, j, :], hid_lo[:, 0, j, :]
                    else:
                        a, b = hc_hi[:, j, rng(slots), :], hc_lo[:, j, rng(slots), :]
                    for w, x in ((dn2_hi[u], a), (dn2_hi[u], b), (dn2_lo[u], a)):
                        last = mm(banks[2 + cnt % 2][0:HD, 0:size], w[:, j, m * HD:(m + 1) * HD], x, n == 0,
                                  n == 3 * HT - 1)
                        n += 1
                last.then_inc(S("dn2_mm"), 1)

        for kind, u in ORDER:
            if kind == "up":
                up_unit(*UP[u])
            elif kind == "down":
                down_unit2(*DOWN[u])
            else:
                spread_shares()
        pe.wait_ge(*upto("yT", 1))
        for tt in range(TT):
            for kt in range(2):
                last = nc.tensor.transpose(banks[4 + tt // 2][:, (tt % 2) * D + kt * HD:(tt % 2) * D + (kt + 1) * HD],
                                           yT[:, kt, tt * P:(tt + 1) * P], ident[0:HD, 0:HD])
            last.then_inc(S("y_tok"), 1)

    def act_prog(a):
        act = nc.scalar.activation

        def evac_T(tag, dst):
            flat = dst.rearrange("p k n -> p (k n)")
            rows = dst.shape[0]
            for c in range(3):
                a.wait_ge(*upto(tag + "_T", c + 1))
                act(flat[:, c * 512:(c + 1) * 512], banks[c][0:rows, :], ACT.Copy).then_inc(S(tag + "_xT"), 1)

        def high_and_scaled(high, raw):
            act(high, raw, ACT.Copy, scale=WS)
            return act(raw, raw, ACT.Copy, scale=WS)

        def high_only(d, c, k):
            return act((gu_mix if k else gu_hi)[:, d, c:c + HID], gu_raw[:, d, k, c:c + HID], ACT.Copy, scale=WS)

        def high_part(d, c, k):
            return high_and_scaled((gu_mix if k else gu_hi)[:, d, c:c + HID], gu_raw[:, d, k, c:c + HID])

        evac_T("a0", xT_att)
        for hf in range(2):
            a.wait_ge(*upto("hid_mm", hf + 1))
            act(hidT[:, hf * HALF:(hf + 1) * HALF], banks[3 + hf][:, 0:HALF], ACT.Silu).then_inc(S("hid_act"), 1)
        a.wait_ge(*upto("par_sb", 1))
        pv = par[:, :].rearrange("p (n f) -> p n f", f=5)
        act(gv[0][:, :], pv[:, :, 0], ACT.Tanh, scale=0.5).then_inc(S("gate_t"), 1)
        act(gv[1][:, :], pv[:, :, 1], ACT.Tanh).then_inc(S("gate_t"), 1)
        act(gv[2][:, :], pv[:, :, 2], ACT.Tanh, scale=0.5).then_inc(S("gate_t"), 1)
        act(gv[3][:, :], pv[:, :, 3], ACT.Tanh).then_inc(S("gate_t"), 1)
        a.wait_ge(*upto("gate_arg", 1))
        act(gv[1][:, :], gv[1][:, :], ACT.Sin).then_inc(S("gate_sin"), 1)
        a.wait_ge(*upto("gate_int", 1))
        act(gv[0][:, :], gv[0][:, :], ACT.Tanh).then_inc(S("gate_tanh"), 1)
        a.wait_ge(*upto("gate_int2", 1))
        act(gv[0][:, :], gv[0][:, :], ACT.Tanh, scale=0.5).then_inc(S("gate_tanh"), 1)
        for n in range(8):
            a.wait_ge(*upto("l0_qk", n + 1))
            if n >= 2:
                a.wait_ge(*upto("l0_qf", n - 1))
            act(qe[:, n % 2, :], banks[n % 2][0:HD, 0:HALF], ACT.Exp,
                bias=small["bqkv"][:, n // 2:n // 2 + 1]).then_inc(S("l0_qexp"), 1)
        a.wait_ge(*upto("gu_in0", 16))
        for k in range(4):
            high_part(0, k % 2 * HID, k // 2).then_inc(S("gu_high0"), 1)
        a.wait_ge(*upto("d_in0", 16))
        for k in range(2):
            high_and_scaled(d_hi[:, 0, 3 * k:3 * k + 3, :],
                            d_raw[:, 0, 3 * k:3 * k + 3, :]).then_inc(S("d_high0"), 1)
        for c in range(4):
            cols = slice(2 * c * HEADS, 2 * (c + 1) * HEADS)
            a.wait_ge(*upto("ovar", c + 1))
            act(ovar[:, cols], ovar[:, cols], ACT.Sqrt, bias=eps[0:HD, :], scale=1.0 / DH).then_inc(S("ostd"), 1)
        evac_T("f0", xT[:, :, :])
        a.wait_ge(*upto("logit", 1))
        act(score[:, :, :], logit[:, :, :], ACT.Exp).then_inc(S("score_exp"), 1)

        def unit(i, d, hb, splits):
            for j in range(HT):
                cnt = 24 * i + (12 * d + 6 * hb + j)
                a.wait_ge(*upto("gu_mm", 2 * cnt + 1))
                if not (type(i) is int and cnt < 2):
                    a.wait_ge(*upto("hid_w", cnt - 1))
                act(sg[:, j % 2, :], banks[2 * (j % 2)][:, 0:HALF], ACT.Silu, scale=1.0 / WS).then_inc(S("silu"), 1)
                if j in splits:
                    splits[j]()

        def expert(i, d, nxt):
            unit(i, d, 0, {1 + k: (lambda k=k: nxt("gu", k)) for k in range(4)} if nxt else {})
            unit(i, d, 1, {1 + 2 * k: (lambda k=k: nxt("d", k)) for k in range(2)} if nxt else {})

        def next_expert(i, d):
            def part(kind, k):
                if k == 0:
                    a.wait_ge(*upto(f"{kind}_in{d}", 16 * i + 16))
                if kind == "gu":
                    high_part(d, k % 2 * HID, k // 2).then_inc(S(f"gu_high{d}"), 1)
                else:
                    if k == 0 and not (type(i) is int and i == 0):
                        a.wait_ge(*upto("down", 12 * i + (6 * d - 6)))
                    high_and_scaled(d_hi[:, d, 3 * k:3 * k + 3, :],
                                    d_raw[:, d, 3 * k:3 * k + 3, :]).then_inc(S(f"d_high{d}"), 1)
            return part

        def up2_unit0(kind, k):
            if kind == "gu" and k < 2:
                if k == 0:
                    a.wait_ge(*upto("up2_in0", 16))
                up2_high(0, k)
            elif kind == "d" and k == 0:
                a.wait_ge(*upto("down", 6 * EXPERTS - 6))
                dn2_high(0)

        def up2_high(u, k):
            d, c = up2_at[u]
            part = high_part if u < 4 else high_only
            part(d, c, k).then_inc(S("up2_whigh"), 1)

        def dn2_high(u):
            a.wait_ge(*upto(f"dn2_in{u}", 16))
            if u < 2:
                high_and_scaled(dn2_hi[u], d_raw[:, u % 2, :, :]).then_inc(S("dn2_whigh"), 1)
            else:
                act(dn2_hi[u], d_raw[:, u % 2, :, :], ACT.Copy, scale=WS).then_inc(S("dn2_whigh"), 1)

        last_pair = EXPERTS // 2 - 1
        expert(0, 0, next_expert(0, 1))
        expert(0, 1, next_expert(1, 0))
        with a.Fori(1, last_pair) as i:
            expert(i, 0, next_expert(i, 1))
            expert(i, 1, next_expert(i + 1, 0))
        expert(last_pair, 0, next_expert(last_pair, 1))
        expert(last_pair, 1, up2_unit0)

        evac_T("a2", xT_att)
        for u in (1, 2, 3):
            a.wait_ge(*upto(f"up2_in{u}", 16))
            for k in range(2):
                up2_high(u, k)
            if u == 1:
                a.wait_ge(*upto("down", 6 * EXPERTS))
                dn2_high(1)
        for n in range(2 * AT):
            a.wait_ge(*upto("l1_sub", 2 * n + 2))
            if n >= 2:
                a.wait_ge(*upto("l1_pT", 2 * (n - 1)))
            act(pr[:, n % 2, :, :], pr[:, n % 2, :, :], ACT.Exp, scale=SOFT_SCALE).then_inc(S("l1_exp"), 1)
            for g in range(2):
                a.wait_ge(*upto("l1_pT", 2 * n + g + 1))
                if n >= 2:
                    a.wait_ge(*upto("l1_pv", n - 1))
                act(pt[:, n % 2, 3 * g:3 * g + 3, :], banks[6 + g][0:HD, 0:3 * HD].rearrange("p (k n) -> p k n", k=3),
                    ACT.Copy).then_inc(S("l1_pt"), 1)
        evac_T("f1", xT[:, :, :])
        a.wait_ge(*upto("gsub", 1))
        act(gl[:, :, :], gl[:, :, :], ACT.Exp).then_inc(S("gexp"), 1)
        for u, cols, slots in UP:
            size = cols[2] * BATCH
            for j in range(HT):
                cnt = 6 * u + j
                a.wait_ge(*upto("up2_mm", cnt + 1))
                src = banks[UP_BANKS[cnt % 4]][:, 0:size].rearrange("p (r b) -> p r b", b=BATCH)
                dst = (hid[:, 0, j, :].rearrange("p (r b) -> p r b", b=BATCH) if slots is None
                       else hc[:, j, rng(slots), :])
                act(dst, src, ACT.Gelu, bias=small["b1"][:, u, j:j + 1], scale=1.0 / WS).then_inc(S("up2_act"), 1)
            if u < 2:
                a.wait_ge(*upto(f"up2_in{u + 4}", 16))
                for k in range(2):
                    up2_high(u + 4, k)
            elif u < 4:
                dn2_high(u)
            elif u == 4:
                a.wait_ge(*upto("dn2_mm", 2))
                dn2_high(4)
        a.wait_ge(*upto("dn2_mm", 4))
        dn2_high(5)

    def pool_prog(pool):
        def less_high(dst, raw, high):
            return nc.gpsimd.tensor_tensor(dst, raw, high, ALU.subtract)

        def low_part(d, c, k):
            if k == 0:
                return less_high(gu_lo[:, d, c:c + HID], gu_raw[:, d, 0, c:c + HID], gu_hi[:, d, c:c + HID])
            return less_high(gu_mix[REST:P, d, c:c + HID], gu_raw[REST:P, d, 1, c:c + HID],
                             gu_mix[REST:P, d, c:c + HID])

        def expert(i, d):
            for k in range(4):
                pool.wait_ge(*upto(f"gu_high{d}", 4 * i + (k + 1)))
                if k == 2:
                    pool.wait_ge(*upto(f"gu_low{d}", 4 * i + 2))
                low_part(d, k % 2 * HID, k // 2).then_inc(S(f"gu_low{d}"), 1)
            pool.wait_ge(*upto(f"gu_low{d}", 4 * i + 4))
            for k in range(2):
                pool.wait_ge(*upto(f"d_high{d}", 2 * i + (k + 1)))
                less_high(d_lo[:, d, 3 * k:3 * k + 3, :], d_raw[:, d, 3 * k:3 * k + 3, :],
                          d_hi[:, d, 3 * k:3 * k + 3, :]).then_inc(S(f"d_low{d}"), 1)

        def up2(u):
            for k in range(2):
                pool.wait_ge(*upto("up2_whigh", 2 * u + k + 1))
                if 2 * u + k > 0:
                    pool.wait_ge(*upto("up2_wlow", 2 * u + k))
                low_part(*up2_at[u], k).then_inc(S("up2_wlow"), 1)

        def dn2(u, ups):
            pool.wait_ge(*upto("dn2_whigh", u + 1))
            pool.wait_ge(*upto("up2_wlow", 2 * ups))
            less_high(dn2_lo[u], d_raw[:, u % 2, :, :], dn2_hi[u]).then_inc(S("dn2_wlow"), 1)

        def inverse_std(tag):
            for n, tiles in enumerate((slice(0, 4), slice(4, 6))):
                pool.wait_ge(*upto(tag + "_vare", n + 1))
                nc.gpsimd.tensor_tensor(sdv[:, tiles], var[:, tiles], minus_half[:, tiles],
                                        ALU.pow).then_inc(S(tag + "_std"), 1)

        def spread(tag, row):
            for n in range(2 * AT):
                a, hf = n // 2, n % 2
                if n >= 2:
                    pool.wait_ge(*upto(tag + "_s", 2 * (n - 1)))
                nc.gpsimd.tensor_tensor(blkd[0:HD, n % 2, :, :],
                                        qk[0:HD, row + hf, a * HD:(a + 1) * HD].unsqueeze(1).broadcast_to([HD, 6, HD]),
                                        hm[:, :].unsqueeze(2).broadcast_to([HD, 6, HD]),
                                        ALU.mult).then_inc(S(tag + "_blk"), 1)

        pool.wait_ge(conv["s"]["tail_act"], conv["tail"])
        nc.gpsimd.memset(minus_half[:, :], -0.5).then_inc(S("half_set"), 1)
        pool.wait_ge(*upto("half_set", 1))
        inverse_std("f")
        pool.wait_ge(*upto("f_std", 2))
        nc.gpsimd.memset(x2T[HD:HB, :, :], 1.0).then_inc(S("half_set"), 1)
        nc.gpsimd.memset(xT[HD:HB, :, :], 1.0).then_inc(S("half_set"), 1)
        pool.wait_ge(*upto("half_set", 3))
        inverse_std("ln0")
        pool.wait_ge(*upto("ln1_vare", 1))
        nc.gpsimd.tensor_tensor(sdv[:, :], var[:, :], minus_half[:, :], ALU.pow).then_inc(S("ln1_std"), 1)
        pool.wait_ge(*upto("l0_qf", 8))
        pool.wait_ge(*upto("ln1_std", 1))
        spread("l0", 0)
        pool.wait_ge(*upto("l0_blk", 2 * AT))
        expert(0, 0)
        inverse_std("ln2")
        expert(0, 1)
        with pool.Fori(1, EXPERTS // 2) as i:
            for d in range(2):
                expert(i, d)
        up2(0)
        dn2(0, 1)
        pool.wait_ge(*upto("gu_mm", 24 * EXPERTS))
        pool.wait_ge(*upto("dn2_wlow", 1))
        nc.gpsimd.memset(xT[HD:HB, :, :], 1.0).then_inc(S("half_set"), 1)
        pool.wait_ge(*upto("half_set", 4))
        inverse_std("ln3")
        up2(1)
        dn2(1, 2)
        up2(2)
        up2(3)
        pool.wait_ge(*upto("l1_qkd", 8))
        pool.wait_ge(*upto("up2_wlow", 8))
        spread("l1", 2)
        pool.wait_ge(*upto("l1_blk", 2 * AT))
        inverse_std("ln4")

    def dve_prog(v):
        chain = [0]

        def link(ins):
            chain[0] += 1
            ins.then_inc(S("dve_chain"), 1)
            v.wait_ge(*upto("dve_chain", chain[0]))

        tt_ = nc.vector.tensor_tensor
        ts_ = nc.vector.tensor_scalar
        stt = nc.vector.scalar_tensor_tensor

        def add_pair(tag, pair, other):
            v.wait_ge(*upto(tag + "_mm", pair + 2))
            for i in (pair, pair + 1):
                src = banks[4 + i // 2][:, (i % 2) * D:(i % 2 + 1) * D]
                tt_(h[:, i, :], src, other(i), ALU.add).then_inc(S("h_add"), 1)
            v.wait_ge(*upto("h_add" + tag, pair + 2))

        def layer_norm(tag, src, dst, packed=False, before=None):
            for pair in range(0, TT, 2):
                if before is not None:
                    before(pair)
                for i in (pair, pair + 1):
                    nc.vector.bn_stats(st[:, i, :], src(i)).then_inc(S(tag + "_st"), 1)
                v.wait_ge(*upto(tag + "_st", pair + 2))
                for i in (pair, pair + 1):
                    nc.vector.bn_aggr(mv[:, i, :], st[:, i, :]).then_inc(S(tag + "_var"), 1)
                if pair >= 2:
                    tiles = slice(0, 4) if pair == 2 else slice(4, 6)
                    v.wait_ge(*upto(tag + "_var", pair + 2))
                    ts_(var[:, tiles], mv[:, tiles, 1], EPS, None, ALU.add).then_inc(S(tag + "_vare"), 1)
            for i in range(TT):
                v.wait_ge(*upto(tag + "_std", 1 if i < 4 else 2))
                if packed:
                    ts_(x_tok[:, i, D:2 * P], src(i)[:, P:D], mv[:, i, 0:1], sdv[:, i:i + 1], ALU.subtract, ALU.mult)
                ts_(dst(i), src(i), mv[:, i, 0:1], sdv[:, i:i + 1], ALU.subtract, ALU.mult).then_inc(S(tag + "_ln"), 1)

        h_tile = lambda i: h[:, i, :]
        x_tile = lambda i: x_tok[:, i, 0:D]

        nc.vector.memset(eps[:, :], EPS).then_inc(S("const_set"), 1)
        v.wait_ge(t["small_in"], 16 * len(t["small"]))
        v.wait_ge(*upto("f_T", TT))
        layer_norm("f", lambda i: banks[i // 4][:, (i % 4) * P:(i % 4 + 1) * P], lambda i: xn_f[:, i, :])
        for c, (lo, hi) in enumerate(((0, 4), (4, 6))):
            v.wait_ge(*upto("f_T2", hi))
            ts_(nT[:, lo * P:hi * P], banks[2 + c][:, 0:(hi - lo) * P], small["fln"][:, 0:1], small["fln"][:, 1:2],
                ALU.mult, ALU.add).then_inc(S("f_nT"), 1)
        layer_norm("ln0", h_tile, x_tile, before=lambda pair: add_pair("tok", pair, lambda i: small["proj_b"][:, :]))
        v.wait_ge(*upto("ln0_ln", TT))
        link(tt_(var[:, :], sdv[:, :], sdv[:, :], ALU.mult))
        link(tt_(var[:, :], var[:, :], mv[:, :, 1], ALU.mult))
        ts_(var[:, :], var[:, :], EPS, None, ALU.add).then_inc(S("ln1_vare"), 1)
        v.wait_ge(*upto("ln1_std", 1))
        for i in range(TT):
            ts_(x2_tok[:, i, :], x_tile(i), sdv[:, i:i + 1], None, ALU.mult).then_inc(S("ln1_ln"), 1)
        flat = x2T[:, :, :].rearrange("p k n -> p (k n)")
        flat = flat[0:HD]
        for c in range(3):
            v.wait_ge(*upto("a1_T", c + 1))
            for lo, hi in ((c * 512, min((c + 1) * 512, NTOK)), (max(c * 512, NTOK), (c + 1) * 512)):
                if lo >= hi:
                    continue
                kt = lo // NTOK
                ins = ts_(flat[:, lo:hi], banks[c][0:HD, lo - c * 512:hi - c * 512], small["ln_wb"][:, 0, kt:kt + 1],
                          small["ln_wb"][:, 1, kt:kt + 1], ALU.mult, ALU.add)
                if hi == (c + 1) * 512:
                    ins.then_inc(S("a1_xT"), 1)
        w = small["Wqkv"][:, :, 2 * D:3 * D].rearrange("p k (n e) -> p k n e", e=DH)
        link(nc.vector.tensor_reduce(vmean[:, :, :], w, AX, ALU.add))
        link(ts_(vmean[:, :, :], vmean[:, :, :], 1.0 / DH, None, ALU.mult))
        tt_(w, w, vmean[:, :, :].unsqueeze(3).broadcast_to([HB, 2, HEADS, DH]), ALU.subtract).then_inc(S("l0_wv"), 1)
        v.wait_ge(*upto("par_mm", 1))
        nc.vector.tensor_copy(par[:, :], banks[6][0:HD, 0:AT * 60]).then_inc(S("par_sb"), 1)
        link(ts_(tempc[:, :], small["temp"][0:HD, :], 0.1, 2.0, ALU.max, ALU.min))
        v.wait_ge(*upto("gate_t", 4))
        link(tt_(gv[1][:, :], gv[1][:, :], gv[3][:, :], ALU.subtract))
        link(ts_(gv[1][:, :], gv[1][:, :], PI_HALF, 3.1415925, ALU.mult, ALU.min))
        ts_(gv[1][:, :], gv[1][:, :], -3.1415925, None, ALU.max).then_inc(S("gate_arg"), 1)
        link(ts_(gv[0][:, :], gv[0][:, :], 0.5, 0.5, ALU.mult, ALU.add))
        link(ts_(gv[2][:, :], gv[2][:, :], 0.5, 0.5, ALU.mult, ALU.add))
        link(tt_(gv[0][:, :], gv[0][:, :], gv[2][:, :], ALU.mult))
        v.wait_ge(*upto("gate_sin", 1))
        link(tt_(gv[1][:, :], gv[1][:, :], gv[1][:, :], ALU.mult))
        link(ts_(gv[1][:, :], gv[1][:, :], -2.0, 1.0, ALU.mult, ALU.add))
        tt_(gv[0][:, :], gv[0][:, :], gv[1][:, :], ALU.mult).then_inc(S("gate_int"), 1)
        v.wait_ge(*upto("gate_tanh", 1))
        ts_(gv[0][:, :], gv[0][:, :], tempc[:, :], None, ALU.mult).then_inc(S("gate_int2"), 1)
        v.wait_ge(*upto("gate_tanh", 2))
        ts_(gv[4][:, :], gv[0][:, :], 0.5, 1.5, ALU.mult, ALU.add).then_inc(S("gates"), 1)
        nc.vector.memset(vg[:, :, :, DH:DH + 1], 1.0).then_inc(S("vones"), 1)
        v.wait_ge(*upto("gates", 1))
        gate1 = gv[4][:, :].rearrange("p (a n) -> p a n", a=AT)

        def gated_values(tiles):
            for a in tiles:
                v.wait_ge(*upto("l0_v", a + 1))
                tt_(vg[:, a, :, 0:DH], banks[2 + a % 4][0:HD, 0:D].rearrange("p (n e) -> p n e", n=HEADS),
                    gate1[:, a, :].unsqueeze(2).broadcast_to([HD, HEADS, DH]), ALU.mult).then_inc(S("l0_vd"), 1)

        gated_values(range(4))
        for n in range(8):
            m, hf = n // 2, n % 2
            v.wait_ge(*upto("l0_qk", n + 1))
            v.wait_ge(*upto("l0_qexp", n + 1))
            ts_(qr[:, n % 2, :], banks[n % 2][0:HD, 0:HALF], small["bqkv"][:, m:m + 1], 0.0, ALU.add,
                ALU.max).then_inc(S("l0_qkd"), 1)
            v.wait_ge(*upto("l0_qkd", n + 1))
            stt(out=qk[0:HD, m, hf * HALF:(hf + 1) * HALF], in0=qe[:, n % 2, :], scalar=1.0, in1=qr[:, n % 2, :],
                op0=ALU.min, op1=ALU.add).then_inc(S("l0_qf"), 1)
        gated_values(range(4, AT))

        causal = small["causal"][:, :].unsqueeze(1).broadcast_to([HD, 3, HD])
        o3 = oa[:, :, :, :].rearrange("p a n e -> p (a n) e")
        q3 = osq[:, :, :, :].rearrange("p a n e -> p (a n) e")
        pair = lambda c: slice(2 * c * HEADS, 2 * (c + 1) * HEADS)

        def head_variance(c):
            v.wait_ge(*upto("l0_o", 2 * c + 2))
            link(tt_(q3[:, pair(c), :], o3[:, pair(c), :], o3[:, pair(c), :], ALU.mult))
            nc.vector.reduce_sum(ovar[:, pair(c)], q3[:, pair(c), :], AX).then_inc(S("ovar"), 1)

        def head_norm(c):
            v.wait_ge(*upto("ostd", c + 1))
            link(nc.vector.reciprocal(ovar[:, pair(c)], ovar[:, pair(c)]))
            tt_(o3[:, pair(c), :], o3[:, pair(c), :], ovar[:, pair(c)].unsqueeze(2).broadcast_to([HD, 2 * HEADS, DH]),
                ALU.mult).then_inc(S("l0_oln"), 1)

        for n in range(2 * AT):
            for g in range(2):
                v.wait_ge(*upto("l0_s", 2 * n + g + 1))
                if n >= 2:
                    v.wait_ge(*upto("l0_pv", n - 1))
                tt_(pr[:, n % 2, 3 * g:3 * g + 3, :],
                    banks[2 * (n % 2) + g][0:HD, 0:3 * HD].rearrange("p (k n) -> p k n", k=3), causal,
                    ALU.mult).then_inc(S("l0_p"), 1)
            if n % 2 == 1 and n > 1:
                o_norm0(v, n // 2 - 1, link, tt_, ts_)
            if n % 4 == 3 and n > 3:
                head_variance(n // 4 - 1)
            if n % 4 == 1 and n > 5:
                head_norm((n - 5) // 4 - 1)
        o_norm0(v, AT - 1, link, tt_, ts_)
        head_variance(3)
        head_norm(2)
        head_norm(3)
        for c in range(4):
            v.wait_ge(*upto("l0_oT", c + 1))
            ts_(xT_att[:, c // 2, (c % 2) * HALF:(c % 2 + 1) * HALF], banks[c][0:HD, 0:HALF], small["mn"][:, 0:1],
                small["mn"][:, 1:2], ALU.mult, ALU.add).then_inc(S("l0_aT"), 1)

        layer_norm("ln2", h_tile, x_tile, packed=True, before=lambda pair: add_pair("l0p", pair, h_tile))
        v.wait_ge(*upto("f0_xT", 3))
        tt_(x_lo[:, :, :], xT[:, :, :], x_hi, ALU.subtract).then_inc(S("x_lo"), 1)
        v.wait_ge(*upto("route", 1))
        lg = banks[7][:, 0:TT * 8].rearrange("p (t e) -> p t e", e=8)
        bc = lambda x: x[:, :].unsqueeze(2).broadcast_to([P, TT, 8])
        link(nc.vector.tensor_reduce(r1[0][:, :], lg, AX, ALU.max))
        tt_(logit[:, :, :], lg, bc(r1[0]), ALU.subtract).then_inc(S("logit"), 1)

        def route_scores():
            v.wait_ge(*upto("logit", 1))
            v.wait_ge(*upto("score_exp", 1))
            nc.vector.reduce_sum(r1[0][:, :], score[:, :, :], AX).then_inc(S("route_read"), 1)
            v.wait_ge(*upto("route_read", 1))
            link(nc.vector.reciprocal(r1[0][:, :], r1[0][:, :]))
            link(tt_(score[:, :, :], score[:, :, :], bc(r1[0]), ALU.mult))

        def route_top():
            for i in range(TT):
                nc.vector.max(top8[:, i, :], score[:, i, :]).then_inc(S("top"), 1)
            v.wait_ge(*upto("top", TT))
            for i in range(TT):
                nc.vector.max_index(topi[:, i, :], top8[:, i, :], score[:, i, :]).then_inc(S("top"), 1)
            v.wait_ge(*upto("top", 2 * TT))
            link(nc.vector.tensor_copy(topf[:, :, :], topi[:, :, :]))

        def route_shares():
            link(tt_(r1[1][:, :], top8[:, :, 0], top8[:, :, 1], ALU.add))
            link(ts_(r1[1][:, :], r1[1][:, :], 1e-8, None, ALU.add))
            link(nc.vector.reciprocal(r1[1][:, :], r1[1][:, :]))
            link(ts_(r1[1][:, :], r1[1][:, :], 1.0 / WS, None, ALU.mult))

        def route_expert(k):
            iota = small["iota8"][:, :].unsqueeze(1).broadcast_to([P, TT, 8])
            link(nc.vector.tensor_copy(r1[2][:, :], topf[:, :, k]))
            link(tt_(mk[k][:, :, :], iota, bc(r1[2]), ALU.is_equal))
            link(tt_(r1[2][:, :], top8[:, :, k], r1[1][:, :], ALU.mult))
            link(tt_(mk[k][:, :, :], mk[k][:, :, :], bc(r1[2]), ALU.mult))

        def route_weights():
            link(tt_(cw[:, 0:8, :], mk[0][:, :, :].rearrange("p t e -> p e t"),
                     mk[1][:, :, :].rearrange("p t e -> p e t"), ALU.add))
            link(nc.vector.memset(cw[:, 8:10, :], 0.5 / WS))

        def unit(i, d, hb, between={}):
            for j in range(HT):
                cnt = 24 * i + (12 * d + 6 * hb + j)
                v.wait_ge(*upto("gu_mm", 2 * cnt + 2))
                v.wait_ge(*upto("silu", cnt + 1))
                stt(out=hid[:, hb, j, :], in0=banks[2 * (j % 2) + 1][:, 0:HALF], scalar=1.0 / WS, in1=sg[:, j % 2, :],
                    op0=ALU.mult, op1=ALU.mult).then_inc(S("hid_w"), 1)
                v.wait_ge(*upto("hid_w", cnt + 1))
                tt_(hid_lo[:, hb, j, :], hid[:, hb, j, :], hid_hi[:, hb, j, :], ALU.subtract).then_inc(S("hid_low"), 1)
                if j in between:
                    between[j]()

        def add_tile(i, d, hb, k):
            v.wait_ge(*upto("down", 12 * i + (6 * d + 3 * hb) + (2, 2, 3)[k]))
            src = banks[4 + 2 * hb + k // 2][:, (k % 2) * D:(k % 2 + 1) * D]
            tk = 3 * hb + k
            stt(out=h[:, tk, :], in0=src, scalar=cwc[:, d, tk:tk + 1], in1=h[:, tk, :], op0=ALU.mult,
                op1=ALU.add).then_inc(S("added"), 1)

        def add(i, d, hb):
            for k in range(3):
                add_tile(i, d, hb, k)

        routing = {0: route_scores, 1: route_top, 2: route_shares, 3: lambda: route_expert(0),
                   4: lambda: route_expert(1), 5: route_weights}

        def moe_iter(i, first):
            for d in range(2):
                unit(i, d, 0, routing if first and d == 0 else {})
                if d == 1:
                    add(i, 0, 1)
                else:
                    if not first:
                        add(i - 1, 1, 1)
                        v.wait_ge(*upto("added", 12 * i))
                    nc.vector.tensor_copy(cwc[:, :, :], cw[:, bass.ds(2 * i, 2), :]).then_inc(S("cwc"), 1)
                    v.wait_ge(*upto("cwc", i + 1))
                unit(i, d, 1)
                add(i, d, 0)

        moe_iter(0, True)
        with v.Fori(1, EXPERTS // 2) as i:
            moe_iter(i, False)

        def last_adds(pair):
            last = EXPERTS // 2 - 1
            for k in {0: (), 2: (0,), 4: (1, 2)}[pair]:
                add_tile(last, 1, 1, k)
            v.wait_ge(*upto("added", 6 * EXPERTS - 3 + max(0, pair - 1)))

        layer_norm("ln3", h_tile, x_tile, before=last_adds)
        for n in range(8):
            m, hf = n // 2, n % 2
            v.wait_ge(*upto("l1_qk", n + 1))
            ts_(qk[0:HD, m, hf * HALF:(hf + 1) * HALF], banks[n % 2][0:HD, 0:HALF], small["b_qkv"][:, m:m + 1], None,
                ALU.add).then_inc(S("l1_qkd"), 1)
        for a in range(AT):
            v.wait_ge(*upto("l1_v", a + 1))
            nc.vector.tensor_copy(vg[:, a, :, 0:DH],
                                  banks[2 + a % 4][0:HD, 0:D].rearrange("p (n e) -> p n e", n=HEADS)).then_inc(S("l1_vd"), 1)
        for n in range(2 * AT):
            if n >= 2:
                v.wait_ge(*upto("l1_pT", 2 * (n - 1)))
            scores = [banks[2 * (n % 2) + g][0:HD, 0:3 * HD].rearrange("p (k n) -> p k n", k=3) for g in range(2)]
            for g in range(2):
                v.wait_ge(*upto("l1_s", 2 * n + g + 1))
                nc.vector.tensor_reduce(mxs[:, n % 2, 3 * g:3 * g + 3], scores[g], AX, ALU.max).then_inc(S("l1_max"), 1)
            for g in range(2):
                v.wait_ge(*upto("l1_max", 2 * n + g + 1))
                tt_(pr[:, n % 2, 3 * g:3 * g + 3, :], scores[g],
                    mxs[:, n % 2, 3 * g:3 * g + 3].unsqueeze(2).broadcast_to([HD, 3, HD]),
                    ALU.subtract).then_inc(S("l1_sub"), 1)
            if n % 2 == 1 and n > 1:
                o_norm1(v, n // 2 - 1, link, tt_)
        o_norm1(v, AT - 1, link, tt_)
        for c in range(4):
            v.wait_ge(*upto("l1_oT", c + 1))
            nc.vector.tensor_copy(xT_att[:, c // 2, (c % 2) * HALF:(c % 2 + 1) * HALF],
                                  banks[c][0:HD, 0:HALF]).then_inc(S("l1_aT"), 1)

        layer_norm("ln4", h_tile, x_tile, packed=True, before=lambda pair: add_pair("l1p", pair, h_tile))
        v.wait_ge(*upto("f1_xT", 3))
        tt_(x_lo[:, :, :], xT[:, :, :], x_hi, ALU.subtract).then_inc(S("x_lo2"), 1)
        v.wait_ge(*upto("glog", 1))
        logits = banks[7][0:BATCH, 0:12].rearrange("p (i k) -> p i k", k=2)
        gb2 = gr[:, :].unsqueeze(2).broadcast_to([BATCH, 6, 2])
        link(nc.vector.tensor_reduce(gr[:, :], logits, AX, ALU.max))
        tt_(gl[:, :, :], logits, gb2, ALU.subtract).then_inc(S("gsub"), 1)
        v.wait_ge(*upto("gexp", 1))
        link(nc.vector.reduce_sum(gr[:, :], gl[:, :, :], AX))
        link(nc.vector.reciprocal(gr[:, :], gr[:, :]))
        link(tt_(gl[:, :, :], gl[:, :, :], gb2, ALU.mult))
        link(nc.vector.tensor_reduce(gr[:, :], gl[:, :, :], AX, ALU.min))
        link(tt_(gkeep[:, :, :], gl[:, :, :], gb2, ALU.is_gt))
        link(tt_(gl[:, :, :], gl[:, :, :], gkeep[:, :, :], ALU.mult))
        link(nc.vector.reduce_sum(gr[:, :], gl[:, :, :], AX))
        link(ts_(gr[:, :], gr[:, :], 1e-6, None, ALU.max))
        link(nc.vector.reciprocal(gr[:, :], gr[:, :]))
        link(tt_(gl[:, :, :], gl[:, :, :], gb2, ALU.mult))
        tt_(gdiag[:, :, :, :], gl[:, :, :].rearrange("p i k -> p k i").unsqueeze(3).broadcast_to([BATCH, 2, 6, BATCH]),
            ident[0:BATCH, 0:BATCH].unsqueeze(1).unsqueeze(1).broadcast_to([BATCH, 2, 6, BATCH]),
            ALU.mult).then_inc(S("gdiag"), 1)

        def split_up2(u):
            d, c = up2_at[u]
            cols = slice(c, c + HID)
            v.wait_ge(*upto("up2_whigh", 2 * u + 1))
            stt(out=gu_lo[:, d, cols], in0=gu_raw[:, d, 0, cols], scalar=WS, in1=gu_hi[:, d, cols], op0=ALU.mult,
                op1=ALU.subtract).then_inc(S("up2_wlow"), 1)
            v.wait_ge(*upto("up2_whigh", 2 * u + 2))
            stt(out=gu_mix[REST:P, d, cols], in0=gu_raw[REST:P, d, 1, cols], scalar=WS, in1=gu_mix[REST:P, d, cols],
                op0=ALU.mult, op1=ALU.subtract).then_inc(S("up2_wlow"), 1)

        def split_dn2(u):
            v.wait_ge(*upto("dn2_whigh", u + 1))
            stt(out=dn2_lo[u], in0=d_raw[:, u % 2, :, :], scalar=WS, in1=dn2_hi[u], op0=ALU.mult,
                op1=ALU.subtract).then_inc(S("dn2_wlow"), 1)

        yr = yT[:, :, :].rearrange("p k (b r) -> p k r b", r=12)

        def weigh(k, m):
            tt_(yd[:, k, m, :, :], yd[:, k, m, :, :], banks[6 + k][0:HD, 0:HALF].rearrange("p (i b) -> p i b", i=6),
                ALU.mult).then_inc(S("weighed"), 1)

        def up_lows(u, cols, slots):
            for j in range(HT):
                v.wait_ge(*upto("up2_act", 6 * u + j + 1))
                if slots is None:
                    tt_(hid_lo[:, 0, j, :], hid[:, 0, j, :], hid_hi[:, 0, j, :], ALU.subtract).then_inc(S("up2_low"), 1)
                else:
                    tt_(hc_lo[:, j, rng(slots), :], hc[:, j, rng(slots), :], hc_hi[:, j, rng(slots), :],
                        ALU.subtract).then_inc(S("up2_low"), 1)
            if u in (1, 2):
                split_up2(u + 3)
            elif u in (3, 4):
                split_dn2(u - 1)
            elif u == 5:
                split_dn2(4)
                split_dn2(5)

        def down_out(u, slots, direction, classes):
            for m in range(2):
                cnt = 2 * u + m
                v.wait_ge(*upto("dn2_mm", cnt + 1))
                if slots is None:
                    src = banks[2 + cnt % 2][0:HD, 0:HALF].rearrange("p (r b) -> p r b", b=BATCH)
                    dst = yr[:, m, 6:12, :]
                else:
                    src = banks[2 + cnt % 2][0:HD, 0:slots[2] * BATCH].rearrange("p (r b) -> p r b", b=BATCH)
                    dst = yd[:, direction, m, rng(classes), :]
                ts_(dst, src, 1.0 / WS, small["b2"][:, m, u:u + 1], ALU.mult, ALU.add).then_inc(S("dn2_read"), 1)
            if u == 2:
                v.wait_ge(*upto("gall", 2))
                v.wait_ge(*upto("dn2_read", 6))
                for m in range(2):
                    weigh(0, m)

        for kind, u in ORDER:
            if kind == "up":
                up_lows(*UP[u])
            elif kind == "down":
                down_out(*DOWN[u])
        v.wait_ge(*upto("dn2_read", 12))
        for m in range(2):
            weigh(1, m)
        v.wait_ge(*upto("weighed", 4))
        for m in range(2):
            ins = tt_(yr[:, m, 0:6, :], yd[:, 0, m, :, :], yd[:, 1, m, :, :], ALU.add)
        ins.then_inc(S("yT"), 1)
        for i in range(TT):
            v.wait_ge(*upto("y_tok", i // 2 * 2 + 2))
            tt_(outb[:, i, 0:D], banks[4 + i // 2][:, (i % 2) * D:(i % 2 + 1) * D], h[:, i, :],
                ALU.add).then_inc(S("out_ready"), 1)

    def o_norm0(v, a, link, tt_, ts_):
        v.wait_ge(*upto("l0_pv", 2 * a + 2))
        o = banks[4 + a % 2][0:HD, 0:HEADS * (DH + 1)].rearrange("p (n e) -> p n e", n=HEADS)
        r = rden[:, a * HEADS:(a + 1) * HEADS]
        link(ts_(r, o[:, :, DH], 1e-6, None, ALU.add))
        link(nc.vector.reciprocal(r, r))
        tt_(oa[:, a, :, :], o[:, :, 0:DH], r.unsqueeze(2).broadcast_to([HD, HEADS, DH]),
            ALU.mult).then_inc(S("l0_o"), 1)

    def o_norm1(v, a, link, tt_):
        v.wait_ge(*upto("l1_pv", 2 * a + 2))
        o = banks[4 + a % 2][0:HD, 0:HEADS * (DH + 1)].rearrange("p (n e) -> p n e", n=HEADS)
        r = rden[:, a * HEADS:(a + 1) * HEADS]
        link(nc.vector.reciprocal(r, o[:, :, DH]))
        tt_(oa[:, a, :, :], o[:, :, 0:DH], r.unsqueeze(2).broadcast_to([HD, HEADS, DH]),
            ALU.mult).then_inc(S("l1_o"), 1)

    return dict(sync=sync_prog, pool=pool_prog, act=act_prog, pe=pe_prog, dve=dve_prog)


def halves(w):
    return w.reshape(2, HD, -1).transpose(1, 0, 2)


def halves_bias(w, bias):
    return np.concatenate([halves(w), np.stack([bias, np.zeros_like(bias)])[None]])


def packed(w):
    return np.stack([w[..., 0:P, :], np.concatenate([w[..., P:D, :], w[..., P:D, :]], axis=-2)], axis=-2)


def rest_inputs(i):
    b12 = np.arange(HD) // 12
    same = b12[:, None] == b12[None, :]
    causal = same & (np.arange(HD)[:, None] <= np.arange(HD)[None, :])
    up1 = [np.concatenate([i[f"L0_ffn_{k}_gate"], i[f"L0_ffn_{k}_up"]], axis=1) for k in ("routed", "shared")]
    gu = np.concatenate(up1)
    dn = np.concatenate([i["L0_ffn_routed_down"], i["L0_ffn_shared_down"]])
    up2 = np.concatenate([i["L1_ffn_moe0_W1"][None], i["L1_ffn_A1_W"]])
    order = [0, 4, 5, 1, 2, 3]
    dn2 = np.concatenate([i["L1_ffn_moe0_W2"][None], i["L1_ffn_A2_W"]])[order]
    b1 = np.concatenate([i["L1_ffn_moe0_b1"][None], i["L1_ffn_A1_b"]])
    b2 = np.concatenate([i["L1_ffn_moe0_b2"][None], i["L1_ffn_A2_b"]])[order]
    small = {
        "fln": np.stack([i["L0_tok_fln_g"], i["L0_tok_fln_b"]], -1),
        "proj_w": i["L0_tok_proj_w"], "proj_b": np.broadcast_to(i["L0_tok_proj_b"], (P, D)),
        "Wb1": halves(i["L0_attn_Wb1"]), "Wb2": i["L0_attn_Wb2"],
        "Wqkv": halves_bias(i["L0_attn_Wqkv"], i["L0_attn_bqkv"]), "bqkv": i["L0_attn_bqkv"].reshape(6, HD).T,
        "ln_wb": np.stack([i["L0_attn_ln_w"].reshape(2, HD).T, i["L0_attn_ln_b"].reshape(2, HD).T], 1),
        "temp": np.broadcast_to(i["L0_attn_temperature"][None], (P, 1)),
        "mn": np.stack([np.tile(i["L0_attn_mn_w"], 6), np.tile(i["L0_attn_mn_b"], 6)], -1),
        "Wproj": halves_bias(i["L0_attn_Wproj"], i["L0_attn_bproj"]),
        "gate_w": packed(i["L0_ffn_gate_w"].T),
        "w_qkv": halves_bias(i["L1_attn_w_qkv"], i["L1_attn_b_qkv"]), "b_qkv": i["L1_attn_b_qkv"].reshape(6, HD).T,
        "w_proj": halves_bias(i["L1_attn_w_proj"], i["L1_attn_b_proj"]),
        "G_W": packed(i["L1_ffn_G_W"].transpose(1, 0, 2).reshape(D, 12)).reshape(P, 2, 6, 2),
        "ones": np.ones((BATCH, HD), np.float32),
        "b1": b1.reshape(6, HT, P).transpose(2, 0, 1), "b2": b2.reshape(6, 2, HD).transpose(2, 1, 0),
        "headmask": (np.arange(HD)[:, None] // DH == np.arange(6)[None]).astype(np.float32),
        "causal": causal.astype(np.float32),
        "iota8": np.broadcast_to(np.arange(8, dtype=np.float32), (P, 8)),
    }
    tile_rows = b12[None] == np.arange(AT)[:, None]
    large = {
        "row_of": np.broadcast_to(tile_rows.astype(np.float32)[:, None, None], (AT, 2, AT, HD)).reshape(AT, 2, NTOK),
        "apart": np.broadcast_to(np.where(tile_rows, 0, -1e30).astype(np.float32)[:, None, None], (AT, 2, 6, HD)),
        "gu": packed(gu.transpose(0, 2, 1)),
        "dn": dn.transpose(0, 2, 1).reshape(EXPERTS, HT, P, D).transpose(0, 2, 1, 3),
        "up2": packed(up2),
        "dn2": dn2.reshape(6, HT, P, D).transpose(0, 2, 1, 3),
    }
    return small, large


def build(nc, t, out):
    with ExitStack() as ctx, ExitStack() as conv_ctx:
        sb = lambda n, sh, dt: ctx.enter_context(nc.sbuf_tensor(n, sh, dt))
        conv_sb = lambda n, sh, dt: conv_ctx.enter_context(nc.sbuf_tensor(n, sh, dt))
        sem = lambda n: ctx.enter_context(nc.semaphore(n))
        banks = [ctx.enter_context(nc.psum_tensor(f"bank{i}", [P, 512], F32)) for i in range(8)]
        t["ident"] = sb("ident", [P, P], F32)
        t["scratch"] = nc.dram_tensor("scratch", (2, TAPS0, STREAM0), F16).ap()
        t["out"] = out.rearrange("b r d -> (b r) d").rearrange("(t p) d -> p t d", p=P)
        t["gu_flat"] = t["gu"].rearrange("e p k n -> (e p) (k n)")
        t["dn_flat"] = t["dn"].rearrange("e p k n -> (e p) (k n)")
        act6 = sb("act6", [P, NTOK], F32)
        t["small_sb"] = {n: sb("s_" + n, list(a.shape), a.dtype) for n, a in t["small"].items()}
        t["small_in"] = sem("small_in")

        def load_small(sp):
            for n, a in t["small"].items():
                sp.dma_start(t["small_sb"][n][tuple(slice(None) for _ in a.shape)], a).then_inc(t["small_in"], 16)

        conv = build_conv(nc, conv_sb, lambda i: banks[i], sem, t, act6, load_small)
        conv_ctx.close()
        rest = build_rest(nc, sb, banks, sem, t, act6, conv)
        block = ctx.enter_context(nc.Block())

        @block.sync
        def _(sp):
            conv["sync"](sp)
            sp.wait_ge(conv["s"]["tail_act"], conv["tail"])
            rest["sync"](sp)

        @block.gpsimd
        def _(pool):
            conv["pool"](pool)
            rest["pool"](pool)

        @block.scalar
        def _(act):
            conv["act"](act)
            rest["act"](act)

        @block.tensor
        def _(pe):
            conv["pe"](pe)
            rest["pe"](pe)

        @block.vector
        def _(dve):
            conv["dve"](dve)
            dve.wait_ge(conv["s"]["tail_act"], conv["tail"])
            rest["dve"](dve)


def kernel(**inputs):
    import concourse.bacc as bacc
    from concourse.bass_utils import run_bass_kernel_spmd

    inputs = {k: np.asarray(v) for k, v in inputs.items()}
    small, large = rest_inputs(inputs)
    nc = bacc.Bacc("TRN2", target_bir_lowering=False, num_devices=1)
    arrays, t = {}, {"small": {}}
    for group, given in ((t, conv_inputs(inputs["x"], inputs)), (t["small"], small), (t, large)):
        for n, a in given.items():
            a = np.ascontiguousarray(a)
            arrays["in_" + n] = a
            group[n] = nc.dram_tensor("in_" + n, a.shape, mybir.dt.from_np(a.dtype), kind="ExternalInput").ap()
    out = nc.dram_tensor("out", (BATCH, 12, D), F32, kind="ExternalOutput").ap()
    build(nc, t, out)
    r = run_bass_kernel_spmd(nc, [arrays], core_ids=[0])
    return r.results[0]["out"]
```
